# Optimizing a Trainium2 kernel written in Bass

```python
import numpy as np
import jax
import jax.numpy as jnp

def _softmax(x, axis=-1):
    return jax.nn.softmax(x, axis=axis)

def _gelu(x):
    return jax.nn.gelu(x, approximate=True)

def _silu(x):
    return jax.nn.silu(x)

def _sigmoid(x):
    return jax.nn.sigmoid(x)

def _layernorm(x, axis=-1, eps=1e-05):
    m = jnp.mean(x, axis=axis, keepdims=True)
    v = jnp.var(x, axis=axis, keepdims=True)
    return (x - m) / jnp.sqrt(v + eps)

def _scatter_add(tgt, idx, src, axis=0):
    return tgt.at[idx].add(src)

def _segment_sum(src, seg, n):
    return jax.ops.segment_sum(src, seg, n)
kernel_name = 'mk_seq_postln_d1_jaxref_r8_a62ccd'

def setup_inputs(seed: int=0):
    np.random.seed(seed)
    _w = jnp.asarray

    def _L0_attn_setup():
        import jax, jax.numpy as jnp
        import numpy as np
        H = 128
        D = 32
        CHUNK = 64
        LR = 0.1
        GRAD_SCALE = 0.1
        MAX_GRAD_NORM = 1.0
        EPS = 1e-06
        P = 2 * D * D

        def _xavier(k, shape, gain=0.1):
            fan_out, fan_in = shape
            a = gain * np.sqrt(6.0 / (fan_in + fan_out))
            return jax.random.uniform(k, shape, jnp.float32, -a, a)

        def _causal_dwconv(x, w, b):
            T = x.shape[1]
            xp = jnp.pad(x, ((0, 0), (3, 0), (0, 0)))
            y = b
            for j in range(4):
                y = y + xp[:, j:j + T, :] * w[:, j]
            return y

        def _mem_loss(p, k_t, v_t):
            W1 = p[:D * D].reshape(D, D)
            W2 = p[D * D:].reshape(D, D)
            pred = jax.nn.silu(k_t @ W1.T) @ W2.T
            return jnp.sum((pred - v_t) ** 2)
        _grad_fn = jax.vmap(jax.vmap(jax.grad(_mem_loss), in_axes=(None, 0, 0)), in_axes=(0, 0, 0))

        def _forward(hidden, Wk, Wv, Wq, Wo, ckw, ckb, cvw, cvb, cqw, cqb, mW1, mW2, aW, ab, eW, eb, tW, tb, norm_g, gW, gb):
            B, S, _ = hidden.shape
            k = _causal_dwconv(hidden @ Wk.T, ckw, ckb)
            v = _causal_dwconv(hidden @ Wv.T, cvw, cvb)
            q = _causal_dwconv(hidden @ Wq.T, cqw, cqb)
            alpha = (jax.nn.sigmoid(hidden @ aW.T + ab) * 0.1).mean(-1)
            eta = (jax.nn.sigmoid(hidden @ eW.T + eb) * 0.9 + 0.05).mean(-1)
            theta = (jax.nn.softplus(hidden @ tW.T + tb) * LR).mean(-1)
            W_state = jnp.tile(jnp.concatenate([mW1.ravel(), mW2.ravel()])[None], (B, 1))
            S_state = jnp.zeros_like(W_state)

            def step(carry, xs):
                Sm, Wm = carry
                gt, et, tt, at = xs
                Sm = et[:, None] * Sm - tt[:, None] * gt
                Wm = (1.0 - at[:, None]) * Wm + Sm
                return ((Sm, Wm), Wm)
            outs = []
            for c0 in range(0, S, CHUNK):
                sl = slice(c0, c0 + CHUNK)
                g = _grad_fn(W_state, k[:, sl], v[:, sl]) * GRAD_SCALE
                gn = jnp.maximum(jnp.linalg.norm(g, axis=-1, keepdims=True), EPS)
                g = g * jnp.minimum(MAX_GRAD_NORM / gn, 1.0)
                g = jax.lax.stop_gradient(g)
                xs = (jnp.swapaxes(g, 0, 1), eta[:, sl].T, theta[:, sl].T, alpha[:, sl].T)
                (S_state, W_state), Wtraj = jax.lax.scan(step, (S_state, W_state), xs)
                Wtraj = jnp.swapaxes(Wtraj, 0, 1)
                T = Wtraj.shape[1]
                W1t = Wtraj[..., :D * D].reshape(B, T, D, D)
                W2t = Wtraj[..., D * D:].reshape(B, T, D, D)
                h = jax.nn.silu(jnp.einsum('btd,btod->bto', q[:, sl], W1t))
                outs.append(jnp.einsum('bto,btpo->btp', h, W2t))
            retrieved = jnp.concatenate(outs, axis=1)
            out = retrieved @ Wo.T
            out = out * jax.lax.rsqrt(jnp.mean(out * out, -1, keepdims=True) + EPS) * norm_g
            gate = hidden @ gW.T + gb
            return out * gate
        key = jax.random.key(seed)
        ks = jax.random.split(key, 24)
        B, S = (1, 128)
        return {'hidden': jax.random.normal(ks[0], (B, S, H), jnp.float32), 'Wk': _xavier(ks[1], (D, H)), 'Wv': _xavier(ks[2], (D, H)), 'Wq': _xavier(ks[3], (D, H)), 'Wo': _xavier(ks[4], (H, D)), 'ckw': jax.random.normal(ks[5], (D, 4), jnp.float32) * 0.05, 'ckb': jnp.zeros((D,), jnp.float32), 'cvw': jax.random.normal(ks[6], (D, 4), jnp.float32) * 0.05, 'cvb': jnp.zeros((D,), jnp.float32), 'cqw': jax.random.normal(ks[7], (D, 4), jnp.float32) * 0.05, 'cqb': jnp.zeros((D,), jnp.float32), 'mW1': _xavier(ks[8], (D, D)), 'mW2': _xavier(ks[9], (D, D)), 'aW': jax.random.normal(ks[10], (D, H), jnp.float32) * 0.02, 'ab': jnp.zeros((D,), jnp.float32), 'eW': jax.random.normal(ks[11], (D, H), jnp.float32) * 0.02, 'eb': jnp.zeros((D,), jnp.float32), 'tW': jax.random.normal(ks[12], (D, H), jnp.float32) * 0.02, 'tb': jnp.zeros((D,), jnp.float32), 'norm_g': jnp.ones((H,), jnp.float32), 'gW': jnp.zeros((H, H), jnp.float32), 'gb': jnp.ones((H,), jnp.float32)}
    _L0_attn_in = _L0_attn_setup()

    def _L0_ffn_setup():
        import jax, jax.numpy as jnp
        import numpy as np
        DIM = 128
        DEPTH = 2
        HEADS = 8
        DIM_HEAD = 64
        WINDOW = 64
        INNER = HEADS * DIM_HEAD
        HID = int(DIM * 4 * 2 / 3)
        B, N = (2, 1024)
        QK_SCALE = 8.0

        def shift_token(t):
            t1, t2 = jnp.split(t, 2, axis=-1)
            t2 = jnp.pad(t2, ((0, 0), (1, 0), (0, 0)))[:, :-1]
            return jnp.concatenate([t1, t2], axis=-1)

        def l2norm(t):
            return t / jnp.clip(jnp.linalg.norm(t, axis=-1, keepdims=True), 1e-12)

        def rotate_half(x):
            x1, x2 = jnp.split(x, 2, axis=-1)
            return jnp.concatenate([-x2, x1], axis=-1)

        def rotary_xpos(q, k):
            n = q.shape[-2]
            half_idx = jnp.arange(0, DIM_HEAD, 2, dtype=jnp.float32)
            inv_freq = 1.0 / 10000.0 ** (half_idx / DIM_HEAD)
            t = jnp.arange(n, dtype=jnp.float32)
            freqs = t[:, None] * inv_freq[None, :]
            freqs = jnp.concatenate([freqs, freqs], axis=-1)
            base = (half_idx + 0.4 * DIM_HEAD) / (1.4 * DIM_HEAD)
            power = (t - n // 2) / float(WINDOW // 2)
            scale = base[None, :] ** power[:, None]
            scale = jnp.concatenate([scale, scale], axis=-1)
            cos, sin = (jnp.cos(freqs), jnp.sin(freqs))
            q = q * cos * scale + rotate_half(q) * sin * scale
            k = k * cos / scale + rotate_half(k) * sin / scale
            return (q, k)

        def local_attention(q, k, v):
            b, h, n, d = q.shape
            w = n // WINDOW
            bq = q.reshape(b, h, w, WINDOW, d) * QK_SCALE
            bk = k.reshape(b, h, w, WINDOW, d)
            bv = v.reshape(b, h, w, WINDOW, d)

            def look_around(t):
                p = jnp.pad(t, ((0, 0), (0, 0), (1, 0), (0, 0), (0, 0)))
                return jnp.concatenate([p[:, :, :w], p[:, :, 1:]], axis=3)
            bk, bv = (look_around(bk), look_around(bv))
            bt = jnp.arange(n).reshape(w, WINDOW)
            btp = jnp.pad(bt, ((1, 0), (0, 0)), constant_values=-1)
            btk = jnp.concatenate([btp[:w], btp[1:]], axis=1)
            sim = jnp.einsum('bhwid,bhwjd->bhwij', bq, bk)
            i = bt[:, :, None]
            j = btk[:, None, :]
            mask = (i < j) | (i > j + WINDOW) | (j == -1)
            sim = jnp.where(mask, -jnp.finfo(sim.dtype).max, sim)
            attn = jax.nn.softmax(sim, axis=-1)
            out = jnp.einsum('bhwij,bhwjd->bhwid', attn, bv)
            return out.reshape(b, h, n, d)

        def _layer(x, wqkv, qs, ksc, wo, lg, lb, w1, b1, w2, b2):
            b, n, _ = x.shape
            h = shift_token(x)
            qkv = h @ wqkv
            q, k, v = jnp.split(qkv, 3, axis=-1)
            to_heads = lambda t: t.reshape(b, n, HEADS, DIM_HEAD).transpose(0, 2, 1, 3)
            q, k, v = (to_heads(q), to_heads(k), to_heads(v))
            q = l2norm(q) * qs
            k = l2norm(k) * ksc
            q, k = rotary_xpos(q, k)
            o = local_attention(q, k, v)
            o = o.transpose(0, 2, 1, 3).reshape(b, n, INNER)
            x = x + o @ wo
            h = shift_token(x)
            mu = h.mean(-1, keepdims=True)
            var = h.var(-1, keepdims=True)
            h = (h - mu) / jnp.sqrt(var + 1e-05) * lg + lb
            h = h @ w1 + b1
            a, g = jnp.split(h, 2, axis=-1)
            h = a * jax.nn.gelu(g, approximate=False)
            x = x + h @ w2 + b2
            return x
        key = jax.random.key(seed)
        ks = jax.random.split(key, 6)
        return {'x': jax.random.normal(ks[0], (B, N, DIM), jnp.float32), 'wqkv': jax.random.normal(ks[1], (DEPTH, DIM, 3 * INNER), jnp.float32) * 0.02, 'q_scale': jnp.ones((DEPTH, DIM_HEAD), jnp.float32), 'k_scale': jnp.ones((DEPTH, DIM_HEAD), jnp.float32), 'wo': jax.random.normal(ks[2], (DEPTH, INNER, DIM), jnp.float32) * 0.02, 'ln_g': jnp.ones((DEPTH, DIM), jnp.float32), 'ln_b': jnp.zeros((DEPTH, DIM), jnp.float32), 'w1': jax.random.normal(ks[3], (DEPTH, DIM, 2 * HID), jnp.float32) * 0.02, 'b1': jnp.zeros((DEPTH, 2 * HID), jnp.float32), 'w2': jax.random.normal(ks[4], (DEPTH, HID, DIM), jnp.float32) * 0.02, 'b2': jnp.zeros((DEPTH, DIM), jnp.float32)}
    _L0_ffn_in = _L0_ffn_setup()
    _d = {'L0_attn_hidden': _L0_attn_in['hidden'], 'L0_attn_Wk': _L0_attn_in['Wk'], 'L0_attn_Wv': _L0_attn_in['Wv'], 'L0_attn_Wq': _L0_attn_in['Wq'], 'L0_attn_Wo': _L0_attn_in['Wo'], 'L0_attn_ckw': _L0_attn_in['ckw'], 'L0_attn_ckb': _L0_attn_in['ckb'], 'L0_attn_cvw': _L0_attn_in['cvw'], 'L0_attn_cvb': _L0_attn_in['cvb'], 'L0_attn_cqw': _L0_attn_in['cqw'], 'L0_attn_cqb': _L0_attn_in['cqb'], 'L0_attn_mW1': _L0_attn_in['mW1'], 'L0_attn_mW2': _L0_attn_in['mW2'], 'L0_attn_aW': _L0_attn_in['aW'], 'L0_attn_ab': _L0_attn_in['ab'], 'L0_attn_eW': _L0_attn_in['eW'], 'L0_attn_eb': _L0_attn_in['eb'], 'L0_attn_tW': _L0_attn_in['tW'], 'L0_attn_tb': _L0_attn_in['tb'], 'L0_attn_norm_g': _L0_attn_in['norm_g'], 'L0_attn_gW': _L0_attn_in['gW'], 'L0_attn_gb': _L0_attn_in['gb'], 'L0_ffn_wqkv': _L0_ffn_in['wqkv'], 'L0_ffn_q_scale': _L0_ffn_in['q_scale'], 'L0_ffn_k_scale': _L0_ffn_in['k_scale'], 'L0_ffn_wo': _L0_ffn_in['wo'], 'L0_ffn_ln_g': _L0_ffn_in['ln_g'], 'L0_ffn_ln_b': _L0_ffn_in['ln_b'], 'L0_ffn_w1': _L0_ffn_in['w1'], 'L0_ffn_b1': _L0_ffn_in['b1'], 'L0_ffn_w2': _L0_ffn_in['w2'], 'L0_ffn_b2': _L0_ffn_in['b2']}
    _x0 = _d['L0_attn_hidden']
    _d['L0_attn_hidden'] = jax.random.normal(jax.random.fold_in(jax.random.key(seed), 1), (8, 256, 128), dtype=_x0.dtype)
    del _x0
    return _d

def reference(L0_attn_hidden, L0_attn_Wk, L0_attn_Wv, L0_attn_Wq, L0_attn_Wo, L0_attn_ckw, L0_attn_ckb, L0_attn_cvw, L0_attn_cvb, L0_attn_cqw, L0_attn_cqb, L0_attn_mW1, L0_attn_mW2, L0_attn_aW, L0_attn_ab, L0_attn_eW, L0_attn_eb, L0_attn_tW, L0_attn_tb, L0_attn_norm_g, L0_attn_gW, L0_attn_gb, L0_ffn_wqkv, L0_ffn_q_scale, L0_ffn_k_scale, L0_ffn_wo, L0_ffn_ln_g, L0_ffn_ln_b, L0_ffn_w1, L0_ffn_b1, L0_ffn_w2, L0_ffn_b2):

    def _L0_attn_ref(hidden, Wk, Wv, Wq, Wo, ckw, ckb, cvw, cvb, cqw, cqb, mW1, mW2, aW, ab, eW, eb, tW, tb, norm_g, gW, gb):
        import jax, jax.numpy as jnp
        import numpy as np
        H = 128
        D = 32
        CHUNK = 64
        LR = 0.1
        GRAD_SCALE = 0.1
        MAX_GRAD_NORM = 1.0
        EPS = 1e-06
        P = 2 * D * D

        def _xavier(k, shape, gain=0.1):
            fan_out, fan_in = shape
            a = gain * np.sqrt(6.0 / (fan_in + fan_out))
            return jax.random.uniform(k, shape, jnp.float32, -a, a)

        def _causal_dwconv(x, w, b):
            T = x.shape[1]
            xp = jnp.pad(x, ((0, 0), (3, 0), (0, 0)))
            y = b
            for j in range(4):
                y = y + xp[:, j:j + T, :] * w[:, j]
            return y

        def _mem_loss(p, k_t, v_t):
            W1 = p[:D * D].reshape(D, D)
            W2 = p[D * D:].reshape(D, D)
            pred = jax.nn.silu(k_t @ W1.T) @ W2.T
            return jnp.sum((pred - v_t) ** 2)
        _grad_fn = jax.vmap(jax.vmap(jax.grad(_mem_loss), in_axes=(None, 0, 0)), in_axes=(0, 0, 0))

        def _forward(hidden, Wk, Wv, Wq, Wo, ckw, ckb, cvw, cvb, cqw, cqb, mW1, mW2, aW, ab, eW, eb, tW, tb, norm_g, gW, gb):
            B, S, _ = hidden.shape
            k = _causal_dwconv(hidden @ Wk.T, ckw, ckb)
            v = _causal_dwconv(hidden @ Wv.T, cvw, cvb)
            q = _causal_dwconv(hidden @ Wq.T, cqw, cqb)
            alpha = (jax.nn.sigmoid(hidden @ aW.T + ab) * 0.1).mean(-1)
            eta = (jax.nn.sigmoid(hidden @ eW.T + eb) * 0.9 + 0.05).mean(-1)
            theta = (jax.nn.softplus(hidden @ tW.T + tb) * LR).mean(-1)
            W_state = jnp.tile(jnp.concatenate([mW1.ravel(), mW2.ravel()])[None], (B, 1))
            S_state = jnp.zeros_like(W_state)

            def step(carry, xs):
                Sm, Wm = carry
                gt, et, tt, at = xs
                Sm = et[:, None] * Sm - tt[:, None] * gt
                Wm = (1.0 - at[:, None]) * Wm + Sm
                return ((Sm, Wm), Wm)
            outs = []
            for c0 in range(0, S, CHUNK):
                sl = slice(c0, c0 + CHUNK)
                g = _grad_fn(W_state, k[:, sl], v[:, sl]) * GRAD_SCALE
                gn = jnp.maximum(jnp.linalg.norm(g, axis=-1, keepdims=True), EPS)
                g = g * jnp.minimum(MAX_GRAD_NORM / gn, 1.0)
                g = jax.lax.stop_gradient(g)
                xs = (jnp.swapaxes(g, 0, 1), eta[:, sl].T, theta[:, sl].T, alpha[:, sl].T)
                (S_state, W_state), Wtraj = jax.lax.scan(step, (S_state, W_state), xs)
                Wtraj = jnp.swapaxes(Wtraj, 0, 1)
                T = Wtraj.shape[1]
                W1t = Wtraj[..., :D * D].reshape(B, T, D, D)
                W2t = Wtraj[..., D * D:].reshape(B, T, D, D)
                h = jax.nn.silu(jnp.einsum('btd,btod->bto', q[:, sl], W1t))
                outs.append(jnp.einsum('bto,btpo->btp', h, W2t))
            retrieved = jnp.concatenate(outs, axis=1)
            out = retrieved @ Wo.T
            out = out * jax.lax.rsqrt(jnp.mean(out * out, -1, keepdims=True) + EPS) * norm_g
            gate = hidden @ gW.T + gb
            return out * gate
        return _forward(hidden, Wk, Wv, Wq, Wo, ckw, ckb, cvw, cvb, cqw, cqb, mW1, mW2, aW, ab, eW, eb, tW, tb, norm_g, gW, gb)

    def _L0_ffn_ref(x, wqkv, q_scale, k_scale, wo, ln_g, ln_b, w1, b1, w2, b2):
        import jax, jax.numpy as jnp
        import numpy as np
        DIM = 128
        DEPTH = 2
        HEADS = 8
        DIM_HEAD = 64
        WINDOW = 64
        INNER = HEADS * DIM_HEAD
        HID = int(DIM * 4 * 2 / 3)
        B, N = (2, 1024)
        QK_SCALE = 8.0

        def shift_token(t):
            t1, t2 = jnp.split(t, 2, axis=-1)
            t2 = jnp.pad(t2, ((0, 0), (1, 0), (0, 0)))[:, :-1]
            return jnp.concatenate([t1, t2], axis=-1)

        def l2norm(t):
            return t / jnp.clip(jnp.linalg.norm(t, axis=-1, keepdims=True), 1e-12)

        def rotate_half(x):
            x1, x2 = jnp.split(x, 2, axis=-1)
            return jnp.concatenate([-x2, x1], axis=-1)

        def rotary_xpos(q, k):
            n = q.shape[-2]
            half_idx = jnp.arange(0, DIM_HEAD, 2, dtype=jnp.float32)
            inv_freq = 1.0 / 10000.0 ** (half_idx / DIM_HEAD)
            t = jnp.arange(n, dtype=jnp.float32)
            freqs = t[:, None] * inv_freq[None, :]
            freqs = jnp.concatenate([freqs, freqs], axis=-1)
            base = (half_idx + 0.4 * DIM_HEAD) / (1.4 * DIM_HEAD)
            power = (t - n // 2) / float(WINDOW // 2)
            scale = base[None, :] ** power[:, None]
            scale = jnp.concatenate([scale, scale], axis=-1)
            cos, sin = (jnp.cos(freqs), jnp.sin(freqs))
            q = q * cos * scale + rotate_half(q) * sin * scale
            k = k * cos / scale + rotate_half(k) * sin / scale
            return (q, k)

        def local_attention(q, k, v):
            b, h, n, d = q.shape
            w = n // WINDOW
            bq = q.reshape(b, h, w, WINDOW, d) * QK_SCALE
            bk = k.reshape(b, h, w, WINDOW, d)
            bv = v.reshape(b, h, w, WINDOW, d)

            def look_around(t):
                p = jnp.pad(t, ((0, 0), (0, 0), (1, 0), (0, 0), (0, 0)))
                return jnp.concatenate([p[:, :, :w], p[:, :, 1:]], axis=3)
            bk, bv = (look_around(bk), look_around(bv))
            bt = jnp.arange(n).reshape(w, WINDOW)
            btp = jnp.pad(bt, ((1, 0), (0, 0)), constant_values=-1)
            btk = jnp.concatenate([btp[:w], btp[1:]], axis=1)
            sim = jnp.einsum('bhwid,bhwjd->bhwij', bq, bk)
            i = bt[:, :, None]
            j = btk[:, None, :]
            mask = (i < j) | (i > j + WINDOW) | (j == -1)
            sim = jnp.where(mask, -jnp.finfo(sim.dtype).max, sim)
            attn = jax.nn.softmax(sim, axis=-1)
            out = jnp.einsum('bhwij,bhwjd->bhwid', attn, bv)
            return out.reshape(b, h, n, d)

        def _layer(x, wqkv, qs, ksc, wo, lg, lb, w1, b1, w2, b2):
            b, n, _ = x.shape
            h = shift_token(x)
            qkv = h @ wqkv
            q, k, v = jnp.split(qkv, 3, axis=-1)
            to_heads = lambda t: t.reshape(b, n, HEADS, DIM_HEAD).transpose(0, 2, 1, 3)
            q, k, v = (to_heads(q), to_heads(k), to_heads(v))
            q = l2norm(q) * qs
            k = l2norm(k) * ksc
            q, k = rotary_xpos(q, k)
            o = local_attention(q, k, v)
            o = o.transpose(0, 2, 1, 3).reshape(b, n, INNER)
            x = x + o @ wo
            h = shift_token(x)
            mu = h.mean(-1, keepdims=True)
            var = h.var(-1, keepdims=True)
            h = (h - mu) / jnp.sqrt(var + 1e-05) * lg + lb
            h = h @ w1 + b1
            a, g = jnp.split(h, 2, axis=-1)
            h = a * jax.nn.gelu(g, approximate=False)
            x = x + h @ w2 + b2
            return x
        for l in range(DEPTH):
            x = _layer(x, wqkv[l], q_scale[l], k_scale[l], wo[l], ln_g[l], ln_b[l], w1[l], b1[l], w2[l], b2[l])
        return x
    x = L0_attn_hidden
    x = _layernorm(x + _L0_attn_ref(x, L0_attn_Wk, L0_attn_Wv, L0_attn_Wq, L0_attn_Wo, L0_attn_ckw, L0_attn_ckb, L0_attn_cvw, L0_attn_cvb, L0_attn_cqw, L0_attn_cqb, L0_attn_mW1, L0_attn_mW2, L0_attn_aW, L0_attn_ab, L0_attn_eW, L0_attn_eb, L0_attn_tW, L0_attn_tb, L0_attn_norm_g, L0_attn_gW, L0_attn_gb), axis=-1)
    x = _layernorm(x + _L0_ffn_ref(x, L0_ffn_wqkv, L0_ffn_q_scale, L0_ffn_k_scale, L0_ffn_wo, L0_ffn_ln_g, L0_ffn_ln_b, L0_ffn_w1, L0_ffn_b1, L0_ffn_w2, L0_ffn_b2), axis=-1)
    return x

_drawn_inputs = setup_inputs


def setup_inputs(seed=0):
    import zlib

    import numpy as np

    out = dict(_drawn_inputs(seed))
    spreads = {'L0_attn_ckb': (0.0, 0.8),
     'L0_attn_cvb': (0.0, 0.8),
     'L0_attn_cqb': (0.0, 0.8),
     'L0_attn_ab': (0.0, 0.8),
     'L0_attn_eb': (0.0, 0.8),
     'L0_attn_tb': (0.0, 0.8),
     'L0_attn_norm_g': (1.0, 0.6),
     'L0_attn_gW': (0.0, 0.8),
     'L0_attn_gb': (1.0, 0.6),
     'L0_ffn_q_scale': (1.0, 0.6),
     'L0_ffn_k_scale': (1.0, 0.6),
     'L0_ffn_ln_g': (1.0, 0.6),
     'L0_ffn_ln_b': (0.0, 0.8),
     'L0_ffn_b1': (0.0, 0.8),
     'L0_ffn_b2': (0.0, 0.456)}
    factors = {'L0_attn_Wk': 8.0,
     'L0_attn_Wv': 8.0,
     'L0_attn_Wq': 8.0,
     'L0_attn_Wo': 6.269,
     'L0_attn_ckw': 8.0,
     'L0_attn_cvw': 8.0,
     'L0_attn_cqw': 8.0,
     'L0_attn_mW1': 6.019,
     'L0_attn_mW2': 5.46,
     'L0_attn_aW': 8.0,
     'L0_attn_eW': 8.0,
     'L0_attn_tW': 8.0,
     'L0_ffn_wqkv': 3.413,
     'L0_ffn_wo': 3.418,
     'L0_ffn_w1': 6.217,
     'L0_ffn_w2': 6.12}
    for name, (base, spread) in spreads.items():
        noise = np.random.default_rng([zlib.crc32(name.encode()), seed]).standard_normal(out[name].shape)
        drawn = base * np.exp(spread * noise) if base else spread * noise
        out[name] = jnp.asarray(drawn.astype(out[name].dtype))
    for name, factor in factors.items():
        out[name] = (out[name] * factor).astype(out[name].dtype)
    return out
```

```python
import numpy as np
from contextlib import ExitStack

import concourse.bass as bass
from concourse import mybir

B, T, H = 8, 256, 128
D, CH = 32, 64
NCH = T // CH
G, R = 2, 4
HEADS, DH, WIN = 8, 64, 64
INNER = HEADS * DH
HID = int(H * 4 * 2 / 3)
LAYERS = 2
PAIRS = HEADS // 2
NWIN = T // WIN
EPS = 1e-6
LN_EPS = 1e-5
NT = B * T // 128
HB = [128, 128, HID - 256]
PHASES = 2


def build(nc, t, out):
    f32, bf16 = mybir.dt.float32, mybir.dt.bfloat16
    ALU, ACT, AX = mybir.AluOpType, mybir.ActivationFunctionType, mybir.AxisListType
    MUL, ADD, SUB, MAX, MIN, POW = ALU.mult, ALU.add, ALU.subtract, ALU.max, ALU.min, ALU.pow

    with ExitStack() as ctx:
        def sb(name, shape, dt=f32):
            return ctx.enter_context(nc.sbuf_tensor(name, shape, dt))

        def sem(name):
            return ctx.enter_context(nc.semaphore(name))

        bank = [ctx.enter_context(nc.psum_tensor(f"bank{i}", [128, 512], f32)) for i in range(8)]

        ident = sb("ident", [128, 128])
        sel = sb("sel", [96, 257])
        eyes = sb("eyes", [128, CH + R])
        w_nat = sb("w_nat", [96, H])
        g_nat = sb("g_nat", [96, H])
        gw_nat = sb("gw_nat", [H, H])
        wo_nat = sb("wo_nat", [H, D])
        m_nat = sb("m_nat", [D, 2, D])
        m_rep = sb("m_rep", [D, 2, R, D])
        w2_nat = sb("w2_nat", [128, D])
        wo_stage = sb("wo_stage", [H, R, 128])
        cw = sb("cw", [128, 3, 4])
        cb = sb("cb", [128, 3])
        gate_bias = sb("gate_bias", [96, 1])
        norm_g = sb("norm_g", [128, H])
        gb = sb("gb", [128, H])
        w_t = sb("w_t", [128, 320])
        wo_bd = sb("wo_bd", [128, R, H])

        x_tok = sb("x_tok", [128, NT, H])
        x_fm = sb("x_fm", [H, B * T])
        kvq = sb("kvq", [128, 3, G, T])
        kvq_c = kvq[:, :, :, :].rearrange("p i g (c t) -> p i g c t", t=CH)
        w_end = sb("w_end", [128, 2, NCH, R])
        theta = sb("theta", [128, NCH, R])
        q_a = sb("q_a", [128, G, T])
        q_b = sb("q_b", [128, G, T])
        kc = sb("kc", [128, G, CH])
        qc = sb("qc", [128, R, G, CH])
        sig = sb("sig", [128, G, CH])
        act = sb("act", [128, G, CH])
        t_sp = sb("t_sp", [128, G, CH])
        dact = sb("dact", [128, G, CH])
        err = sb("err", [128, G, CH])
        dz = sb("dz", [128, G, CH])
        tokm = sb("tokm", [128, 4, R, D])
        sqm = sb("sqm", [128, 4, R, D])
        n4 = sb("n4", [128, 4 * R])
        n2 = sb("n2", [128, 2 * R])
        n1 = sb("n1", [128, R])
        inv = sb("inv", [128, R])
        ln_eps = sb("ln_eps", [128, 1])
        minus_half = sb("minus_half", [128, 2 * HEADS])
        coef = sb("coef", [128, R])
        gc = sb("gc", [128, 2, R, D])
        u = sb("u", [128, 2, 2, R, D])
        q1 = sb("q1", [128, R, CH])
        sig_y = sb("sig_y", [128, G, CH])
        hy = sb("hy", [128, G, CH])
        hc = sb("hc", [128, R, G, CH])
        h_a = sb("h_a", [128, G, CH])
        h_b = sb("h_b", [128, G, CH])
        am = sb("am", [128, R, CH])
        w_st = sb("w_st", [128, G, 3, D])
        s_st = sb("s_st", [128, G, 3, D])
        t_st = sb("t_st", [128, G, 3, D])
        bd = sb("bd", [128, G, 5, 128])
        ret = sb("ret", [128, G, T])
        ret_c = ret[:, :, :].rearrange("p g (c t) -> p g c t", t=CH)
        gate = sb("gate", [128, R, H])
        o_sq = sb("o_sq", [128, R, H])
        o_n = sb("o_n", [128, R, H])
        st4 = sb("st4", [128, 4, R])
        x1 = sb("x1", [128, NT, H])

        ident_bf = sb("ident_bf", [128, 128], bf16)
        masks_in = sb("masks_in", [128, 3, 2 * WIN])
        masks = sb("masks", [128, 3, 2 * WIN], bf16)
        tabs = sb("tabs", [128, 2, 2, 2, DH])
        scales = sb("scales", [128, LAYERS, 2, DH])
        cos_t = sb("cos_t", [128, LAYERS, 2, 2, DH])
        sin_t = sb("sin_t", [128, LAYERS, 2, 2, DH])
        wqkv = sb("wqkv", [H, LAYERS, 3 * INNER])
        wo_sb = sb("wo_sb", [128, LAYERS, 4, H])
        w1 = sb("w1", [H, LAYERS, 2 * HID])
        w2 = sb("w2", [128, LAYERS, 3, H])
        ln_gb = sb("ln_gb", [H, 2, LAYERS])
        b1 = sb("b1", [128, LAYERS, 6])
        mean_h = sb("mean_h", [128, 128])
        ones = sb("ones", [128, 128])
        xs = [sb(f"xs{i}", [128, 2, H]) for i in range(2)]
        fm = [sb(f"fm{i}", [H, T + 2]) for i in range(2)]
        qb = [sb(f"qb{i}", [128, NWIN, 4, 2, WIN]) for i in range(2)]
        kt = [sb(f"kt{i}", [128, 4, T]) for i in range(2)]
        ss = [sb(f"ss{i}", [128, 2 * HEADS]) for i in range(2)]
        rn = [sb(f"rn{i}", [128, 2 * HEADS]) for i in range(2)]
        h_var = sb("h_var", [128, 2])
        h_inv = sb("h_inv", [128, 2])
        diag = sb("diag", [128, 2, 128])
        nmx = [sb(f"nmx{i}", [128, 4]) for i in range(2)]
        rs = [sb(f"rs{i}", [128, 4]) for i in range(2)]
        rr = [sb(f"rr{i}", [128, 4]) for i in range(2)]
        hh = sb("hh", [128, 3, T])
        yb = [sb(f"yb{i}", [128, 2, H]) for i in range(2)]
        y_sum = sb("y_sum", [128, 2])
        y_sq = sb("y_sq", [128, 2, H])
        y_var = sb("y_var", [128, 2])
        y_inv = sb("y_inv", [128, 2])
        y_all = x_tok

        mixer_scratch = ExitStack()

        def sb_mixer(name, shape):
            return mixer_scratch.enter_context(nc.sbuf_tensor(name, shape, f32))

        sg_all = sb_mixer("sg_all", [96, B * T])
        sp_abs = sb_mixer("sp_abs", [96, B * T])
        keep_f = sb_mixer("keep_f", [128, G * T])
        eta_f = sb_mixer("eta_f", [128, G * T])
        first_f = sb_mixer("first_f", [128, G * T])
        a_cum = sb_mixer("a_cum", [128, G * T])
        b_cum = sb_mixer("b_cum", [128, G * T])
        e_cum = sb_mixer("e_cum", [128, G * T])
        keep_s = sb_mixer("keep_s", [128, R * T])
        eta_s = sb_mixer("eta_s", [128, R * T])
        eye_s = sb_mixer("eye_s", [128, R * T])
        p_mat = sb_mixer("p_mat", [128, R * T])
        m_mat = sb_mixer("m_mat", [128, R * T])
        mixer_scratch.close()
        vt = [sb(f"vt{i}", [128, 3, INNER]) for i in range(2)]
        qk = [sb(f"qk{i}", [128, 2, HEADS, DH]) for i in range(2)]
        qk_sq = sb("qk_sq", [128, 2, HEADS, DH])
        rot = [sb(f"rot{i}", [128, 2, HEADS, DH]) for i in range(2)]
        rot_s = [sb(f"rot_s{i}", [128, 2, HEADS, DH]) for i in range(2)]
        pm = [sb(f"pm{i}", [128, 4, 2 * WIN]) for i in range(2)]
        pt = sb("pt", [128, 4, 2 * WIN])
        ot = sb("ot", [128, 4, 128])
        h_cen = sb("h_cen", [H, T])
        h_sq = sb("h_sq", [H, T])
        h_ln = sb("h_ln", [H, T])
        h_rstd = sb("h_rstd", [H, T])
        h_n = sb("h_n", [H, T])
        gl = sb("gl", [128, 3, T])

        def per_chunk(a, g_dim):
            return a[:, :].rearrange("p (g c t) -> p g c t", g=g_dim, t=CH)

        a_cum_c, b_cum_c, e_cum_c = (per_chunk(a, G) for a in (a_cum, b_cum, e_cum))
        m_mat_c, p_mat_c = per_chunk(m_mat, R), per_chunk(p_mat, R)
        q_a_c = q_a[:, :, :].rearrange("p g (c t) -> p g c t", t=CH)
        q_b_c = q_b[:, :, :].rearrange("p g (c t) -> p g c t", t=CH)
        def gt(b, g=None):
            v = b[:, 0:G * CH].rearrange("p (g t) -> p g t", g=G)
            return v if g is None else v[:, g, :]

        tok_bank = bank[2][:, :].rearrange("p (k x) -> p k x", k=4)
        qk_bank = bank[3][:, 0:R * CH].rearrange("p (r t) -> p r t", r=R)
        d_bank = [bank[4 + g][:, 0:6 * D].rearrange("p (j k o) -> p j k o", j=2, k=3) for g in range(G)]
        y_bank = [bank[6 + g][:, 0:CH] for g in range(G)]

        names = """x_loaded0 x_loaded1 x_loaded2 x_loaded3 small_loaded stored
          zeroed staged x_turned w_turned fm_ready_v fm_ready_s wt_ready wo_ready st_ready0 projected
          conv_first conv_v gates_ready gates_done gates_out spread_f spread_s theta_out
          keep_done theta_done scanned first_done mats_ready qab_ready gates_abs gates_exp gates_ln gates_soft
          kc_free kc_ready qc_ready z_ready qk_ready pred_ready da_ready tok_ready y1_ready d_ready ah_ready
          y2_ready ret_done sig_ready act_ready sp_step sp_ready q1_ready err_ready dz_ready tokm_ready
          sq_ready norm_step norm_ready inv_norm ms_ready ms_inv gc_ready u_ready sigy_ready h_ready hc_v hc_s hab_ready am_ready st_step
          st_ready exp_v exp_s
          mix_out mix_gate gate_step gate_ready osq_ready mix_step on_ready cen_ready csq_ready x1_ready
          f_loaded tabs_ready masks_ready w1_ready bias_out f_zeroed ones_ready
          xs_loaded xf_turned fm_ready proj proj_out ss_step rn_ready ss_ready sum_ready c_ready s_ready rot_ready
          qk_turned qt_out kt_out score_ready max_ready exp_done rr_ready pn_ready p_turned p_out pv_done o_out
          wo_done xa_ready h_turned h_out mu_done hc_ready hsq_ready var_done diag_ready hn_ready
          w1_done gelu_done hh_ready w2_done x_ready fin_step yvar_ready yinv_ready y_ready var_ready hinv_ready bc_done
        """.split()
        s = {n: sem(n) for n in names}

        block = ctx.enter_context(nc.Block())

        def expand(copy, r):
            rows = slice(D * r, D * r + D)
            copy(bd[rows, :, 0:3, rows], w_st[rows, :, :, :])
            return copy(bd[rows, :, 3:5, rows], s_st[rows, :, 0:2, :])

        SMALL = 0
        FL = 0
        y_tiles = y_all[:, :, :].rearrange("p (b h) d -> p b h d", h=2)
        x1_tiles = x1[:, :, :].rearrange("p (b h) d -> p b h d", h=2)

        def count(per, it, j, k):
            return it * (4 * per) + (j * per + k)

        def spot(j):
            return j // 2 % 2, j % 2

        def over_items(eng, first, item):
            first()
            with eng.Fori(0, PAIRS - 1) as it:
                for j in range(4):
                    item(it, j, True)
            for j in range(4):
                item(PAIRS - 1, j, j < 3)

        def heads4(b):
            return bank[b][:, :].rearrange("p (k x) -> p k x", k=4)


        @block.sync
        def _(sp):
            nonlocal SMALL, FL
            for i in range(4):
                sp.dma_start(x_tok[:, 4 * i:4 * i + 4, :],
                             t["hidden"][2 * i:2 * i + 2].rearrange("b (h p) d -> p (b h) d", p=128)
                             ).then_inc(s[f"x_loaded{i}"], 16)
                if i == 0:
                    sp.dma_start(ident[:, :], t["c_ident"]).then_inc(s["small_loaded"], 16)
                    SMALL += 1
            loads = [(w_nat[0:32, :], t["Wk"]), (w_nat[32:64, :], t["Wv"]), (w_nat[64:96, :], t["Wq"]),
                     (g_nat[0:32, :], t["aW"]), (g_nat[32:64, :], t["eW"]), (g_nat[64:96, :], t["tW"]),
                     (gw_nat[:, :], t["gW"]), (wo_nat[:, :], t["Wo"]),
                     (m_nat[:, 0, :], t["mW1"]), (m_nat[:, 1, :], t["mW2"]),
                     (sel[:, :], t["c_sel"]), (eyes[:, :], t["c_eyes"]),
                     (gate_bias[0:32, :], t["ab"].unsqueeze(1)), (gate_bias[32:64, :], t["eb"].unsqueeze(1)),
                     (gate_bias[64:96, :], t["tb"].unsqueeze(1)),
                     (norm_g[:, :], t["norm_g"].partition_broadcast(128)),
                     (gb[:, :], t["gb"].partition_broadcast(128))]
            for r in range(R):
                rows = slice(D * r, D * r + D)
                loads.append((w2_nat[rows, :], t["mW2"]))
                for i, (w, b) in enumerate((("ckw", "ckb"), ("cvw", "cvb"), ("cqw", "cqb"))):
                    loads.append((cw[rows, i, :], t[w]))
                    loads.append((cb[rows, i:i + 1], t[b].unsqueeze(1)))
            for dst, src in loads:
                sp.dma_start(dst, src).then_inc(s["small_loaded"], 16)
            SMALL += len(loads)
            f_loads = []
            for l in range(LAYERS):
                f_loads += [(wqkv[:, l, :], t["f_wqkv"][l]),
                            (wo_sb[:, l, :, :], t["f_wo"][l].rearrange("(k p) n -> p k n", p=128)),
                            (w1[:, l, :], t["f_w1"][l]),
                            (w2[:, l, 0:2, :], t["f_w2"][l, 0:256].rearrange("(k p) n -> p k n", p=128)),
                            (w2[0:HB[2], l, 2, :], t["f_w2"][l, 256:HID]),
                            (w2[HB[2]:HB[2] + 1, l, 2, :], t["f_b2"][l:l + 1]),
                            (scales[:, l, 0, :], t["f_q_scale"][l].partition_broadcast(128)),
                            (scales[:, l, 1, :], t["f_k_scale"][l].partition_broadcast(128)),
                            (ln_gb[:, 0, l:l + 1], t["f_ln_g"][l].unsqueeze(1)),
                            (ln_gb[:, 1, l:l + 1], t["f_ln_b"][l].unsqueeze(1))]
                for part in range(2):
                    for k in range(3):
                        at = HID * part + 128 * k
                        f_loads.append((b1[0:HB[k], l, 3 * part + k:3 * part + k + 1],
                                        t["f_b1"][l, at:at + HB[k]].unsqueeze(1)))
            f_loads += [(tabs[:, :, :, :, :], t["c_tabs"]), (masks_in[:, :, :], t["c_masks"])]
            for dst, src in f_loads:
                sp.dma_start(dst, src).then_inc(s["f_loaded"], 16)
            FL = 16 * len(f_loads)
            if PHASES == 2:
                with sp.Fori(0, PAIRS) as it:
                    for sl in range(2):
                        sp.wait_ge(s["y_ready"], it * 2 + (sl + 1))
                        sp.dma_start(out[it * 2 + sl, :, :].rearrange("(h p) d -> p h d", p=128),
                                     y_tiles[:, it * 2 + sl, :, :]).then_inc(s["stored"], 16)
                sp.wait_ge(s["stored"], 16 * B)
            if PHASES == 1:
                for i in range(4):
                    sp.wait_ge(s["x1_ready"], 4)
                    sp.dma_start(out[2 * i:2 * i + 2].rearrange("b (h p) d -> p (b h) d", p=128),
                                 x1[:, 4 * i:4 * i + 4, :]).then_inc(s["stored"], 16)
                sp.wait_ge(s["stored"], 64)

        @block.gpsimd
        def _(po):
            po.memset(bd[:, :, :, :], 0.0)
            po.memset(hc[:, :, :, :], 0.0)
            po.memset(s_st[:, :, :, :], 0.0)
            po.memset(minus_half[:, :], -0.5)
            po.memset(ln_eps[:, :], LN_EPS)
            po.memset(first_f[:, :], 0.0).then_inc(s["zeroed"], 1)
            po.wait_ge(s["scanned"], 3)
            po.wait_ge(s["conv_v"], 3)
            po.tensor_tensor(q_a[:, :, :], kvq[:, 2, :, :], a_cum[:, :].rearrange("p (g t) -> p g t", g=G), MUL)
            po.tensor_tensor(q_b[:, :, :], kvq[:, 2, :, :], b_cum[:, :].rearrange("p (g t) -> p g t", g=G), MUL
                             ).then_inc(s["qab_ready"], 1)
            with po.Fori(0, NCH) as c:
                po.wait_ge(s["mats_ready"], 1)
                po.wait_ge(s["kc_free"], c + 1)
                po.tensor_copy(kc[:, :, :], kvq_c[:, 0, :, c, :]).then_inc(s["kc_ready"], 1)
                for g in range(G):
                    ins = po.tensor_tensor(qc[:, :, g, :],
                                           kvq_c[:, 2, g, c, :].unsqueeze(1).to_broadcast([128, R, CH]),
                                           eyes[:, CH:CH + R].unsqueeze(2).to_broadcast([128, R, CH]), MUL)
                ins.then_inc(s["qc_ready"], 1)
                po.wait_ge(s["act_ready"], c + 1)
                po.tensor_tensor(t_sp[:, :, :], act[:, :, :], sig[:, :, :], MUL).then_inc(s["sp_step"], 1)
                po.wait_ge(s["sp_step"], 2 * c + 1)
                po.tensor_tensor(t_sp[:, :, :], act[:, :, :], t_sp[:, :, :], SUB).then_inc(s["sp_step"], 1)
                po.wait_ge(s["sp_step"], 2 * c + 2)
                po.tensor_tensor(dact[:, :, :], t_sp[:, :, :], sig[:, :, :], ADD).then_inc(s["sp_ready"], 1)
                po.wait_ge(s["norm_ready"], c + 1)
                po.tensor_tensor(inv[:, :], n1[:, :], minus_half[:, 0:R], POW).then_inc(s["inv_norm"], 1)
                po.wait_ge(s["h_ready"], c + 1)
                po.tensor_tensor(h_a[:, :, :], hy[:, :, :], a_cum_c[:, :, c, :], MUL)
                po.tensor_tensor(h_b[:, :, :], hy[:, :, :], b_cum_c[:, :, c, :], MUL).then_inc(s["hab_ready"], 1)
            for k in range(8):
                po.wait_ge(s["ms_ready"], k + 1)
                po.tensor_tensor(st4[:, 1 + 2 * (k % 2), :], st4[:, 1 + 2 * (k % 2), :], minus_half[:, 0:R], POW
                                 ).then_inc(s["ms_inv"], 1)

            for i in range(2):
                po.memset(qb[i][:, :, :, :, :], 0.0)
                po.memset(fm[i][:, :], 0.0)
            po.memset(mean_h[:, :], 1.0 / H)
            po.memset(ones[:, :], 1.0)
            po.memset(hh[:, :, :], 1.0).then_inc(s["f_zeroed"], 1)
            po.wait_ge(s["f_loaded"], FL)
            q = DH // 2
            for l in range(LAYERS):
                for k in range(2):
                    shape = [128, 2, DH]
                    po.tensor_tensor(cos_t[:, l, :, k, :], tabs[:, :, 0, k, :],
                                     scales[:, l, k, :].unsqueeze(1).to_broadcast(shape), MUL)
                    for to, fro in ((slice(0, q), slice(q, DH)), (slice(q, DH), slice(0, q))):
                        ins = po.tensor_tensor(sin_t[:, l, :, k, to], tabs[:, :, 1, k, to],
                                               scales[:, l, k, fro].unsqueeze(1).to_broadcast([128, 2, q]), MUL)
            ins.then_inc(s["tabs_ready"], 1)
            po.sem_inc(s["x_ready"], 1)

            def load_xs(it, j):
                l, sl = spot(j)
                if l == 0:
                    po.wait_ge(s["x1_ready"], 4)
                    if not (isinstance(it, int) and j < 2 and it == 0):
                        po.wait_ge(s["x_ready"], count(1, it, j, 0))
                    po.tensor_copy(xs[sl][:, :, :], x1_tiles[:, it * 2 + (j // 4 * 2 + sl), :, :]
                                   ).then_inc(s["xs_loaded"], 1)

            def sin_part(it, j, tile, kind):
                l, sl = spot(j)
                po.wait_ge(s["proj_out"], count(6, it, j, 3 * tile + kind + 1))
                if kind == 0 and not (isinstance(it, int) and it == 0 and j == 0):
                    po.wait_ge(s["rot_ready"], count(2, it, j, tile - 1))
                for to, fro in ((slice(0, q), slice(q, DH)), (slice(q, DH), slice(0, q))):
                    ins = po.tensor_tensor(rot_s[tile][:, kind, :, to], qk[tile][:, kind, :, fro],
                                           sin_t[:, l, tile, kind, to].unsqueeze(1).to_broadcast([128, HEADS, q]), MUL)
                ins.then_inc(s["s_ready"], 1)

            def inv_norms(it, j, tile):
                po.wait_ge(s["ss_ready"], count(2, it, j, tile + 1))
                po.tensor_tensor(rn[tile][:, :], ss[tile][:, :], minus_half[:, :], POW).then_inc(s["rn_ready"], 1)

            def inv_std(it, j):
                po.wait_ge(s["var_ready"], count(1, it, j, 1))
                po.tensor_tensor(h_inv[:, :], h_var[:, :], minus_half[:, 0:2], POW).then_inc(s["hinv_ready"], 1)

            def normalise(it, j, w):
                po.wait_ge(s["rr_ready"], count(4, it, j, w + 1))
                po.tensor_tensor(pm[w % 2][:, :, :], pm[w % 2][:, :, :],
                                 rr[w % 2][:, :].unsqueeze(2).to_broadcast([128, 4, 2 * WIN]), MUL
                                 ).then_inc(s["pn_ready"], 1)

            def first():
                load_xs(0, 0)
                for tile in range(2):
                    sin_part(0, 0, tile, 0)
                    sin_part(0, 0, tile, 1)
                    inv_norms(0, 0, tile)

            def item(it, j, more):
                l, sl = spot(j)
                def ahead(step, *a):
                    if more:
                        step(it, j + 1, *a)

                ahead(load_xs)
                normalise(it, j, 0)
                normalise(it, j, 1)
                normalise(it, j, 2)
                ahead(sin_part, 0, 0)
                normalise(it, j, 3)
                ahead(sin_part, 0, 1)
                ahead(inv_norms, 0)
                ahead(sin_part, 1, 0)
                ahead(sin_part, 1, 1)
                inv_std(it, j)
                ahead(inv_norms, 1)
                if l == 1:
                    po.wait_ge(s["yvar_ready"], it * 2 + (sl + 1))
                    po.tensor_tensor(y_inv[:, :], y_var[:, :], minus_half[:, 0:2], POW).then_inc(s["yinv_ready"], 1)

            over_items(po, first, item)

        @block.tensor
        def _(pe):
            for i in range(4):
                pe.wait_ge(s[f"x_loaded{i}"], 16)
                if i == 0:
                    pe.wait_ge(s["small_loaded"], 16 * SMALL)
                for j in range(4):
                    ins = pe.transpose(bank[i][:, 128 * j:128 * j + 128], x_tok[:, 4 * i + j, :], ident[:, :])
                ins.then_inc(s["x_turned"], 1)
            pe.transpose(bank[4][:, 0:96], w_nat[:, :], ident[0:96, 0:96])
            pe.transpose(bank[4][:, 96:192], g_nat[:, :], ident[0:96, 0:96])
            pe.transpose(bank[4][:, 192:320], gw_nat[:, :], ident[:, :]).then_inc(s["w_turned"], 1)
            pe.wait_ge(s["staged"], 1)
            for r in range(R):
                ins = pe.transpose(bank[5][:, 128 * r:128 * r + 128], wo_stage[:, r, :], ident[:, :])
            ins.then_inc(s["w_turned"], 1)
            for k in range(2):
                ins = pe.transpose(bank[6][:, D * k:D * k + D], m_rep[:, k, :, :], ident[0:D, 0:D])
            ins.then_inc(s["w_turned"], 1)
            pe.wait_ge(s["wt_ready"], 1)
            pe.wait_ge(s["fm_ready_v"], 2)
            pe.wait_ge(s["fm_ready_s"], 2)
            for i in range(3):
                for g in range(G):
                    for r in range(R):
                        b = R * g + r
                        ins = pe.matmul(bank[i][D * r:D * r + D, T * g:T * g + T], w_t[:, D * i:D * i + D],
                                        x_fm[:, T * b:T * b + T], start=True, stop=True)
                ins.then_inc(s["projected"], 1)
            pe.wait_ge(s["wo_ready"], 1)
            pe.wait_ge(s["st_ready0"], 1)
            for i in range(4):
                pe.matmul(bank[3 + i][0:96, :], w_t[:, 96:192], x_fm[:, 512 * i:512 * i + 512],
                          start=True, stop=True).then_inc(s["gates_out"], 1)
            pe.wait_ge(s["gates_ready"], 4)
            pe.wait_ge(s["gates_soft"], 1)
            pe.wait_ge(s["conv_v"], 3)
            for i, col in ((7, 0), (0, 128)):
                for g in range(G):
                    for r in range(R):
                        b = R * g + r
                        ins = pe.matmul(bank[i][D * r:D * r + D, T * g:T * g + T], sel[:, col:col + D],
                                        sg_all[:, T * b:T * b + T], start=True, stop=True)
                ins.then_inc(s["spread_f"], 1)
            for i, col in ((1, 0), (3, 128)):
                for half in range(2):
                    for g in range(G):
                        at = T * R * g + 512 * half
                        ins = pe.matmul(bank[i + half][CH * g:CH * g + CH, :], sel[:, col:col + CH],
                                        sg_all[:, at:at + 512], start=True, stop=True)
                ins.then_inc(s["spread_s"], 1)
            for g in range(G):
                for r in range(R):
                    for c in range(NCH):
                        at = T * (R * g + r) + CH * c
                        ins = pe.matmul(bank[5][CH * g:CH * g + CH, R * c + r:R * c + r + 1],
                                        sg_all[:, at:at + CH], sel[:, 256:257], start=True, stop=True)
            ins.then_inc(s["theta_out"], 1)
            pe.wait_ge(s["mats_ready"], 1)
            pe.wait_ge(s["qab_ready"], 1)
            pe.sem_inc(s["kc_free"], 1)
            with pe.Fori(0, NCH) as c:
                pe.wait_ge(s["kc_ready"], c + 1)
                pe.wait_ge(s["exp_v"], c + 1)
                pe.wait_ge(s["exp_s"], c + 1)
                for g in range(G):
                    ins = pe.matmul(gt(bank[0], g), bd[:, g, 0, :], kc[:, g, :], start=True, stop=True)
                ins.then_inc(s["z_ready"], 1)
                pe.wait_ge(s["qc_ready"], c + 1)
                for g in range(G):
                    ins = pe.matmul(qk_bank[CH * g:CH * g + CH, :, :], kc[:, g, :], qc[:, :, g, :],
                                    start=True, stop=True)
                ins.then_inc(s["qk_ready"], 1)
                pe.wait_ge(s["act_ready"], c + 1)
                for g in range(G):
                    ins = pe.matmul(gt(bank[1], g), bd[:, g, 1, :], act[:, g, :], start=True, stop=True)
                ins.then_inc(s["pred_ready"], 1)
                pe.transpose(tok_bank[:, 3, :], kc[:, :, :], ident[:, :])
                pe.transpose(tok_bank[:, 0, :], act[:, :, :], ident[:, :])
                pe.wait_ge(s["err_ready"], c + 1)
                for g in range(G):
                    ins = pe.matmul(gt(bank[0], g), bd[:, g, 2, :], err[:, g, :], start=True, stop=True)
                ins.then_inc(s["da_ready"], 1)
                pe.transpose(tok_bank[:, 2, :], err[:, :, :], ident[:, :])
                pe.wait_ge(s["dz_ready"], c + 1)
                pe.transpose(tok_bank[:, 1, :], dz[:, :, :], ident[:, :]).then_inc(s["tok_ready"], 1)
                pe.wait_ge(s["ret_done"], c + 1)
                pe.wait_ge(s["gc_ready"], c + 1)
                pe.wait_ge(s["q1_ready"], c + 1)
                for g in range(G):
                    pe.matmul(y_bank[g], bd[:, g, 0, :], q_a_c[:, g, c, :], start=True, stop=False)
                    pe.matmul(y_bank[g], bd[:, g, 3, :], q_b_c[:, g, c, :], start=False, stop=True)
                for r in range(R):
                    for g in range(G):
                        rows, cols = slice(CH * g, CH * g + CH), slice(D * r, D * r + D)
                        ins = pe.matmul(y_bank[g][cols, :], gc[rows, 0, r, :], q1[rows, r, :],
                                        start=False, stop=True, skip_group_check=True)
                ins.then_inc(s["y1_ready"], 1)
                pe.wait_ge(s["u_ready"], c + 1)
                pe.sem_inc(s["kc_free"], 1)
                for r in range(R):
                    for g in range(G):
                        rows, cols = slice(CH * g, CH * g + CH), slice(D * r, D * r + D)
                        pe.matmul(d_bank[g][cols, :, 0, :], tokm[rows, 3, r, :], u[rows, :, 0, r, :],
                                  start=True, stop=True)
                        pe.matmul(d_bank[g][cols, :, 1, :], tokm[rows, 0, r, :], u[rows, :, 1, r, :],
                                  start=True, stop=True)
                        for j in range(2):
                            ins = pe.matmul(d_bank[g][cols, j, 2, :], u[rows, j, 1, r, :], tokm[rows, 0, r, :],
                                            start=True, stop=True)
                ins.then_inc(s["d_ready"], 1)
                pe.wait_ge(s["hc_v"], c + 1)
                pe.wait_ge(s["hc_s"], c + 1)
                for g in range(G):
                    ins = pe.matmul(qk_bank[CH * g:CH * g + CH, :, :], act[:, g, :], hc[:, :, g, :],
                                    start=True, stop=True)
                ins.then_inc(s["ah_ready"], 1)
                pe.wait_ge(s["hab_ready"], c + 1)
                pe.wait_ge(s["am_ready"], c + 1)
                for g in range(G):
                    pe.matmul(y_bank[g], bd[:, g, 1, :], h_a[:, g, :], start=True, stop=False)
                    pe.matmul(y_bank[g], bd[:, g, 4, :], h_b[:, g, :], start=False, stop=True)
                for r in range(R):
                    for g in range(G):
                        rows, cols = slice(CH * g, CH * g + CH), slice(D * r, D * r + D)
                        ins = pe.matmul(y_bank[g][cols, :], gc[rows, 1, r, :], am[rows, r, :],
                                        start=False, stop=True, skip_group_check=True)
                ins.then_inc(s["y2_ready"], 1)
            pe.wait_ge(s["ret_done"], NCH + 1)
            for m in range(4):
                g, half = m // 2, m % 2
                if m >= 2:
                    pe.wait_ge(s["on_ready"], m - 1)
                pe.matmul(bank[m % 2][:, :], ret[:, g, 128 * half:128 * half + 128], wo_bd[:, :, :],
                          start=True, stop=True).then_inc(s["mix_out"], 1)
                for r in range(R):
                    at = T * (R * g + r) + 128 * half
                    ins = pe.matmul(bank[2 + m % 2][:, 128 * r:128 * r + 128], x_fm[:, at:at + 128],
                                    w_t[:, 192:320], start=True, stop=True)
                ins.then_inc(s["mix_gate"], 1)

            pe.wait_ge(s["f_loaded"], FL)
            for l in range(LAYERS):
                for part in range(2):
                    for k in range(3):
                        at_w = HID * part + 128 * k
                        col = 6 * l + 3 * part + k
                        ins = pe.matmul(bank[7][0:HB[k], col:col + 1], w1[:, l, at_w:at_w + HB[k]],
                                        ln_gb[:, 1, l:l + 1], start=True, stop=True)
            ins.then_inc(s["bias_out"], 1)

            def turn_x(it, j):
                l, sl = spot(j)
                if l == 0:
                    pe.wait_ge(s["xs_loaded"], it * 2 + (j // 4 * 2 + sl + 1))
                else:
                    pe.wait_ge(s["x_ready"], count(1, it, j, 0))
                if not (isinstance(it, int) and it == 0 and j == 0):
                    pe.wait_ge(s["kt_out"], count(2, it, j, 0))
                for tile in range(2):
                    ins = pe.transpose(bank[6][:, 128 * tile:128 * tile + 128], xs[sl][:, tile, :], ident[:, :])
                ins.then_inc(s["xf_turned"], 1)

            def project(it, j, k):
                l, sl = spot(j)
                if k == 0:
                    pe.wait_ge(s["fm_ready"], count(1, it, j, 1))
                if not (isinstance(it, int) and it == 0 and j == 0 and k < 2):
                    pe.wait_ge(s["proj_out"], count(6, it, j, k - 1))
                tile, kind = k // 3, k % 3
                pe.matmul(bank[4 + k % 2][:, :], fm[sl][:, 128 * tile:128 * tile + 128],
                          wqkv[:, l, INNER * kind:INNER * kind + INNER], start=True, stop=True).then_inc(s["proj"], 1)

            def turn_qk(it, j, i):
                tile, kind = i // 2, i % 2
                pe.wait_ge(s["rot_ready"], count(2, it, j, tile + 1))
                if i:
                    pe.wait_ge(s["qt_out" if i % 2 else "kt_out"], count(2, it, j, (i + 1) // 2))
                for h in range(4):
                    ins = pe.transpose(bank[6][:, 128 * h:128 * h + 128], rot[tile][:, kind, 2 * h:2 * h + 2, :],
                                       ident[:, :])
                ins.then_inc(s["qk_turned"], 1)

            def scores(it, j, w):
                l, sl = spot(j)
                if w == 0:
                    pe.wait_ge(s["qt_out"], count(2, it, j, 2))
                    pe.wait_ge(s["kt_out"], count(2, it, j, 2))
                if w >= 2:
                    pe.wait_ge(s["exp_done"], count(4, it, j, w - 1))
                b = w % 2
                kind = (0, 1, 2, 1)[w]
                pe.matmul(heads4(b), ident_bf[:, :], masks[:, kind, :].unsqueeze(1).to_broadcast([128, 4, 2 * WIN]),
                          start=True, stop=False)
                for h in range(4):
                    q_blocks = qb[sl][:, w, h, :, :]
                    if w == 2:
                        for c, key in ((0, 2 * WIN), (WIN, WIN)):
                            ins = pe.matmul(heads4(b)[:, h, c:c + WIN], q_blocks, kt[sl][:, h, key:key + WIN],
                                            start=False, stop=(h == 3 and c > 0))
                    else:
                        key = 0 if w < 2 else 2 * WIN
                        ins = pe.matmul(heads4(b)[:, h, :], q_blocks, kt[sl][:, h, key:key + 2 * WIN],
                                        start=False, stop=(h == 3))
                ins.then_inc(s["score_ready"], 1)

            def turn_p(it, j, w):
                pe.wait_ge(s["pn_ready"], count(4, it, j, w + 1))
                for h in range(4):
                    ins = pe.transpose(heads4(2)[:, h, :], pm[w % 2][:, h, :], ident[:, :])
                ins.then_inc(s["p_turned"], 1)

            def weigh_v(it, j, w):
                l, sl = spot(j)
                src = (0, 0, 2, 1)[w]
                pe.wait_ge(s["p_out"], count(4, it, j, w + 1))
                for h in range(4):
                    for e in range(2):
                        c = 128 * h + WIN * (w % 2)
                        ins = pe.matmul(bank[3][DH * e:DH * e + DH, c:c + WIN],
                                        vt[sl][:, src, DH * (2 * h + e):DH * (2 * h + e) + DH],
                                        pt[:, h, WIN * e:WIN * e + WIN], start=True, stop=True)
                if w % 2:
                    ins.then_inc(s["pv_done"], 1)

            def project_o(it, j, tile):
                l, sl = spot(j)
                pe.wait_ge(s["o_out"], count(2, it, j, tile + 1))
                if tile:
                    pe.wait_ge(s["xa_ready"], count(2, it, j, tile))
                else:
                    pe.wait_ge(s["x_ready"], count(1, it, j, 1))
                for h in range(4):
                    ins = pe.matmul(bank[7][:, 128 * tile:128 * tile + 128], ot[:, h, :], wo_sb[:, l, h, :],
                                    start=(h == 0), stop=(h == 3))
                ins.then_inc(s["wo_done"], 1)

            def turn_h(it, j):
                l, sl = spot(j)
                pe.wait_ge(s["xa_ready"], count(2, it, j, 2))
                for tile in range(2):
                    ins = pe.transpose(bank[3][:, 128 * tile:128 * tile + 128], xs[sl][:, tile, :], ident[:, :])
                ins.then_inc(s["h_turned"], 1)

            def mean(it, j):
                l, sl = spot(j)
                pe.wait_ge(s["h_out"], count(1, it, j, 1))
                pe.matmul(bank[7][:, 0:T], mean_h[:, :], fm[sl][:, 0:T], start=True, stop=True
                          ).then_inc(s["mu_done"], 1)

            def variance(it, j):
                pe.wait_ge(s["hsq_ready"], count(1, it, j, 1))
                for tile in range(2):
                    ins = pe.matmul(bank[3][:, tile:tile + 1], h_sq[:, 128 * tile:128 * tile + 128], mean_h[:, 0:1],
                                    start=True, stop=True)
                ins.then_inc(s["var_done"], 1)

            def spread_inv(it, j):
                pe.wait_ge(s["diag_ready"], count(1, it, j, 1))
                for tile in range(2):
                    ins = pe.matmul(bank[3][:, 128 * tile:128 * tile + 128], ones[:, :], diag[:, tile, :],
                                    start=True, stop=True)
                ins.then_inc(s["bc_done"], 1)

            def ffn_up(it, j, k):
                l, sl = spot(j)
                if k == 0:
                    pe.wait_ge(s["hn_ready"], count(1, it, j, 1))
                if k == 2:
                    pe.wait_ge(s["hh_ready"], count(3, it, j, 1))
                for part, c in ((1, 0), (0, T)):
                    at_w = HID * part + 128 * k
                    ins = pe.matmul(bank[k % 2][0:HB[k], c:c + T], w1[:, l, at_w:at_w + HB[k]], h_n[:, :],
                                    start=True, stop=True)
                ins.then_inc(s["w1_done"], 1)

            def ffn_down(it, j):
                l, sl = spot(j)
                pe.wait_ge(s["hh_ready"], count(3, it, j, 3))
                for tile in range(2):
                    for k in range(3):
                        rows = HB[k] + (k == 2)
                        ins = pe.matmul(bank[7][:, 128 * tile:128 * tile + 128],
                                        hh[0:rows, k, 128 * tile:128 * tile + 128], w2[0:rows, l, k, :],
                                        start=(k == 0), stop=(k == 2))
                ins.then_inc(s["w2_done"], 1)

            def first():
                pe.wait_ge(s["f_zeroed"], 1)
                pe.wait_ge(s["masks_ready"], 1)
                turn_x(0, 0)
                for k in range(6):
                    project(0, 0, k)
                for i in range(4):
                    turn_qk(0, 0, i)
                pe.wait_ge(s["w1_ready"], 1)

            def item(it, j, more):
                def ahead(step, *a):
                    if more:
                        step(it, j + 1, *a)

                scores(it, j, 0)
                scores(it, j, 1)
                ahead(turn_x)
                scores(it, j, 2)
                turn_p(it, j, 0)
                ahead(project, 0)
                weigh_v(it, j, 0)
                ahead(project, 1)
                turn_p(it, j, 1)
                scores(it, j, 3)
                weigh_v(it, j, 1)
                turn_p(it, j, 2)
                ahead(project, 2)
                project_o(it, j, 0)
                weigh_v(it, j, 2)
                ahead(project, 3)
                turn_p(it, j, 3)
                ahead(project, 4)
                weigh_v(it, j, 3)
                ahead(project, 5)
                project_o(it, j, 1)
                turn_h(it, j)
                ahead(turn_qk, 0)
                mean(it, j)
                ahead(turn_qk, 1)
                variance(it, j)
                spread_inv(it, j)
                for k in range(3):
                    ffn_up(it, j, k)
                ahead(turn_qk, 2)
                ffn_down(it, j)
                ahead(turn_qk, 3)

            over_items(pe, first, item)

        @block.scalar
        def _(ac):
            for i in (1, 3):
                ac.wait_ge(s["x_turned"], i + 1)
                ac.activation(x_fm[:, 512 * i:512 * i + 512], bank[i][:, :], ACT.Copy).then_inc(s["fm_ready_s"], 1)
            ac.wait_ge(s["w_turned"], 1)
            ac.activation(w_t[:, :], bank[4][:, 0:320], ACT.Copy).then_inc(s["wt_ready"], 1)
            for i in range(3):
                ac.wait_ge(s["projected"], i + 1)
                ac.activation(kvq[:, i, :, :], bank[i][:, :].rearrange("p (g t) -> p g t", g=G), ACT.Identity,
                              bias=cb[:, i:i + 1], scale=cw[:, i, 3:4]).then_inc(s["conv_first"], 1)
            for i in range(4):
                cols = slice(512 * i, 512 * i + 512)
                ac.wait_ge(s["gates_out"], i + 1)
                ac.activation(sg_all[0:64, cols], bank[3 + i][0:64, :], ACT.Sigmoid, bias=gate_bias[0:64, :]
                              ).then_inc(s["gates_ready"], 1)
            for i in range(4):
                cols = slice(512 * i, 512 * i + 512)
                ins = ac.activation(sp_abs[64:96, cols], bank[3 + i][64:96, :], ACT.Abs, bias=gate_bias[64:96, :])
            ins.then_inc(s["gates_abs"], 1)
            ac.wait_ge(s["gates_abs"], 1)
            ac.activation(sp_abs[64:96, :], sp_abs[64:96, :], ACT.Exp, scale=-1.0).then_inc(s["gates_exp"], 1)
            ac.wait_ge(s["gates_exp"], 1)
            ac.activation(sp_abs[64:96, :], sp_abs[64:96, :], ACT.Ln, bias=1.0).then_inc(s["gates_ln"], 1)
            ac.sem_inc(s["ret_done"], 1)
            ac.wait_ge(s["zeroed"], 1)
            ac.wait_ge(s["st_ready0"], 1)
            expand(ac.copy, 2)
            expand(ac.copy, 3).then_inc(s["exp_s"], 1)
            with ac.Fori(0, NCH) as c:
                ac.wait_ge(s["z_ready"], c + 1)
                ac.activation(sig[:, :, :], gt(bank[0]), ACT.Sigmoid).then_inc(s["sig_ready"], 1)
                ac.wait_ge(s["tokm_ready"], c + 1)
                ac.activation(sqm[:, :, :, :], tokm[:, :, :, :], ACT.Square).then_inc(s["sq_ready"], 1)
                ac.wait_ge(s["y1_ready"], c + 1)
                for g in range(G):
                    ins = ac.activation(sig_y[:, g, :], y_bank[g], ACT.Sigmoid)
                ins.then_inc(s["sigy_ready"], 1)
                ac.wait_ge(s["h_ready"], c + 1)
                for r in (2, 3):
                    rows = slice(D * r, D * r + D)
                    ins = ac.activation(hc[rows, r, :, :], hy[rows, :, :], ACT.Copy)
                ins.then_inc(s["hc_s"], 1)
                ac.wait_ge(s["y2_ready"], c + 1)
                for g in range(G):
                    ins = ac.activation(ret_c[:, g, c, :], y_bank[g], ACT.Copy)
                ins.then_inc(s["ret_done"], 1)
                ac.wait_ge(s["st_ready"], c + 1)
                expand(ac.copy, 2)
                expand(ac.copy, 3).then_inc(s["exp_s"], 1)
            for m in range(4):
                ac.wait_ge(s["mix_out"], m + 1)
                if m >= 1:
                    ac.wait_ge(s["x1_ready"], m)
                ac.activation(o_sq[:, :, :], bank[m % 2][:, :].rearrange("p (r h) -> p r h", r=R), ACT.Square
                              ).then_inc(s["osq_ready"], 1)
                ac.wait_ge(s["cen_ready"], m + 1)
                ac.activation(o_sq[:, :, :], o_n[:, :, :], ACT.Square).then_inc(s["csq_ready"], 1)


            def copy_x(it, j, src, turned, ready):
                l, sl = spot(j)
                ac.wait_ge(s[turned], count(1, it, j, 1))
                ac.activation(fm[sl][0:64, 0:T], src[0:64, 0:T], ACT.Copy)
                ac.activation(fm[sl][64:128, 1:T + 1], src[64:128, 0:T], ACT.Copy).then_inc(s[ready], 1)

            def copy_proj(it, j, k):
                l, sl = spot(j)
                tile, kind = k // 3, k % 3
                ac.wait_ge(s["proj"], count(6, it, j, k + 1))
                src = bank[4 + k % 2]
                if kind < 2:
                    if kind == 0 and not (isinstance(it, int) and it == 0 and j == 0):
                        ac.wait_ge(s["rot_ready"], count(2, it, j, tile - 1))
                    if not (isinstance(it, int) and it == 0 and j == 0 and tile == 0):
                        ac.wait_ge(s["ss_ready"], count(2, it, j, tile))
                    view = src[:, :].rearrange("p (h d) -> p h d", d=DH)
                    ac.activation(qk_sq[:, kind, :, :], view, ACT.Square)
                    ac.activation(qk[tile][:, kind, :, :], view, ACT.Copy).then_inc(s["proj_out"], 1)
                else:
                    ac.activation(vt[sl][:, tile, :], src[:, :], ACT.Copy)
                    rows = slice(64, 128) if tile == 0 else slice(0, 64)
                    ac.activation(vt[sl][rows, 2, :], src[rows, :], ACT.Copy).then_inc(s["proj_out"], 1)

            def exps(it, j, w):
                ac.wait_ge(s["max_ready"], count(4, it, j, w + 1))
                if w >= 2:
                    ac.wait_ge(s["p_turned"], count(4, it, j, w - 1))
                for h in range(4):
                    ins = ac.activation(pm[w % 2][:, h, :], heads4(w % 2)[:, h, :], ACT.Exp, bias=nmx[w % 2][:, h:h + 1],
                                        accum_out=rs[w % 2][:, h:h + 1])
                ins.then_inc(s["exp_done"], 1)

            def copy_o(it, j, tile):
                ac.wait_ge(s["pv_done"], count(2, it, j, tile + 1))
                ac.activation(ot[:, :, :], heads4(3), ACT.Copy).then_inc(s["o_out"], 1)

            def copy_q(it, j, tile):
                l, sl = spot(j)
                ac.wait_ge(s["qk_turned"], count(4, it, j, 2 * tile + 1))
                for e in range(2):
                    rows = slice(DH * e, DH * e + DH)
                    ins = ac.activation(qb[sl][rows, 2 * tile:2 * tile + 2, :, e, :].rearrange("p w h q -> p h w q"),
                                        bank[6][rows, :].rearrange("p (h w q) -> p h w q", h=4, w=2), ACT.Copy)
                ins.then_inc(s["qt_out"], 1)

            def squares(it, j):
                ac.wait_ge(s["hc_ready"], count(1, it, j, 1))
                ac.activation(h_sq[:, :], h_cen[:, :], ACT.Square).then_inc(s["hsq_ready"], 1)

            def gelu(it, j, k):
                l, sl = spot(j)
                ac.wait_ge(s["w1_done"], count(3, it, j, k + 1))
                ac.activation(gl[0:HB[k], k, :], bank[k % 2][0:HB[k], 0:T], ACT.Gelu, bias=b1[0:HB[k], l, 3 + k:4 + k]
                              ).then_inc(s["gelu_done"], 1)

            def first():
                ac.wait_ge(s["f_zeroed"], 1)
                copy_x(0, 0, bank[6], "xf_turned", "fm_ready")
                for k in range(6):
                    copy_proj(0, 0, k)
                for tile in range(2):
                    copy_q(0, 0, tile)

            def item(it, j, more):
                def ahead(step, *a):
                    if more:
                        step(it, j + 1, *a)

                exps(it, j, 0)
                ahead(copy_x, bank[6], "xf_turned", "fm_ready")
                exps(it, j, 1)
                exps(it, j, 2)
                ahead(copy_proj, 0)
                ahead(copy_proj, 1)
                exps(it, j, 3)
                copy_o(it, j, 0)
                ahead(copy_proj, 2)
                ahead(copy_proj, 3)
                ahead(copy_proj, 4)
                copy_o(it, j, 1)
                ahead(copy_proj, 5)
                copy_x(it, j, bank[3], "h_turned", "h_out")
                ahead(copy_q, 0)
                squares(it, j)
                for k in range(3):
                    gelu(it, j, k)
                ahead(copy_q, 1)

            over_items(ac, first, item)

        @block.vector
        def _(ve):
            ve.wait_ge(s["small_loaded"], 16 * SMALL)
            ve.memset(wo_stage[:, :, :], 0.0).then_inc(s["norm_step"], 1)
            for k in range(2):
                ve.tensor_copy(m_rep[:, k, :, :], m_nat[:, k, :].unsqueeze(1).to_broadcast([D, R, D]))
            ve.wait_ge(s["norm_step"], 1)
            for r in range(R):
                ins = ve.tensor_copy(wo_stage[:, r, D * r:D * r + D], wo_nat[:, :])
            ins.then_inc(s["staged"], 1)
            ve.tensor_copy(eye_s[:, :].rearrange("p (n t) -> p n t", t=CH),
                           eyes[:, 0:CH].unsqueeze(1).to_broadcast([128, R * NCH, CH])).then_inc(s["norm_step"], 1)
            for i in (0, 2):
                ve.wait_ge(s["x_turned"], i + 1)
                ve.tensor_copy(x_fm[:, 512 * i:512 * i + 512], bank[i][:, :]).then_inc(s["fm_ready_v"], 1)
            ve.wait_ge(s["w_turned"], 2)
            ve.tensor_copy(wo_bd[:, :, :], bank[5][:, :].rearrange("p (r h) -> p r h", r=R)).then_inc(s["wo_ready"], 1)
            ve.wait_ge(s["w_turned"], 3)
            for g in range(G):
                ve.tensor_copy(w_st[:, g, 0:2, :], bank[6][:, 0:2 * D].rearrange("p (k o) -> p k o", k=2))
                ins = ve.tensor_copy(w_st[:, g, 2, :], w2_nat[:, :])
            ins.then_inc(s["st_ready0"], 1)
            for i in range(3):
                src = bank[i][:, :].rearrange("p (g t) -> p g t", g=G)
                ve.wait_ge(s["conv_first"], i + 1)
                for d in (1, 2, 3):
                    ins = ve.scalar_tensor_tensor(kvq[:, i, :, d:], src[:, :, 0:T - d], cw[:, i, 3 - d:4 - d],
                                                  kvq[:, i, :, d:], MUL, ADD)
                    if d < 3:
                        ins.then_inc(s["norm_step"], 1)
                        ve.wait_ge(s["norm_step"], 2 + 2 * i + d)
                ins.then_inc(s["conv_v"], 1)
            ve.wait_ge(s["gates_ready"], 4)
            ve.wait_ge(s["gates_ln"], 1)
            for i in range(4):
                ins = ve.tensor_scalar(sg_all[64:96, 512 * i:512 * i + 512], bank[3 + i][64:96, :],
                                       gate_bias[64:96, :], 0.0, ADD, MAX)
            ins.then_inc(s["norm_step"], 1)
            ve.wait_ge(s["norm_step"], 9)
            ve.tensor_tensor(sg_all[64:96, :], sg_all[64:96, :], sp_abs[64:96, :], ADD).then_inc(s["gates_soft"], 1)
            f_first = first_f[:, :].rearrange("p (n t) -> p n t", t=CH)[:, :, 0]

            def starts(a):
                return a[:, :].rearrange("p (n t) -> p n t", t=CH)[:, :, 0]

            ve.wait_ge(s["zeroed"], 1)
            ve.wait_ge(s["spread_f"], 2)
            ve.tensor_scalar(keep_f[:, :], bank[7][:, :], -1.0, 1.0, MUL, ADD).then_inc(s["keep_done"], 1)
            ve.tensor_scalar(eta_f[:, :], bank[0][:, :], 0.05, None, ADD).then_inc(s["keep_done"], 1)
            ve.wait_ge(s["spread_s"], 2)
            for half in range(2):
                ve.tensor_scalar(keep_s[:, 512 * half:512 * half + 512], bank[1 + half][:, :], -1.0, 1.0, MUL, ADD)
                ins = ve.tensor_scalar(eta_s[:, 512 * half:512 * half + 512], bank[3 + half][:, :], 0.05, None, ADD)
            ins.then_inc(s["keep_done"], 1)
            ve.wait_ge(s["theta_out"], 1)
            ve.tensor_copy(theta[:, :, :], bank[5][:, 0:NCH * R].rearrange("p (c r) -> p c r", r=R))
            ve.wait_ge(s["keep_done"], 3)
            ve.tensor_copy(f_first, starts(eta_f)).then_inc(s["first_done"], 1)
            ve.memset(starts(keep_s), 0.0)
            ve.memset(starts(eta_s), 0.0)
            ve.wait_ge(s["first_done"], 1)
            ve.memset(starts(eta_f), 0.0).then_inc(s["first_done"], 1)
            ve.wait_ge(s["first_done"], 2)
            ve.tensor_tensor_scan(e_cum[:, :], eta_f[:, :], first_f[:, :], 0.0, MUL, ADD).then_inc(s["scanned"], 1)
            ve.wait_ge(s["scanned"], 1)
            ve.tensor_copy(f_first, starts(keep_f)).then_inc(s["first_done"], 1)
            ve.wait_ge(s["first_done"], 3)
            ve.memset(starts(keep_f), 0.0).then_inc(s["first_done"], 1)
            ve.wait_ge(s["first_done"], 4)
            ve.tensor_tensor_scan(a_cum[:, :], keep_f[:, :], first_f[:, :], 0.0, MUL, ADD).then_inc(s["scanned"], 1)
            ve.tensor_tensor_scan(b_cum[:, :], keep_f[:, :], e_cum[:, :], 0.0, MUL, ADD).then_inc(s["scanned"], 1)
            ve.tensor_tensor_scan(p_mat[:, :], eta_s[:, :], eye_s[:, :], 0.0, MUL, ADD).then_inc(s["scanned"], 1)
            ve.wait_ge(s["scanned"], 4)
            ve.tensor_tensor_scan(m_mat[:, :], keep_s[:, :], p_mat[:, :], 0.0, MUL, ADD).then_inc(s["scanned"], 1)
            ve.wait_ge(s["scanned"], 5)
            ve.tensor_copy(w_end[:, 0, :, :], m_mat_c[:, :, :, CH - 1].rearrange("p r c -> p c r"))
            ve.tensor_copy(w_end[:, 1, :, :], p_mat_c[:, :, :, CH - 1].rearrange("p r c -> p c r")
                           ).then_inc(s["mats_ready"], 1)
            ve.wait_ge(s["mats_ready"], 1)
            expand(ve.tensor_copy, 0)
            expand(ve.tensor_copy, 1).then_inc(s["exp_v"], 1)
            N0 = 9
            NS = 5
            with ve.Fori(0, NCH) as c:
                def step(k):
                    ve.wait_ge(s["norm_step"], c * NS + (N0 + k))

                ve.wait_ge(s["sig_ready"], c + 1)
                ve.tensor_tensor(act[:, :, :], gt(bank[0]), sig[:, :, :], MUL).then_inc(s["act_ready"], 1)
                ve.wait_ge(s["pred_ready"], c + 1)
                ve.tensor_tensor(err[:, :, :], gt(bank[1]), kvq_c[:, 1, :, c, :], SUB).then_inc(s["err_ready"], 1)
                ve.wait_ge(s["qk_ready"], c + 1)
                ve.tensor_tensor(q1[:, :, :], qk_bank, m_mat_c[:, :, c, :], MUL).then_inc(s["q1_ready"], 1)
                ve.wait_ge(s["da_ready"], c + 1)
                ve.wait_ge(s["sp_ready"], c + 1)
                ve.tensor_tensor(dz[:, :, :], gt(bank[0]), dact[:, :, :], MUL).then_inc(s["dz_ready"], 1)
                ve.wait_ge(s["tok_ready"], c + 1)
                ve.tensor_copy(tokm[:, :, :, :], tok_bank.rearrange("p k (r o) -> p k r o", r=R)
                               ).then_inc(s["tokm_ready"], 1)
                ve.wait_ge(s["sq_ready"], c + 1)
                ve.tensor_reduce(n4[:, :], sqm[:, :, :, :].rearrange("p k r o -> p (k r) o"), AX.X, ADD
                                 ).then_inc(s["norm_step"], 1)
                step(1)
                ve.tensor_tensor(n2[:, :], n4[:, 0:2 * R], n4[:, 2 * R:4 * R], MUL).then_inc(s["norm_step"], 1)
                step(2)
                ve.tensor_tensor(n1[:, :], n2[:, 0:R], n2[:, R:2 * R], ADD).then_inc(s["norm_step"], 1)
                step(3)
                ve.tensor_scalar(n1[:, :], n1[:, :], (EPS / 0.2) ** 2, None, MAX).then_inc(s["norm_ready"], 1)
                ve.wait_ge(s["inv_norm"], c + 1)
                ve.scalar_tensor_tensor(coef[:, :], inv[:, :], 0.2, theta[:, c, :], MIN, MUL
                                        ).then_inc(s["norm_step"], 1)
                step(4)
                for i in range(2):
                    ins = ve.tensor_tensor(gc[:, i, :, :], tokm[:, 1 + i, :, :],
                                           coef[:, :].unsqueeze(2).to_broadcast([128, R, D]), MUL)
                ins.then_inc(s["gc_ready"], 1)
                ve.wait_ge(s["gc_ready"], c + 1)
                for j in range(2):
                    for i in range(2):
                        ins = ve.tensor_tensor(u[:, j, i, :, :], gc[:, i, :, :],
                                               w_end[:, j, c, :].unsqueeze(2).to_broadcast([128, R, D]), MUL)
                ins.then_inc(s["u_ready"], 1)
                ve.wait_ge(s["sigy_ready"], c + 1)
                for g in range(G):
                    ins = ve.tensor_tensor(hy[:, g, :], y_bank[g], sig_y[:, g, :], MUL)
                ins.then_inc(s["h_ready"], 1)
                ve.wait_ge(s["h_ready"], c + 1)
                for r in (0, 1):
                    rows = slice(D * r, D * r + D)
                    ins = ve.tensor_copy(hc[rows, r, :, :], hy[rows, :, :])
                ins.then_inc(s["hc_v"], 1)
                ve.wait_ge(s["d_ready"], c + 1)
                for g in range(G):
                    ins = ve.scalar_tensor_tensor(t_st[:, g, :, :], s_st[:, g, :, :], b_cum_c[:, g, c, CH - 1:CH],
                                                  d_bank[g][:, 0, :, :], MUL, ADD)
                ins.then_inc(s["norm_step"], 1)
                step(5)
                for g in range(G):
                    ve.scalar_tensor_tensor(w_st[:, g, :, :], w_st[:, g, :, :], a_cum_c[:, g, c, CH - 1:CH],
                                            t_st[:, g, :, :], MUL, ADD)
                    ins = ve.scalar_tensor_tensor(s_st[:, g, :, :], s_st[:, g, :, :], e_cum_c[:, g, c, CH - 1:CH],
                                                  d_bank[g][:, 1, :, :], MUL, ADD)
                ins.then_inc(s["st_ready"], 1)
                ve.wait_ge(s["ah_ready"], c + 1)
                ve.tensor_tensor(am[:, :, :], qk_bank, m_mat_c[:, :, c, :], MUL).then_inc(s["am_ready"], 1)
                ve.wait_ge(s["st_ready"], c + 1)
                ve.wait_ge(s["y2_ready"], c + 1)
                for r in (0, 1):
                    ins = expand(ve.tensor_copy, r)
                ins.then_inc(s["exp_v"], 1)
            x_grp = x_tok[:, :, :].rearrange("p (g r h) d -> p g h r d", g=G, h=2)
            x1_grp = x1[:, :, :].rearrange("p (g r h) d -> p g h r d", g=G, h=2)
            shape = [128, R, H]
            MS = 6
            for m in range(4):
                g, half = m // 2, m % 2

                def done(ins, k):
                    ins.then_inc(s["mix_step"], 1)
                    ve.wait_ge(s["mix_step"], MS * m + k)

                ve.wait_ge(s["mix_gate"], m + 1)
                done(ve.tensor_tensor(gate[:, :, :], bank[2 + m % 2][:, :].rearrange("p (r h) -> p r h", r=R),
                                      gb[:, :].unsqueeze(1).to_broadcast(shape), ADD), 1)
                done(ve.tensor_tensor(gate[:, :, :], gate[:, :, :],
                                      norm_g[:, :].unsqueeze(1).to_broadcast(shape), MUL), 2)
                ve.wait_ge(s["osq_ready"], m + 1)
                done(ve.tensor_reduce(st4[:, 0, :], o_sq[:, :, :], AX.X, ADD), 3)
                ve.tensor_scalar(st4[:, 1, :], st4[:, 0, :], 1.0 / H, EPS, MUL, ADD).then_inc(s["ms_ready"], 1)
                ve.wait_ge(s["ms_inv"], 2 * m + 1)
                ve.tensor_tensor(gate[:, :, :], gate[:, :, :], st4[:, 1, :].unsqueeze(2).to_broadcast(shape), MUL
                                 ).then_inc(s["gate_step"], 1)
                ve.wait_ge(s["gate_step"], 2 * m + 1)
                ve.tensor_tensor(o_n[:, :, :], bank[m % 2][:, :].rearrange("p (r h) -> p r h", r=R),
                                 gate[:, :, :], MUL).then_inc(s["on_ready"], 1)
                ve.wait_ge(s["on_ready"], m + 1)
                done(ve.tensor_tensor(o_n[:, :, :], o_n[:, :, :], x_grp[:, g, half, :, :], ADD), 4)
                done(ve.tensor_reduce(st4[:, 2, :], o_n[:, :, :], AX.X, ADD), 5)
                ve.tensor_scalar(st4[:, 2, :], st4[:, 2, :], 1.0 / H, None, MUL).then_inc(s["gate_step"], 1)
                ve.wait_ge(s["gate_step"], 2 * m + 2)
                ve.tensor_tensor(o_n[:, :, :], o_n[:, :, :], st4[:, 2, :].unsqueeze(2).to_broadcast(shape), SUB
                                 ).then_inc(s["cen_ready"], 1)
                ve.wait_ge(s["csq_ready"], m + 1)
                done(ve.tensor_reduce(st4[:, 3, :], o_sq[:, :, :], AX.X, ADD), 6)
                ve.tensor_scalar(st4[:, 3, :], st4[:, 3, :], 1.0 / H, LN_EPS, MUL, ADD).then_inc(s["ms_ready"], 1)
                ve.wait_ge(s["ms_inv"], 2 * m + 2)
                ve.tensor_tensor(x1_grp[:, g, half, :, :], o_n[:, :, :],
                                 st4[:, 3, :].unsqueeze(2).to_broadcast(shape), MUL).then_inc(s["x1_ready"], 1)
            ve.wait_ge(s["f_loaded"], FL)
            ve.tensor_copy(masks[:, :, :], masks_in[:, :, :])
            ve.tensor_copy(ident_bf[:, :], ident[:, :]).then_inc(s["masks_ready"], 1)
            ve.wait_ge(s["bias_out"], 1)
            for l in range(LAYERS):
                ve.tensor_scalar(w1[:, l, :], w1[:, l, :], ln_gb[:, 0, l:l + 1], None, MUL)
                for k in range(3):
                    for part in range(2):
                        c = 3 * part + k
                        ins = ve.tensor_tensor(b1[0:HB[k], l, c:c + 1], b1[0:HB[k], l, c:c + 1],
                                               bank[7][0:HB[k], 6 * l + c:6 * l + c + 1], ADD)
            ins.then_inc(s["w1_ready"], 1)

            def norms(it, j, tile):
                ve.wait_ge(s["proj_out"], count(6, it, j, 3 * tile + 2))
                ve.tensor_reduce(ss[tile][:, :], qk_sq[:, :, :, :].rearrange("p k h d -> p (k h) d"), AX.X, ADD
                                 ).then_inc(s["ss_step"], 1)
                ve.wait_ge(s["ss_step"], count(2, it, j, tile + 1))
                ve.tensor_scalar(ss[tile][:, :], ss[tile][:, :], 1e-24, None, MAX).then_inc(s["ss_ready"], 1)

            def cos_part(it, j, tile):
                l, sl = spot(j)
                ve.wait_ge(s["proj_out"], count(6, it, j, 3 * tile + 2))
                ve.tensor_tensor(rot[tile][:, :, :, :], qk[tile][:, :, :, :],
                                 cos_t[:, l, tile, :, :].unsqueeze(2).to_broadcast([128, 2, HEADS, DH]), MUL
                                 ).then_inc(s["c_ready"], 1)

            def sum_parts(it, j, tile):
                ve.wait_ge(s["s_ready"], count(4, it, j, 2 * tile + 2))
                ve.wait_ge(s["c_ready"], count(2, it, j, tile + 1))
                ve.tensor_tensor(rot[tile][:, :, :, :], rot[tile][:, :, :, :], rot_s[tile][:, :, :, :], ADD
                                 ).then_inc(s["sum_ready"], 1)

            def scale_qk(it, j, tile):
                ve.wait_ge(s["rn_ready"], count(2, it, j, tile + 1))
                ve.wait_ge(s["sum_ready"], count(2, it, j, tile + 1))
                flat = rot[tile][:, :, :, :].rearrange("p k h d -> p (k h) d")
                ve.tensor_tensor(flat, flat, rn[tile][:, :].unsqueeze(2).to_broadcast([128, 2 * HEADS, DH]), MUL
                                 ).then_inc(s["rot_ready"], 1)

            def copy_k(it, j, tile):
                l, sl = spot(j)
                ve.wait_ge(s["qk_turned"], count(4, it, j, 2 * tile + 2))
                ve.tensor_copy(kt[sl][:, :, 128 * tile:128 * tile + 128], heads4(6)).then_inc(s["kt_out"], 1)

            def maxima(it, j, w):
                ve.wait_ge(s["score_ready"], count(4, it, j, w + 1))
                ve.tensor_reduce(nmx[w % 2][:, :], heads4(w % 2), AX.X, MAX, negate=True).then_inc(s["max_ready"], 1)

            def inv_sums(it, j, w):
                ve.wait_ge(s["exp_done"], count(4, it, j, w + 1))
                ve.reciprocal(rr[w % 2][:, :], rs[w % 2][:, :]).then_inc(s["rr_ready"], 1)

            def copy_p(it, j, w):
                ve.wait_ge(s["p_turned"], count(4, it, j, w + 1))
                ve.tensor_copy(pt[:, :, :], heads4(2)).then_inc(s["p_out"], 1)

            def add_attention(it, j, tile):
                l, sl = spot(j)
                ve.wait_ge(s["wo_done"], count(2, it, j, tile + 1))
                ve.tensor_tensor(xs[sl][:, tile, :], xs[sl][:, tile, :], bank[7][:, 128 * tile:128 * tile + 128], ADD
                                 ).then_inc(s["xa_ready"], 1)

            def centre(it, j):
                l, sl = spot(j)
                ve.wait_ge(s["mu_done"], count(1, it, j, 1))
                ve.tensor_tensor(h_cen[:, :], fm[sl][:, 0:T], bank[7][:, 0:T], SUB).then_inc(s["hc_ready"], 1)

            def variances(it, j):
                ve.wait_ge(s["var_done"], count(1, it, j, 1))
                ve.tensor_scalar(h_var[:, :], bank[3][:, 0:2], LN_EPS, None, ADD).then_inc(s["var_ready"], 1)

            def diagonal(it, j):
                ve.wait_ge(s["hinv_ready"], count(1, it, j, 1))
                for tile in range(2):
                    ins = ve.tensor_scalar(diag[:, tile, :], ident[:, :], h_inv[:, tile:tile + 1], None, MUL)
                ins.then_inc(s["diag_ready"], 1)

            def scale_h(it, j):
                ve.wait_ge(s["bc_done"], count(1, it, j, 1))
                ve.tensor_tensor(h_n[:, :], h_cen[:, :], bank[3][:, 0:T], MUL).then_inc(s["hn_ready"], 1)

            def gated(it, j, k):
                l, sl = spot(j)
                ve.wait_ge(s["gelu_done"], count(3, it, j, k + 1))
                ve.scalar_tensor_tensor(hh[0:HB[k], k, :], bank[k % 2][0:HB[k], T:2 * T], b1[0:HB[k], l, k:k + 1],
                                        gl[0:HB[k], k, :], ADD, MUL).then_inc(s["hh_ready"], 1)

            def finish(it, j):
                l, sl = spot(j)
                both = bank[7][:, 0:T].rearrange("p (t d) -> p t d", t=2)
                ve.wait_ge(s["w2_done"], count(1, it, j, 1))
                dst = xs[sl] if l == 0 else yb[sl]
                ve.tensor_tensor(dst[:, :, :], xs[sl][:, :, :], both, ADD).then_inc(s["x_ready"], 1)

            FIN = 5

            def last_norm(it, j):
                l, sl = spot(j)
                nth = 0

                def done(ins):
                    nonlocal nth
                    nth += 1
                    ins.then_inc(s["fin_step"], 1)
                    ve.wait_ge(s["fin_step"], it * (2 * FIN) + (FIN * sl + nth))

                ve.wait_ge(s["x_ready"], count(1, it, j, 2))
                done(ve.tensor_tensor(yb[sl][:, :, :], yb[sl][:, :, :], x1_tiles[:, it * 2 + sl, :, :], ADD))
                done(ve.tensor_reduce(y_sum[:, :], yb[sl][:, :, :], AX.X, ADD))
                done(ve.scalar_tensor_tensor(yb[sl][:, :, :], y_sum[:, :].unsqueeze(2).to_broadcast([128, 2, H]),
                                             -1.0 / H, yb[sl][:, :, :], MUL, ADD))
                done(ve.tensor_tensor(y_sq[:, :, :], yb[sl][:, :, :], yb[sl][:, :, :], MUL))
                done(ve.tensor_reduce(y_var[:, :], y_sq[:, :, :], AX.X, ADD))
                assert nth == FIN
                ve.tensor_scalar(y_var[:, :], y_var[:, :], 1.0 / H, LN_EPS, MUL, ADD).then_inc(s["yvar_ready"], 1)

            def last_scale(it, j):
                l, sl = spot(j)
                ve.wait_ge(s["yinv_ready"], it * 2 + (sl + 1))
                for tile in range(2):
                    ins = ve.tensor_scalar(y_tiles[:, it * 2 + sl, tile, :], yb[sl][:, tile, :],
                                           y_inv[:, tile:tile + 1], None, MUL)
                ins.then_inc(s["y_ready"], 1)

            def first():
                ve.wait_ge(s["tabs_ready"], 1)
                for tile in range(2):
                    cos_part(0, 0, tile)
                    norms(0, 0, tile)
                    sum_parts(0, 0, tile)
                    scale_qk(0, 0, tile)
                for tile in range(2):
                    copy_k(0, 0, tile)

            def item(it, j, more):
                def ahead(step, *a):
                    if more:
                        step(it, j + 1, *a)

                l, sl = spot(j)
                maxima(it, j, 0)
                maxima(it, j, 1)
                inv_sums(it, j, 0)
                maxima(it, j, 2)
                copy_p(it, j, 0)
                inv_sums(it, j, 1)
                copy_p(it, j, 1)
                inv_sums(it, j, 2)
                maxima(it, j, 3)
                ahead(cos_part, 0)
                copy_p(it, j, 2)
                inv_sums(it, j, 3)
                ahead(norms, 0)
                add_attention(it, j, 0)
                ahead(sum_parts, 0)
                copy_p(it, j, 3)
                ahead(cos_part, 1)
                ahead(norms, 1)
                ahead(scale_qk, 0)
                add_attention(it, j, 1)
                centre(it, j)
                ahead(sum_parts, 1)
                ahead(copy_k, 0)
                variances(it, j)
                diagonal(it, j)
                scale_h(it, j)
                gated(it, j, 0)
                ahead(scale_qk, 1)
                gated(it, j, 1)
                gated(it, j, 2)
                finish(it, j)
                ahead(copy_k, 1)
                if l == 1:
                    last_norm(it, j)
                    last_scale(it, j)

            over_items(ve, first, item)


def constants():
    ident = np.eye(128, dtype=np.float32)
    eyes = np.concatenate([np.tile(np.eye(CH, dtype=np.float32), (2, 1)),
                           np.repeat(np.eye(R, dtype=np.float32), D, axis=0)], 1)
    sel = np.zeros((96, 257), np.float32)
    sel[0:32, 0:128] = 0.1 / D
    sel[32:64, 128:256] = 0.9 / D
    sel[64:96, 256] = -0.1 / D
    half = np.arange(0, DH, 2, dtype=np.float32)
    inv_freq = (np.float32(1.0) / np.float32(10000.0) ** (half / np.float32(DH))).astype(np.float32)
    pos = np.arange(T, dtype=np.float32)
    freqs = np.tile(pos[:, None] * inv_freq[None, :], (1, 2))
    base = (half + np.float32(0.4 * DH)) / np.float32(1.4 * DH)
    power = (pos - T // 2) / np.float32(WIN // 2)
    scale = np.tile(base[None, :] ** power[:, None], (1, 2)).astype(np.float32)
    cos, sin = np.cos(freqs), np.sin(freqs)
    sign = np.where(np.arange(DH) < DH // 2, -1.0, 1.0).astype(np.float32)
    cs = np.stack([cos * scale * 8.0, cos / scale], 1)
    sn = np.stack([sin * scale * 8.0, sin / scale], 1) * sign
    tabs = np.stack([cs, sn], 1).reshape(2, 128, 2, 2, DH).transpose(1, 0, 2, 3, 4)
    i = np.arange(WIN)[:, None]
    j = np.arange(WIN)[None, :]
    low = np.float32(-1e30)
    causal = np.where(j <= i, 0, low)
    band = np.where(j >= i, 0, low)
    none = np.full((WIN, WIN), low)
    masks = np.stack([np.tile(np.concatenate(m, 1), (2, 1)) for m in
                      ((causal, none), (band, causal), (causal, band))], 1)
    return {"c_ident": ident, "c_eyes": eyes, "c_sel": sel, "c_tabs": np.ascontiguousarray(tabs, np.float32),
            "c_masks": np.ascontiguousarray(masks, np.float32)}


_INS = {"hidden": "L0_attn_hidden"}
for _n in "Wk Wv Wq Wo ckw ckb cvw cvb cqw cqb mW1 mW2 aW ab eW eb tW tb norm_g gW gb".split():
    _INS[_n] = "L0_attn_" + _n
for _n in "wqkv q_scale k_scale wo ln_g ln_b w1 b1 w2 b2".split():
    _INS["f_" + _n] = "L0_ffn_" + _n


def kernel(**inputs):
    import concourse.bacc as bacc
    from concourse.bass_utils import run_bass_kernel_spmd as run

    nc = bacc.Bacc("TRN2", target_bir_lowering=False, num_devices=1)
    arrays, args = {}, {}
    given = {n: np.ascontiguousarray(inputs[full]) for n, full in _INS.items()}
    given.update(constants())
    for name, a in given.items():
        arrays[f"in_{name}"] = a
        args[name] = nc.dram_tensor(f"in_{name}", a.shape, mybir.dt.from_np(a.dtype), kind="ExternalInput").ap()
    out = nc.dram_tensor("out_x", (B, T, H), mybir.dt.float32, kind="ExternalOutput").ap()
    build(nc, args, out)
    return run(nc, [arrays], core_ids=[0]).results[0]["out_x"]
```

```python
import numpy as np
from contextlib import ExitStack

import concourse.bass as bass
from concourse import mybir

B, T, H = 8, 256, 128
D, CH = 32, 64
NCH = T // CH
G, R = 2, 4
HEADS, DH, WIN = 8, 64, 64
INNER = HEADS * DH
HID = int(H * 4 * 2 / 3)
LAYERS = 2
PAIRS = HEADS // 2
NWIN = T // WIN
EPS = 1e-6
LN_EPS = 1e-5
NT = B * T // 128
HB = [128, 128, HID - 256]
PHASES = 2


def build(nc, t, out):
    f32, bf16 = mybir.dt.float32, mybir.dt.bfloat16
    ALU, ACT, AX = mybir.AluOpType, mybir.ActivationFunctionType, mybir.AxisListType
    MUL, ADD, SUB, MAX, MIN, POW = ALU.mult, ALU.add, ALU.subtract, ALU.max, ALU.min, ALU.pow

    with ExitStack() as ctx:
        def sb(name, shape, dt=f32):
            return ctx.enter_context(nc.sbuf_tensor(name, shape, dt))

        def sem(name):
            return ctx.enter_context(nc.semaphore(name))

        bank = [ctx.enter_context(nc.psum_tensor(f"bank{i}", [128, 512], f32)) for i in range(8)]

        ident = sb("ident", [128, 128])
        sel = sb("sel", [96, 257])
        eyes = sb("eyes", [128, CH + R])
        w_nat = sb("w_nat", [96, H])
        g_nat = sb("g_nat", [96, H])
        gw_nat = sb("gw_nat", [H, H])
        wo_nat = sb("wo_nat", [H, D])
        m_nat = sb("m_nat", [D, 2, D])
        m_rep = sb("m_rep", [D, 2, R, D])
        w2_nat = sb("w2_nat", [128, D])
        wo_stage = sb("wo_stage", [H, R, 128])
        cw = sb("cw", [128, 3, 4])
        cb = sb("cb", [128, 3])
        gate_bias = sb("gate_bias", [96, 1])
        norm_g = sb("norm_g", [128, H])
        gb = sb("gb", [128, H])
        w_t = sb("w_t", [128, 320])
        wo_bd = sb("wo_bd", [128, R, H])

        x_tok = sb("x_tok", [128, NT, H])
        x_fm = sb("x_fm", [H, B * T])
        kvq = sb("kvq", [128, 3, G, T])
        kvq_c = kvq[:, :, :, :].rearrange("p i g (c t) -> p i g c t", t=CH)
        w_end = sb("w_end", [128, 2, NCH, R])
        theta = sb("theta", [128, NCH, R])
        q_a = sb("q_a", [128, G, T])
        q_b = sb("q_b", [128, G, T])
        kc = sb("kc", [128, G, CH])
        qc = sb("qc", [128, R, G, CH])
        sig = sb("sig", [128, G, CH])
        act = sb("act", [128, G, CH])
        t_sp = sb("t_sp", [128, G, CH])
        dact = sb("dact", [128, G, CH])
        err = sb("err", [128, G, CH])
        dz = sb("dz", [128, G, CH])
        tokm = sb("tokm", [128, 4, R, D])
        sqm = sb("sqm", [128, 4, R, D])
        n4 = sb("n4", [128, 4 * R])
        n2 = sb("n2", [128, 2 * R])
        n1 = sb("n1", [128, R])
        inv = sb("inv", [128, R])
        minus_half = sb("minus_half", [128, 2 * HEADS])
        coef = sb("coef", [128, R])
        gc = sb("gc", [128, 2, R, D])
        u = sb("u", [128, 2, 2, R, D])
        q1 = sb("q1", [128, R, CH])
        sig_y = sb("sig_y", [128, G, CH])
        hy = sb("hy", [128, G, CH])
        hc = sb("hc", [128, R, G, CH])
        h_a = sb("h_a", [128, G, CH])
        h_b = sb("h_b", [128, G, CH])
        am = sb("am", [128, R, CH])
        w_st = sb("w_st", [128, G, 3, D])
        s_st = sb("s_st", [128, G, 3, D])
        t_st = sb("t_st", [128, G, 3, D])
        bd = sb("bd", [128, G, 5, 128])
        ret = sb("ret", [128, G, T])
        ret_c = ret[:, :, :].rearrange("p g (c t) -> p g c t", t=CH)
        gate = sb("gate", [128, R, H])
        o_sq = sb("o_sq", [128, R, H])
        o_n = sb("o_n", [128, R, H])
        st4 = sb("st4", [128, 4, R])
        x1 = sb("x1", [128, NT, H])

        ident_bf = sb("ident_bf", [128, 128], bf16)
        masks_in = sb("masks_in", [128, 3, 2 * WIN])
        masks = sb("masks", [128, 3, 2 * WIN], bf16)
        tabs = sb("tabs", [128, 2, 2, 2, DH])
        scales = sb("scales", [128, LAYERS, 2, DH])
        cos_t = sb("cos_t", [128, LAYERS, 2, 2, DH])
        sin_t = sb("sin_t", [128, LAYERS, 2, 2, DH])
        wqkv = sb("wqkv", [H, LAYERS, 3 * INNER])
        wo_sb = sb("wo_sb", [128, LAYERS, 4, H])
        w1 = sb("w1", [H, LAYERS, 2 * HID])
        w2 = sb("w2", [128, LAYERS, 3, H])
        ln_gb = sb("ln_gb", [H, 2, LAYERS])
        b1 = sb("b1", [128, LAYERS, 6])
        mean_h = sb("mean_h", [128, 128])
        ones = sb("ones", [128, 128])
        xs = [sb(f"xs{i}", [128, 2, H]) for i in range(2)]
        xa = [sb(f"xa{i}", [128, 2, H]) for i in range(2)]
        fm = sb("fm", [H, T + 2])
        h_fm = sb("h_fm", [H, T + 2])
        qb = [sb(f"qb{i}", [128, NWIN, 4, 2, WIN]) for i in range(2)]
        kt = [sb(f"kt{i}", [128, 4, T]) for i in range(2)]
        ss = [sb(f"ss{i}", [128, 2 * HEADS]) for i in range(2)]
        rn = [sb(f"rn{i}", [128, 2 * HEADS]) for i in range(2)]
        h_var = sb("h_var", [128, 2])
        h_inv = sb("h_inv", [128, 2])
        diag = sb("diag", [128, 2, 128])
        nmx = [sb(f"nmx{i}", [128, 4]) for i in range(2)]
        rs = [sb(f"rs{i}", [128, 4]) for i in range(2)]
        rr = [sb(f"rr{i}", [128, 4]) for i in range(2)]
        hh = sb("hh", [128, 3, T])
        yb = [sb(f"yb{i}", [128, 2, H]) for i in range(2)]
        y_sum = sb("y_sum", [128, 2])
        y_sq = sb("y_sq", [128, 2, H])
        y_var = sb("y_var", [128, 2])
        y_inv = sb("y_inv", [128, 2])
        y_all = x_tok

        mixer_scratch = ExitStack()

        def sb_mixer(name, shape):
            return mixer_scratch.enter_context(nc.sbuf_tensor(name, shape, f32))

        sg_all = sb_mixer("sg_all", [96, B * T])
        sp_abs = sb_mixer("sp_abs", [96, B * T])
        keep_f = sb_mixer("keep_f", [128, G * T])
        eta_f = sb_mixer("eta_f", [128, G * T])
        first_f = sb_mixer("first_f", [128, G * T])
        a_cum = sb_mixer("a_cum", [128, G * T])
        b_cum = sb_mixer("b_cum", [128, G * T])
        e_cum = sb_mixer("e_cum", [128, G * T])
        keep_s = sb_mixer("keep_s", [128, R * T])
        eta_s = sb_mixer("eta_s", [128, R * T])
        eye_s = sb_mixer("eye_s", [128, R * T])
        p_mat = sb_mixer("p_mat", [128, R * T])
        m_mat = sb_mixer("m_mat", [128, R * T])
        mixer_scratch.close()
        vt = [sb(f"vt{i}", [128, 3, INNER]) for i in range(2)]
        qk = [sb(f"qk{i}", [128, 2, HEADS, DH]) for i in range(2)]
        qk_sq = sb("qk_sq", [128, 2, HEADS, DH])
        rot = [sb(f"rot{i}", [128, 2, HEADS, DH]) for i in range(2)]
        rot_s = [sb(f"rot_s{i}", [128, 2, HEADS, DH]) for i in range(2)]
        pm = [sb(f"pm{i}", [128, 4, 2 * WIN]) for i in range(2)]
        pt = sb("pt", [128, 4, 2 * WIN])
        ot = sb("ot", [128, 4, 128])
        h_cen = sb("h_cen", [H, T])
        h_sq = sb("h_sq", [H, T])
        h_n = sb("h_n", [H, T])
        gl = sb("gl", [128, 3, T])

        def per_chunk(a, g_dim):
            return a[:, :].rearrange("p (g c t) -> p g c t", g=g_dim, t=CH)

        a_cum_c, b_cum_c, e_cum_c = (per_chunk(a, G) for a in (a_cum, b_cum, e_cum))
        m_mat_c, p_mat_c = per_chunk(m_mat, R), per_chunk(p_mat, R)
        q_a_c = q_a[:, :, :].rearrange("p g (c t) -> p g c t", t=CH)
        q_b_c = q_b[:, :, :].rearrange("p g (c t) -> p g c t", t=CH)
        def gt(b, g=None):
            v = b[:, 0:G * CH].rearrange("p (g t) -> p g t", g=G)
            return v if g is None else v[:, g, :]

        tok_bank = bank[2][:, :].rearrange("p (k x) -> p k x", k=4)
        qk_bank = bank[3][:, 0:R * CH].rearrange("p (r t) -> p r t", r=R)
        d_bank = [bank[4 + g][:, 0:6 * D].rearrange("p (j k o) -> p j k o", j=2, k=3) for g in range(G)]
        y_bank = [bank[6 + g][:, 0:CH] for g in range(G)]

        names = """x_loaded0 x_loaded1 x_loaded2 x_loaded3 small_loaded stored
          zeroed staged x_turned w_turned fm_ready_v fm_ready_s wt_ready wo_ready st_ready0 projected
          conv_first conv_v gates_ready gates_done gates_out spread_f spread_s theta_out
          keep_done theta_done scanned first_done mats_ready qab_ready gates_abs gates_exp gates_ln gates_soft
          kc_free kc_ready qc_ready z_ready qk_ready pred_ready da_ready tok_ready y1_ready d_ready ah_ready
          y2_ready ret_done sig_ready act_ready sp_step sp_ready q1_ready err_ready dz_ready tokm_ready
          sq_ready norm_step norm_ready inv_norm ms_ready ms_inv gc_ready u_ready sigy_ready h_ready hc_v hc_s hab_ready am_ready st_step
          st_ready exp_v exp_s
          mix_out mix_gate gate_step gate_ready osq_ready mix_step on_ready cen_ready csq_ready x1_ready
          f_loaded tabs_ready masks_ready w1_ready bias_out f_zeroed ones_ready
          xs_loaded xf_turned fm_ready proj proj_out ss_step rn_ready ss_ready sum_ready c_ready s_ready rot_ready
          qk_turned qt_out kt_out score_ready max_ready exp_done rr_ready pn_ready p_turned p_out pv_done o_out
          wo_done xa_ready h_turned h_out mu_done hc_ready hsq_ready var_done diag_ready hn_ready
          w1_done gelu_done hh_ready w2_done x_ready fin_step yvar_ready yinv_ready y_ready var_ready hinv_ready bc_done
        """.split()
        s = {n: sem(n) for n in names}

        block = ctx.enter_context(nc.Block())

        def expand(copy, r):
            rows = slice(D * r, D * r + D)
            copy(bd[rows, :, 0:3, rows], w_st[rows, :, :, :])
            return copy(bd[rows, :, 3:5, rows], s_st[rows, :, 0:2, :])

        SMALL = 0
        FL = 0
        y_tiles = y_all[:, :, :].rearrange("p (b h) d -> p b h d", h=2)
        x1_tiles = x1[:, :, :].rearrange("p (b h) d -> p b h d", h=2)

        def count(per, n, k):
            it, c = n
            return it * (2 * per) + (c * per + k)

        def spot(n):
            return n[1] // B, n[1] % 2

        def batch(n):
            return n[0] * 2 + n[1] % B

        def over_items(eng, project_first, step):
            project_first()
            step((0, 0), (0, 1), None)
            with eng.Fori(0, B // 2 - 1) as it:
                step((it, 1), (it, 2), (it, 0))
                step((it, 2), (it, 3), (it, 1))
            step((0, B - 1), (0, B), (0, B - 2))
            step((0, B), (0, B + 1), (0, B - 1))
            with eng.Fori(0, B // 2 - 1) as it:
                step((it, B + 1), (it, B + 2), (it, B))
                step((it, B + 2), (it, B + 3), (it, B + 1))
            step((0, 2 * B - 1), None, (0, 2 * B - 2))
            step(None, None, (0, 2 * B - 1))

        def heads4(b):
            return bank[b][:, :].rearrange("p (k x) -> p k x", k=4)


        @block.sync
        def _(sp):
            nonlocal SMALL, FL
            for i in range(4):
                sp.dma_start(x_tok[:, 4 * i:4 * i + 4, :],
                             t["hidden"][2 * i:2 * i + 2].rearrange("b (h p) d -> p (b h) d", p=128)
                             ).then_inc(s[f"x_loaded{i}"], 16)
                if i == 0:
                    sp.dma_start(ident[:, :], t["c_ident"]).then_inc(s["small_loaded"], 16)
                    SMALL += 1
            loads = [(w_nat[0:32, :], t["Wk"]), (w_nat[32:64, :], t["Wv"]), (w_nat[64:96, :], t["Wq"]),
                     (g_nat[0:32, :], t["aW"]), (g_nat[32:64, :], t["eW"]), (g_nat[64:96, :], t["tW"]),
                     (gw_nat[:, :], t["gW"]), (wo_nat[:, :], t["Wo"]),
                     (m_nat[:, 0, :], t["mW1"]), (m_nat[:, 1, :], t["mW2"]),
                     (sel[:, :], t["c_sel"]), (eyes[:, :], t["c_eyes"]),
                     (gate_bias[0:32, :], t["ab"].unsqueeze(1)), (gate_bias[32:64, :], t["eb"].unsqueeze(1)),
                     (gate_bias[64:96, :], t["tb"].unsqueeze(1)),
                     (norm_g[:, :], t["norm_g"].partition_broadcast(128)),
                     (gb[:, :], t["gb"].partition_broadcast(128))]
            for r in range(R):
                rows = slice(D * r, D * r + D)
                loads.append((w2_nat[rows, :], t["mW2"]))
                for i, (w, b) in enumerate((("ckw", "ckb"), ("cvw", "cvb"), ("cqw", "cqb"))):
                    loads.append((cw[rows, i, :], t[w]))
                    loads.append((cb[rows, i:i + 1], t[b].unsqueeze(1)))
            for dst, src in loads:
                sp.dma_start(dst, src).then_inc(s["small_loaded"], 16)
            SMALL += len(loads)
            f_loads = []
            for l in range(LAYERS):
                f_loads += [(wqkv[:, l, :], t["f_wqkv"][l]),
                            (wo_sb[:, l, :, :], t["f_wo"][l].rearrange("(k p) n -> p k n", p=128)),
                            (w1[:, l, :], t["f_w1"][l]),
                            (w2[:, l, 0:2, :], t["f_w2"][l, 0:256].rearrange("(k p) n -> p k n", p=128)),
                            (w2[0:HB[2], l, 2, :], t["f_w2"][l, 256:HID]),
                            (w2[HB[2]:HB[2] + 1, l, 2, :], t["f_b2"][l:l + 1]),
                            (scales[:, l, 0, :], t["f_q_scale"][l].partition_broadcast(128)),
                            (scales[:, l, 1, :], t["f_k_scale"][l].partition_broadcast(128)),
                            (ln_gb[:, 0, l:l + 1], t["f_ln_g"][l].unsqueeze(1)),
                            (ln_gb[:, 1, l:l + 1], t["f_ln_b"][l].unsqueeze(1))]
                for part in range(2):
                    for k in range(3):
                        at = HID * part + 128 * k
                        f_loads.append((b1[0:HB[k], l, 3 * part + k:3 * part + k + 1],
                                        t["f_b1"][l, at:at + HB[k]].unsqueeze(1)))
            f_loads += [(tabs[:, :, :, :, :], t["c_tabs"]), (masks_in[:, :, :], t["c_masks"])]
            for dst, src in f_loads:
                sp.dma_start(dst, src).then_inc(s["f_loaded"], 16)
            FL = 16 * len(f_loads)
            if PHASES == 2:
                with sp.Fori(0, PAIRS) as it:
                    for sl in range(2):
                        sp.wait_ge(s["y_ready"], it * 2 + (sl + 1))
                        sp.dma_start(out[it * 2 + sl, :, :].rearrange("(h p) d -> p h d", p=128),
                                     y_tiles[:, it * 2 + sl, :, :]).then_inc(s["stored"], 16)
                sp.wait_ge(s["stored"], 16 * B)
            if PHASES == 1:
                for i in range(4):
                    sp.wait_ge(s["x1_ready"], 4)
                    sp.dma_start(out[2 * i:2 * i + 2].rearrange("b (h p) d -> p (b h) d", p=128),
                                 x1[:, 4 * i:4 * i + 4, :]).then_inc(s["stored"], 16)
                sp.wait_ge(s["stored"], 64)

        @block.gpsimd
        def _(po):
            po.memset(bd[:, :, :, :], 0.0)
            po.memset(hc[:, :, :, :], 0.0)
            po.memset(s_st[:, :, :, :], 0.0)
            po.memset(minus_half[:, :], -0.5)
            po.memset(first_f[:, :], 0.0).then_inc(s["zeroed"], 1)
            po.wait_ge(s["scanned"], 3)
            po.wait_ge(s["conv_v"], 3)
            po.tensor_tensor(q_a[:, :, :], kvq[:, 2, :, :], a_cum[:, :].rearrange("p (g t) -> p g t", g=G), MUL)
            po.tensor_tensor(q_b[:, :, :], kvq[:, 2, :, :], b_cum[:, :].rearrange("p (g t) -> p g t", g=G), MUL
                             ).then_inc(s["qab_ready"], 1)
            with po.Fori(0, NCH) as c:
                po.wait_ge(s["mats_ready"], 1)
                po.wait_ge(s["kc_free"], c + 1)
                po.tensor_copy(kc[:, :, :], kvq_c[:, 0, :, c, :]).then_inc(s["kc_ready"], 1)
                for g in range(G):
                    ins = po.tensor_tensor(qc[:, :, g, :],
                                           kvq_c[:, 2, g, c, :].unsqueeze(1).to_broadcast([128, R, CH]),
                                           eyes[:, CH:CH + R].unsqueeze(2).to_broadcast([128, R, CH]), MUL)
                ins.then_inc(s["qc_ready"], 1)
                po.wait_ge(s["act_ready"], c + 1)
                po.tensor_tensor(t_sp[:, :, :], act[:, :, :], sig[:, :, :], MUL).then_inc(s["sp_step"], 1)
                po.wait_ge(s["sp_step"], 2 * c + 1)
                po.tensor_tensor(t_sp[:, :, :], act[:, :, :], t_sp[:, :, :], SUB).then_inc(s["sp_step"], 1)
                po.wait_ge(s["sp_step"], 2 * c + 2)
                po.tensor_tensor(dact[:, :, :], t_sp[:, :, :], sig[:, :, :], ADD).then_inc(s["sp_ready"], 1)
                po.wait_ge(s["norm_ready"], c + 1)
                po.tensor_tensor(inv[:, :], n1[:, :], minus_half[:, 0:R], POW).then_inc(s["inv_norm"], 1)
                po.wait_ge(s["h_ready"], c + 1)
                po.tensor_tensor(h_a[:, :, :], hy[:, :, :], a_cum_c[:, :, c, :], MUL)
                po.tensor_tensor(h_b[:, :, :], hy[:, :, :], b_cum_c[:, :, c, :], MUL).then_inc(s["hab_ready"], 1)
            for k in range(8):
                po.wait_ge(s["ms_ready"], k + 1)
                po.tensor_tensor(st4[:, 1 + 2 * (k % 2), :], st4[:, 1 + 2 * (k % 2), :], minus_half[:, 0:R], POW
                                 ).then_inc(s["ms_inv"], 1)

            for i in range(2):
                po.memset(qb[i][:, :, :, :, :], 0.0)
            po.memset(fm[:, :], 0.0)
            po.memset(h_fm[:, :], 0.0)
            po.memset(mean_h[:, :], 1.0 / H)
            po.memset(ones[:, :], 1.0)
            po.memset(hh[:, :, :], 1.0).then_inc(s["f_zeroed"], 1)
            po.wait_ge(s["f_loaded"], FL)
            q = DH // 2
            for l in range(LAYERS):
                for k in range(2):
                    shape = [128, 2, DH]
                    po.tensor_tensor(cos_t[:, l, :, k, :], tabs[:, :, 0, k, :],
                                     scales[:, l, k, :].unsqueeze(1).to_broadcast(shape), MUL)
                    for to, fro in ((slice(0, q), slice(q, DH)), (slice(q, DH), slice(0, q))):
                        ins = po.tensor_tensor(sin_t[:, l, :, k, to], tabs[:, :, 1, k, to],
                                               scales[:, l, k, fro].unsqueeze(1).to_broadcast([128, 2, q]), MUL)
            ins.then_inc(s["tabs_ready"], 1)
            po.sem_inc(s["x_ready"], 1)

            def load_xs(n):
                l, sl = spot(n)
                po.wait_ge(s["x1_ready"], 4)
                if l:
                    po.wait_ge(s["x_ready"], count(1, n, 2 - B))
                if n[1] >= 2:
                    po.wait_ge(s["xa_ready"], count(2, n, -2))
                src = x1_tiles if l == 0 else y_tiles
                po.tensor_copy(xs[sl][:, :, :], src[:, batch(n), :, :]).then_inc(s["xs_loaded"], 1)

            def sin_part(n, tile, kind):
                l, sl = spot(n)
                po.wait_ge(s["proj_out"], count(6, n, 3 * tile + kind + 1))
                if kind == 0 and n[1]:
                    po.wait_ge(s["rot_ready"], count(2, n, tile - 1))
                for to, fro in ((slice(0, q), slice(q, DH)), (slice(q, DH), slice(0, q))):
                    ins = po.tensor_tensor(rot_s[tile][:, kind, :, to], qk[tile][:, kind, :, fro],
                                           sin_t[:, l, tile, kind, to].unsqueeze(1).to_broadcast([128, HEADS, q]), MUL)
                ins.then_inc(s["s_ready"], 1)

            def inv_norms(n, tile):
                po.wait_ge(s["ss_ready"], count(2, n, tile + 1))
                po.tensor_tensor(rn[tile][:, :], ss[tile][:, :], minus_half[:, :], POW).then_inc(s["rn_ready"], 1)

            def inv_std(n):
                po.wait_ge(s["var_ready"], count(1, n, 1))
                po.tensor_tensor(h_inv[:, :], h_var[:, :], minus_half[:, 0:2], POW).then_inc(s["hinv_ready"], 1)

            def normalise(n, w):
                po.wait_ge(s["rr_ready"], count(4, n, w + 1))
                po.tensor_tensor(pm[w % 2][:, :, :], pm[w % 2][:, :, :],
                                 rr[w % 2][:, :].unsqueeze(2).to_broadcast([128, 4, 2 * WIN]), MUL
                                 ).then_inc(s["pn_ready"], 1)

            def last_inv(n):
                po.wait_ge(s["yvar_ready"], count(1, n, 1 - B))
                po.tensor_tensor(y_inv[:, :], y_var[:, :], minus_half[:, 0:2], POW).then_inc(s["yinv_ready"], 1)

            def project_first():
                load_xs((0, 0))
                sin_part((0, 0), 0, 0)
                sin_part((0, 0), 0, 1)
                inv_norms((0, 0), 0)
                sin_part((0, 0), 1, 0)
                sin_part((0, 0), 1, 1)
                inv_norms((0, 0), 1)

            def step(a, p, f):
                if p:
                    load_xs(p)
                if a:
                    normalise(a, 0)
                if f:
                    inv_std(f)
                if a:
                    normalise(a, 1)
                if p:
                    sin_part(p, 0, 0)
                    sin_part(p, 0, 1)
                if a:
                    normalise(a, 2)
                if p:
                    inv_norms(p, 0)
                if a:
                    normalise(a, 3)
                if p:
                    sin_part(p, 1, 0)
                    sin_part(p, 1, 1)
                    inv_norms(p, 1)
                if f and spot(f)[0] == 1:
                    last_inv(f)

            over_items(po, project_first, step)

        @block.tensor
        def _(pe):
            for i in range(4):
                pe.wait_ge(s[f"x_loaded{i}"], 16)
                if i == 0:
                    pe.wait_ge(s["small_loaded"], 16 * SMALL)
                for j in range(4):
                    ins = pe.transpose(bank[i][:, 128 * j:128 * j + 128], x_tok[:, 4 * i + j, :], ident[:, :])
                ins.then_inc(s["x_turned"], 1)
            pe.transpose(bank[4][:, 0:96], w_nat[:, :], ident[0:96, 0:96])
            pe.transpose(bank[4][:, 96:192], g_nat[:, :], ident[0:96, 0:96])
            pe.transpose(bank[4][:, 192:320], gw_nat[:, :], ident[:, :]).then_inc(s["w_turned"], 1)
            pe.wait_ge(s["staged"], 1)
            for r in range(R):
                ins = pe.transpose(bank[5][:, 128 * r:128 * r + 128], wo_stage[:, r, :], ident[:, :])
            ins.then_inc(s["w_turned"], 1)
            for k in range(2):
                ins = pe.transpose(bank[6][:, D * k:D * k + D], m_rep[:, k, :, :], ident[0:D, 0:D])
            ins.then_inc(s["w_turned"], 1)
            pe.wait_ge(s["wt_ready"], 1)
            pe.wait_ge(s["fm_ready_v"], 2)
            pe.wait_ge(s["fm_ready_s"], 2)
            for i in range(3):
                for g in range(G):
                    for r in range(R):
                        b = R * g + r
                        ins = pe.matmul(bank[i][D * r:D * r + D, T * g:T * g + T], w_t[:, D * i:D * i + D],
                                        x_fm[:, T * b:T * b + T], start=True, stop=True)
                ins.then_inc(s["projected"], 1)
            pe.wait_ge(s["wo_ready"], 1)
            pe.wait_ge(s["st_ready0"], 1)
            for i in range(4):
                pe.matmul(bank[3 + i][0:96, :], w_t[:, 96:192], x_fm[:, 512 * i:512 * i + 512],
                          start=True, stop=True).then_inc(s["gates_out"], 1)
            pe.wait_ge(s["gates_ready"], 4)
            pe.wait_ge(s["gates_soft"], 1)
            pe.wait_ge(s["conv_v"], 3)
            for i, col in ((7, 0), (0, 128)):
                for g in range(G):
                    for r in range(R):
                        b = R * g + r
                        ins = pe.matmul(bank[i][D * r:D * r + D, T * g:T * g + T], sel[:, col:col + D],
                                        sg_all[:, T * b:T * b + T], start=True, stop=True)
                ins.then_inc(s["spread_f"], 1)
            for i, col in ((1, 0), (3, 128)):
                for half in range(2):
                    for g in range(G):
                        at = T * R * g + 512 * half
                        ins = pe.matmul(bank[i + half][CH * g:CH * g + CH, :], sel[:, col:col + CH],
                                        sg_all[:, at:at + 512], start=True, stop=True)
                ins.then_inc(s["spread_s"], 1)
            for g in range(G):
                for r in range(R):
                    for c in range(NCH):
                        at = T * (R * g + r) + CH * c
                        ins = pe.matmul(bank[5][CH * g:CH * g + CH, R * c + r:R * c + r + 1],
                                        sg_all[:, at:at + CH], sel[:, 256:257], start=True, stop=True)
            ins.then_inc(s["theta_out"], 1)
            pe.wait_ge(s["mats_ready"], 1)
            pe.wait_ge(s["qab_ready"], 1)
            pe.sem_inc(s["kc_free"], 1)
            with pe.Fori(0, NCH) as c:
                pe.wait_ge(s["kc_ready"], c + 1)
                pe.wait_ge(s["exp_v"], c + 1)
                pe.wait_ge(s["exp_s"], c + 1)
                for g in range(G):
                    ins = pe.matmul(gt(bank[0], g), bd[:, g, 0, :], kc[:, g, :], start=True, stop=True)
                ins.then_inc(s["z_ready"], 1)
                pe.wait_ge(s["qc_ready"], c + 1)
                for g in range(G):
                    ins = pe.matmul(qk_bank[CH * g:CH * g + CH, :, :], kc[:, g, :], qc[:, :, g, :],
                                    start=True, stop=True)
                ins.then_inc(s["qk_ready"], 1)
                pe.wait_ge(s["act_ready"], c + 1)
                for g in range(G):
                    ins = pe.matmul(gt(bank[1], g), bd[:, g, 1, :], act[:, g, :], start=True, stop=True)
                ins.then_inc(s["pred_ready"], 1)
                pe.transpose(tok_bank[:, 3, :], kc[:, :, :], ident[:, :])
                pe.transpose(tok_bank[:, 0, :], act[:, :, :], ident[:, :])
                pe.wait_ge(s["err_ready"], c + 1)
                for g in range(G):
                    ins = pe.matmul(gt(bank[0], g), bd[:, g, 2, :], err[:, g, :], start=True, stop=True)
                ins.then_inc(s["da_ready"], 1)
                pe.transpose(tok_bank[:, 2, :], err[:, :, :], ident[:, :])
                pe.wait_ge(s["dz_ready"], c + 1)
                pe.transpose(tok_bank[:, 1, :], dz[:, :, :], ident[:, :]).then_inc(s["tok_ready"], 1)
                pe.wait_ge(s["ret_done"], c + 1)
                pe.wait_ge(s["gc_ready"], c + 1)
                pe.wait_ge(s["q1_ready"], c + 1)
                for g in range(G):
                    pe.matmul(y_bank[g], bd[:, g, 0, :], q_a_c[:, g, c, :], start=True, stop=False)
                    pe.matmul(y_bank[g], bd[:, g, 3, :], q_b_c[:, g, c, :], start=False, stop=True)
                for r in range(R):
                    for g in range(G):
                        rows, cols = slice(CH * g, CH * g + CH), slice(D * r, D * r + D)
                        ins = pe.matmul(y_bank[g][cols, :], gc[rows, 0, r, :], q1[rows, r, :],
                                        start=False, stop=True, skip_group_check=True)
                ins.then_inc(s["y1_ready"], 1)
                pe.wait_ge(s["u_ready"], c + 1)
                pe.sem_inc(s["kc_free"], 1)
                for r in range(R):
                    for g in range(G):
                        rows, cols = slice(CH * g, CH * g + CH), slice(D * r, D * r + D)
                        pe.matmul(d_bank[g][cols, :, 0, :], tokm[rows, 3, r, :], u[rows, :, 0, r, :],
                                  start=True, stop=True)
                        pe.matmul(d_bank[g][cols, :, 1, :], tokm[rows, 0, r, :], u[rows, :, 1, r, :],
                                  start=True, stop=True)
                        for j in range(2):
                            ins = pe.matmul(d_bank[g][cols, j, 2, :], u[rows, j, 1, r, :], tokm[rows, 0, r, :],
                                            start=True, stop=True)
                ins.then_inc(s["d_ready"], 1)
                pe.wait_ge(s["hc_v"], c + 1)
                pe.wait_ge(s["hc_s"], c + 1)
                for g in range(G):
                    ins = pe.matmul(qk_bank[CH * g:CH * g + CH, :, :], act[:, g, :], hc[:, :, g, :],
                                    start=True, stop=True)
                ins.then_inc(s["ah_ready"], 1)
                pe.wait_ge(s["hab_ready"], c + 1)
                pe.wait_ge(s["am_ready"], c + 1)
                for g in range(G):
                    pe.matmul(y_bank[g], bd[:, g, 1, :], h_a[:, g, :], start=True, stop=False)
                    pe.matmul(y_bank[g], bd[:, g, 4, :], h_b[:, g, :], start=False, stop=True)
                for r in range(R):
                    for g in range(G):
                        rows, cols = slice(CH * g, CH * g + CH), slice(D * r, D * r + D)
                        ins = pe.matmul(y_bank[g][cols, :], gc[rows, 1, r, :], am[rows, r, :],
                                        start=False, stop=True, skip_group_check=True)
                ins.then_inc(s["y2_ready"], 1)
            pe.wait_ge(s["ret_done"], NCH + 1)
            for m in range(4):
                g, half = m // 2, m % 2
                if m >= 2:
                    pe.wait_ge(s["on_ready"], m - 1)
                pe.matmul(bank[m % 2][:, :], ret[:, g, 128 * half:128 * half + 128], wo_bd[:, :, :],
                          start=True, stop=True).then_inc(s["mix_out"], 1)
                for r in range(R):
                    at = T * (R * g + r) + 128 * half
                    ins = pe.matmul(bank[2 + m % 2][:, 128 * r:128 * r + 128], x_fm[:, at:at + 128],
                                    w_t[:, 192:320], start=True, stop=True)
                ins.then_inc(s["mix_gate"], 1)

            pe.wait_ge(s["f_loaded"], FL)
            for l in range(LAYERS):
                for part in range(2):
                    for k in range(3):
                        at_w = HID * part + 128 * k
                        col = 6 * l + 3 * part + k
                        ins = pe.matmul(bank[7][0:HB[k], col:col + 1], w1[:, l, at_w:at_w + HB[k]],
                                        ln_gb[:, 1, l:l + 1], start=True, stop=True)
            ins.then_inc(s["bias_out"], 1)

            def turn_x(n):
                l, sl = spot(n)
                pe.wait_ge(s["xs_loaded"], count(1, n, 1))
                if n[1]:
                    pe.wait_ge(s["kt_out"], count(2, n, 0))
                for tile in range(2):
                    ins = pe.transpose(bank[6][:, 128 * tile:128 * tile + 128], xs[sl][:, tile, :], ident[:, :])
                ins.then_inc(s["xf_turned"], 1)

            def project(n, k):
                l, sl = spot(n)
                if k == 0:
                    pe.wait_ge(s["fm_ready"], count(1, n, 1))
                if n[1] or k:
                    pe.wait_ge(s["proj_out"], count(6, n, k))
                tile, kind = k // 3, k % 3
                pe.matmul(bank[4][:, :], fm[:, 128 * tile:128 * tile + 128],
                          wqkv[:, l, INNER * kind:INNER * kind + INNER], start=True, stop=True).then_inc(s["proj"], 1)

            def turn_qk(n, i):
                tile, kind = i // 2, i % 2
                pe.wait_ge(s["rot_ready"], count(2, n, tile + 1))
                if i:
                    pe.wait_ge(s["qt_out" if i % 2 else "kt_out"], count(2, n, (i + 1) // 2))
                for h in range(4):
                    ins = pe.transpose(bank[6][:, 128 * h:128 * h + 128], rot[tile][:, kind, 2 * h:2 * h + 2, :],
                                       ident[:, :])
                ins.then_inc(s["qk_turned"], 1)

            def scores(n, w):
                l, sl = spot(n)
                if w % 2 == 0:
                    pe.wait_ge(s["qt_out"], count(2, n, w // 2 + 1))
                    pe.wait_ge(s["kt_out"], count(2, n, w // 2 + 1))
                if n[1] or w >= 2:
                    pe.wait_ge(s["exp_done"], count(4, n, w - 1))
                b = w % 2
                kind = (0, 1, 2, 1)[w]
                pe.matmul(heads4(b), ident_bf[:, :], masks[:, kind, :].unsqueeze(1).to_broadcast([128, 4, 2 * WIN]),
                          start=True, stop=False)
                for h in range(4):
                    q_blocks = qb[sl][:, w, h, :, :]
                    if w == 2:
                        for c, key in ((0, 2 * WIN), (WIN, WIN)):
                            ins = pe.matmul(heads4(b)[:, h, c:c + WIN], q_blocks, kt[sl][:, h, key:key + WIN],
                                            start=False, stop=(h == 3 and c > 0))
                    else:
                        key = 0 if w < 2 else 2 * WIN
                        ins = pe.matmul(heads4(b)[:, h, :], q_blocks, kt[sl][:, h, key:key + 2 * WIN],
                                        start=False, stop=(h == 3))
                ins.then_inc(s["score_ready"], 1)

            def turn_p(n, w):
                if n[1] or w:
                    pe.wait_ge(s["p_out"], count(4, n, w))
                pe.wait_ge(s["pn_ready"], count(4, n, w + 1))
                for h in range(4):
                    ins = pe.transpose(heads4(2)[:, h, :], pm[w % 2][:, h, :], ident[:, :])
                ins.then_inc(s["p_turned"], 1)

            def weigh_v(n, w):
                l, sl = spot(n)
                src = (0, 0, 2, 1)[w]
                pe.wait_ge(s["p_out"], count(4, n, w + 1))
                if w == 2 or (n[1] and w == 0):
                    pe.wait_ge(s["xa_ready"], count(2, n, w // 2))
                for h in range(4):
                    for e in range(2):
                        c = 128 * h + WIN * (w % 2)
                        ins = pe.matmul(bank[3][DH * e:DH * e + DH, c:c + WIN],
                                        vt[sl][:, src, DH * (2 * h + e):DH * (2 * h + e) + DH],
                                        pt[:, h, WIN * e:WIN * e + WIN], start=True, stop=True)
                if w % 2:
                    ins.then_inc(s["pv_done"], 1)

            def project_o(n, tile):
                l, sl = spot(n)
                pe.wait_ge(s["o_out"], count(2, n, tile + 1))
                for h in range(4):
                    ins = pe.matmul(bank[3][:, 128 * tile:128 * tile + 128], ot[:, h, :], wo_sb[:, l, h, :],
                                    start=(h == 0), stop=(h == 3))
                ins.then_inc(s["wo_done"], 1)

            def turn_h(n):
                l, sl = spot(n)
                pe.wait_ge(s["xa_ready"], count(2, n, 2))
                for tile in range(2):
                    ins = pe.transpose(bank[7][:, 128 * tile:128 * tile + 128], xa[sl][:, tile, :], ident[:, :])
                ins.then_inc(s["h_turned"], 1)

            def mean(n):
                l, sl = spot(n)
                pe.wait_ge(s["h_out"], count(1, n, 1))
                pe.wait_ge(s["x_ready"], count(1, n, 1))
                pe.matmul(bank[5][:, 0:T], mean_h[:, :], h_fm[:, 0:T], start=True, stop=True
                          ).then_inc(s["mu_done"], 1)

            def variance(n):
                pe.wait_ge(s["hsq_ready"], count(1, n, 1))
                for tile in range(2):
                    ins = pe.matmul(bank[7][:, tile:tile + 1], h_sq[:, 128 * tile:128 * tile + 128], mean_h[:, 0:1],
                                    start=True, stop=True)
                ins.then_inc(s["var_done"], 1)

            def spread_inv(n):
                pe.wait_ge(s["diag_ready"], count(1, n, 1))
                for tile in range(2):
                    ins = pe.matmul(bank[5][:, 128 * tile:128 * tile + 128], ones[:, :], diag[:, tile, :],
                                    start=True, stop=True)
                ins.then_inc(s["bc_done"], 1)

            def ffn_up(n, k):
                l, sl = spot(n)
                if k == 0:
                    pe.wait_ge(s["hn_ready"], count(1, n, 1))
                if k == 2:
                    pe.wait_ge(s["hh_ready"], count(3, n, 1))
                for part, c in ((1, 0), (0, T)):
                    at_w = HID * part + 128 * k
                    ins = pe.matmul(bank[(7, 5, 7)[k]][0:HB[k], c:c + T], w1[:, l, at_w:at_w + HB[k]], h_n[:, :],
                                    start=True, stop=True)
                ins.then_inc(s["w1_done"], 1)

            def ffn_down(n):
                l, sl = spot(n)
                pe.wait_ge(s["hh_ready"], count(3, n, 3))
                for tile in range(2):
                    for k in range(3):
                        rows = HB[k] + (k == 2)
                        ins = pe.matmul(bank[5][:, 128 * tile:128 * tile + 128],
                                        hh[0:rows, k, 128 * tile:128 * tile + 128], w2[0:rows, l, k, :],
                                        start=(k == 0), stop=(k == 2))
                ins.then_inc(s["w2_done"], 1)

            def project_first():
                pe.wait_ge(s["f_zeroed"], 1)
                pe.wait_ge(s["masks_ready"], 1)
                turn_x((0, 0))
                project((0, 0), 0)
                project((0, 0), 1)
                project((0, 0), 2)
                project((0, 0), 3)
                project((0, 0), 4)
                turn_qk((0, 0), 0)
                turn_qk((0, 0), 1)
                turn_qk((0, 0), 2)
                project((0, 0), 5)
                pe.wait_ge(s["w1_ready"], 1)

            def step(a, p, f):
                if f:
                    turn_h(f)
                if a:
                    turn_qk(a, 3)
                    scores(a, 0)
                if f:
                    mean(f)
                if a:
                    scores(a, 1)
                if p:
                    turn_x(p)
                if a:
                    scores(a, 2)
                if p:
                    project(p, 0)
                if a:
                    turn_p(a, 0)
                if f:
                    variance(f)
                if a:
                    scores(a, 3)
                if p:
                    project(p, 1)
                if a:
                    weigh_v(a, 0)
                    turn_p(a, 1)
                if f:
                    spread_inv(f)
                if p:
                    project(p, 2)
                if a:
                    weigh_v(a, 1)
                if f:
                    ffn_up(f, 0)
                if p:
                    project(p, 3)
                if f:
                    ffn_up(f, 1)
                if a:
                    turn_p(a, 2)
                if p:
                    project(p, 4)
                if a:
                    project_o(a, 0)
                if p:
                    turn_qk(p, 0)
                if a:
                    weigh_v(a, 2)
                    turn_p(a, 3)
                if f:
                    ffn_up(f, 2)
                if p:
                    turn_qk(p, 1)
                if a:
                    weigh_v(a, 3)
                if f:
                    ffn_down(f)
                if a:
                    project_o(a, 1)
                if p:
                    turn_qk(p, 2)
                    project(p, 5)

            over_items(pe, project_first, step)

        @block.scalar
        def _(ac):
            for i in (1, 3):
                ac.wait_ge(s["x_turned"], i + 1)
                ac.activation(x_fm[:, 512 * i:512 * i + 512], bank[i][:, :], ACT.Copy).then_inc(s["fm_ready_s"], 1)
            ac.wait_ge(s["w_turned"], 1)
            ac.activation(w_t[:, :], bank[4][:, 0:320], ACT.Copy).then_inc(s["wt_ready"], 1)
            for i in range(3):
                ac.wait_ge(s["projected"], i + 1)
                ac.activation(kvq[:, i, :, :], bank[i][:, :].rearrange("p (g t) -> p g t", g=G), ACT.Identity,
                              bias=cb[:, i:i + 1], scale=cw[:, i, 3:4]).then_inc(s["conv_first"], 1)
            for i in range(4):
                cols = slice(512 * i, 512 * i + 512)
                ac.wait_ge(s["gates_out"], i + 1)
                ac.activation(sg_all[0:64, cols], bank[3 + i][0:64, :], ACT.Sigmoid, bias=gate_bias[0:64, :]
                              ).then_inc(s["gates_ready"], 1)
            for i in range(4):
                cols = slice(512 * i, 512 * i + 512)
                ins = ac.activation(sp_abs[64:96, cols], bank[3 + i][64:96, :], ACT.Abs, bias=gate_bias[64:96, :])
            ins.then_inc(s["gates_abs"], 1)
            ac.wait_ge(s["gates_abs"], 1)
            ac.activation(sp_abs[64:96, :], sp_abs[64:96, :], ACT.Exp, scale=-1.0).then_inc(s["gates_exp"], 1)
            ac.wait_ge(s["gates_exp"], 1)
            ac.activation(sp_abs[64:96, :], sp_abs[64:96, :], ACT.Ln, bias=1.0).then_inc(s["gates_ln"], 1)
            ac.sem_inc(s["ret_done"], 1)
            ac.wait_ge(s["zeroed"], 1)
            ac.wait_ge(s["st_ready0"], 1)
            expand(ac.copy, 2)
            expand(ac.copy, 3).then_inc(s["exp_s"], 1)
            with ac.Fori(0, NCH) as c:
                ac.wait_ge(s["z_ready"], c + 1)
                ac.activation(sig[:, :, :], gt(bank[0]), ACT.Sigmoid).then_inc(s["sig_ready"], 1)
                ac.wait_ge(s["tokm_ready"], c + 1)
                ac.activation(sqm[:, :, :, :], tokm[:, :, :, :], ACT.Square).then_inc(s["sq_ready"], 1)
                ac.wait_ge(s["y1_ready"], c + 1)
                for g in range(G):
                    ins = ac.activation(sig_y[:, g, :], y_bank[g], ACT.Sigmoid)
                ins.then_inc(s["sigy_ready"], 1)
                ac.wait_ge(s["h_ready"], c + 1)
                for r in (2, 3):
                    rows = slice(D * r, D * r + D)
                    ins = ac.activation(hc[rows, r, :, :], hy[rows, :, :], ACT.Copy)
                ins.then_inc(s["hc_s"], 1)
                ac.wait_ge(s["y2_ready"], c + 1)
                for g in range(G):
                    ins = ac.activation(ret_c[:, g, c, :], y_bank[g], ACT.Copy)
                ins.then_inc(s["ret_done"], 1)
                ac.wait_ge(s["st_ready"], c + 1)
                expand(ac.copy, 2)
                expand(ac.copy, 3).then_inc(s["exp_s"], 1)
            for m in range(4):
                ac.wait_ge(s["mix_out"], m + 1)
                if m >= 1:
                    ac.wait_ge(s["x1_ready"], m)
                ac.activation(o_sq[:, :, :], bank[m % 2][:, :].rearrange("p (r h) -> p r h", r=R), ACT.Square
                              ).then_inc(s["osq_ready"], 1)
                ac.wait_ge(s["cen_ready"], m + 1)
                ac.activation(o_sq[:, :, :], o_n[:, :, :], ACT.Square).then_inc(s["csq_ready"], 1)


            def shifted(dst, src):
                ac.activation(dst[0:64, 0:T], src[0:64, 0:T], ACT.Copy)
                return ac.activation(dst[64:128, 1:T + 1], src[64:128, 0:T], ACT.Copy)

            def copy_x(n):
                ac.wait_ge(s["xf_turned"], count(1, n, 1))
                shifted(fm, bank[6]).then_inc(s["fm_ready"], 1)

            def copy_h(n):
                ac.wait_ge(s["h_turned"], count(1, n, 1))
                shifted(h_fm, bank[7]).then_inc(s["h_out"], 1)

            def copy_proj(n, k):
                l, sl = spot(n)
                tile, kind = k // 3, k % 3
                ac.wait_ge(s["proj"], count(6, n, k + 1))
                src = bank[4]
                if kind < 2:
                    if kind == 0 and n[1]:
                        ac.wait_ge(s["rot_ready"], count(2, n, tile - 1))
                    if not (n[1] == 0 and tile == 0):
                        ac.wait_ge(s["ss_ready"], count(2, n, tile))
                    view = src[:, :].rearrange("p (h d) -> p h d", d=DH)
                    ac.activation(qk_sq[:, kind, :, :], view, ACT.Square)
                    ac.activation(qk[tile][:, kind, :, :], view, ACT.Copy).then_inc(s["proj_out"], 1)
                else:
                    ac.activation(vt[sl][:, tile, :], src[:, :], ACT.Copy)
                    rows = slice(64, 128) if tile == 0 else slice(0, 64)
                    ac.activation(vt[sl][rows, 2, :], src[rows, :], ACT.Copy).then_inc(s["proj_out"], 1)

            def exps(n, w):
                ac.wait_ge(s["max_ready"], count(4, n, w + 1))
                if n[1] or w >= 2:
                    ac.wait_ge(s["p_turned"], count(4, n, w - 1))
                for h in range(4):
                    ins = ac.activation(pm[w % 2][:, h, :], heads4(w % 2)[:, h, :], ACT.Exp, bias=nmx[w % 2][:, h:h + 1],
                                        accum_out=rs[w % 2][:, h:h + 1])
                ins.then_inc(s["exp_done"], 1)

            def copy_o(n, tile):
                ac.wait_ge(s["pv_done"], count(2, n, tile + 1))
                ac.activation(ot[:, :, :], heads4(3), ACT.Copy).then_inc(s["o_out"], 1)

            def copy_q(n, tile):
                l, sl = spot(n)
                ac.wait_ge(s["qk_turned"], count(4, n, 2 * tile + 1))
                for e in range(2):
                    rows = slice(DH * e, DH * e + DH)
                    ins = ac.activation(qb[sl][rows, 2 * tile:2 * tile + 2, :, e, :].rearrange("p w h q -> p h w q"),
                                        bank[6][rows, :].rearrange("p (h w q) -> p h w q", h=4, w=2), ACT.Copy)
                ins.then_inc(s["qt_out"], 1)

            def squares(n):
                ac.wait_ge(s["hc_ready"], count(1, n, 1))
                ac.activation(h_sq[:, :], h_cen[:, :], ACT.Square).then_inc(s["hsq_ready"], 1)

            def gelu(n, k):
                l, sl = spot(n)
                ac.wait_ge(s["w1_done"], count(3, n, k + 1))
                ac.activation(gl[0:HB[k], k, :], bank[(7, 5, 7)[k]][0:HB[k], 0:T], ACT.Gelu, bias=b1[0:HB[k], l, 3 + k:4 + k]
                              ).then_inc(s["gelu_done"], 1)

            def project_first():
                ac.wait_ge(s["f_zeroed"], 1)
                copy_x((0, 0))
                copy_proj((0, 0), 0)
                copy_proj((0, 0), 1)
                copy_proj((0, 0), 2)
                copy_proj((0, 0), 3)
                copy_proj((0, 0), 4)
                copy_q((0, 0), 0)
                copy_q((0, 0), 1)
                copy_proj((0, 0), 5)

            def step(a, p, f):
                if f:
                    copy_h(f)
                if a:
                    exps(a, 0)
                if p:
                    copy_x(p)
                if f:
                    squares(f)
                if a:
                    exps(a, 1)
                if p:
                    copy_proj(p, 0)
                if a:
                    exps(a, 2)
                if p:
                    copy_proj(p, 1)
                if a:
                    exps(a, 3)
                if p:
                    copy_proj(p, 2)
                if f:
                    gelu(f, 0)
                if p:
                    copy_proj(p, 3)
                if f:
                    gelu(f, 1)
                if a:
                    copy_o(a, 0)
                if p:
                    copy_proj(p, 4)
                    copy_q(p, 0)
                if f:
                    gelu(f, 2)
                if a:
                    copy_o(a, 1)
                if p:
                    copy_q(p, 1)
                    copy_proj(p, 5)

            over_items(ac, project_first, step)

        @block.vector
        def _(ve):
            ve.wait_ge(s["small_loaded"], 16 * SMALL)
            ve.memset(wo_stage[:, :, :], 0.0).then_inc(s["norm_step"], 1)
            for k in range(2):
                ve.tensor_copy(m_rep[:, k, :, :], m_nat[:, k, :].unsqueeze(1).to_broadcast([D, R, D]))
            ve.wait_ge(s["norm_step"], 1)
            for r in range(R):
                ins = ve.tensor_copy(wo_stage[:, r, D * r:D * r + D], wo_nat[:, :])
            ins.then_inc(s["staged"], 1)
            ve.tensor_copy(eye_s[:, :].rearrange("p (n t) -> p n t", t=CH),
                           eyes[:, 0:CH].unsqueeze(1).to_broadcast([128, R * NCH, CH])).then_inc(s["norm_step"], 1)
            for i in (0, 2):
                ve.wait_ge(s["x_turned"], i + 1)
                ve.tensor_copy(x_fm[:, 512 * i:512 * i + 512], bank[i][:, :]).then_inc(s["fm_ready_v"], 1)
            ve.wait_ge(s["w_turned"], 2)
            ve.tensor_copy(wo_bd[:, :, :], bank[5][:, :].rearrange("p (r h) -> p r h", r=R)).then_inc(s["wo_ready"], 1)
            ve.wait_ge(s["w_turned"], 3)
            for g in range(G):
                ve.tensor_copy(w_st[:, g, 0:2, :], bank[6][:, 0:2 * D].rearrange("p (k o) -> p k o", k=2))
                ins = ve.tensor_copy(w_st[:, g, 2, :], w2_nat[:, :])
            ins.then_inc(s["st_ready0"], 1)
            for i in range(3):
                src = bank[i][:, :].rearrange("p (g t) -> p g t", g=G)
                ve.wait_ge(s["conv_first"], i + 1)
                for d in (1, 2, 3):
                    ins = ve.scalar_tensor_tensor(kvq[:, i, :, d:], src[:, :, 0:T - d], cw[:, i, 3 - d:4 - d],
                                                  kvq[:, i, :, d:], MUL, ADD)
                    if d < 3:
                        ins.then_inc(s["norm_step"], 1)
                        ve.wait_ge(s["norm_step"], 2 + 2 * i + d)
                ins.then_inc(s["conv_v"], 1)
            ve.wait_ge(s["gates_ready"], 4)
            ve.wait_ge(s["gates_ln"], 1)
            for i in range(4):
                ins = ve.tensor_scalar(sg_all[64:96, 512 * i:512 * i + 512], bank[3 + i][64:96, :],
                                       gate_bias[64:96, :], 0.0, ADD, MAX)
            ins.then_inc(s["norm_step"], 1)
            ve.wait_ge(s["norm_step"], 9)
            ve.tensor_tensor(sg_all[64:96, :], sg_all[64:96, :], sp_abs[64:96, :], ADD).then_inc(s["gates_soft"], 1)
            f_first = first_f[:, :].rearrange("p (n t) -> p n t", t=CH)[:, :, 0]

            def starts(a):
                return a[:, :].rearrange("p (n t) -> p n t", t=CH)[:, :, 0]

            ve.wait_ge(s["zeroed"], 1)
            ve.wait_ge(s["spread_f"], 2)
            ve.tensor_scalar(keep_f[:, :], bank[7][:, :], -1.0, 1.0, MUL, ADD).then_inc(s["keep_done"], 1)
            ve.tensor_scalar(eta_f[:, :], bank[0][:, :], 0.05, None, ADD).then_inc(s["keep_done"], 1)
            ve.wait_ge(s["spread_s"], 2)
            for half in range(2):
                ve.tensor_scalar(keep_s[:, 512 * half:512 * half + 512], bank[1 + half][:, :], -1.0, 1.0, MUL, ADD)
                ins = ve.tensor_scalar(eta_s[:, 512 * half:512 * half + 512], bank[3 + half][:, :], 0.05, None, ADD)
            ins.then_inc(s["keep_done"], 1)
            ve.wait_ge(s["theta_out"], 1)
            ve.tensor_copy(theta[:, :, :], bank[5][:, 0:NCH * R].rearrange("p (c r) -> p c r", r=R))
            ve.wait_ge(s["keep_done"], 3)
            ve.tensor_copy(f_first, starts(eta_f)).then_inc(s["first_done"], 1)
            ve.memset(starts(keep_s), 0.0)
            ve.memset(starts(eta_s), 0.0)
            ve.wait_ge(s["first_done"], 1)
            ve.memset(starts(eta_f), 0.0).then_inc(s["first_done"], 1)
            ve.wait_ge(s["first_done"], 2)
            ve.tensor_tensor_scan(e_cum[:, :], eta_f[:, :], first_f[:, :], 0.0, MUL, ADD).then_inc(s["scanned"], 1)
            ve.wait_ge(s["scanned"], 1)
            ve.tensor_copy(f_first, starts(keep_f)).then_inc(s["first_done"], 1)
            ve.wait_ge(s["first_done"], 3)
            ve.memset(starts(keep_f), 0.0).then_inc(s["first_done"], 1)
            ve.wait_ge(s["first_done"], 4)
            ve.tensor_tensor_scan(a_cum[:, :], keep_f[:, :], first_f[:, :], 0.0, MUL, ADD).then_inc(s["scanned"], 1)
            ve.tensor_tensor_scan(b_cum[:, :], keep_f[:, :], e_cum[:, :], 0.0, MUL, ADD).then_inc(s["scanned"], 1)
            ve.tensor_tensor_scan(p_mat[:, :], eta_s[:, :], eye_s[:, :], 0.0, MUL, ADD).then_inc(s["scanned"], 1)
            ve.wait_ge(s["scanned"], 4)
            ve.tensor_tensor_scan(m_mat[:, :], keep_s[:, :], p_mat[:, :], 0.0, MUL, ADD).then_inc(s["scanned"], 1)
            ve.wait_ge(s["scanned"], 5)
            ve.tensor_copy(w_end[:, 0, :, :], m_mat_c[:, :, :, CH - 1].rearrange("p r c -> p c r"))
            ve.tensor_copy(w_end[:, 1, :, :], p_mat_c[:, :, :, CH - 1].rearrange("p r c -> p c r")
                           ).then_inc(s["mats_ready"], 1)
            ve.wait_ge(s["mats_ready"], 1)
            expand(ve.tensor_copy, 0)
            expand(ve.tensor_copy, 1).then_inc(s["exp_v"], 1)
            N0 = 9
            NS = 5
            with ve.Fori(0, NCH) as c:
                def step(k):
                    ve.wait_ge(s["norm_step"], c * NS + (N0 + k))

                ve.wait_ge(s["sig_ready"], c + 1)
                ve.tensor_tensor(act[:, :, :], gt(bank[0]), sig[:, :, :], MUL).then_inc(s["act_ready"], 1)
                ve.wait_ge(s["pred_ready"], c + 1)
                ve.tensor_tensor(err[:, :, :], gt(bank[1]), kvq_c[:, 1, :, c, :], SUB).then_inc(s["err_ready"], 1)
                ve.wait_ge(s["qk_ready"], c + 1)
                ve.tensor_tensor(q1[:, :, :], qk_bank, m_mat_c[:, :, c, :], MUL).then_inc(s["q1_ready"], 1)
                ve.wait_ge(s["da_ready"], c + 1)
                ve.wait_ge(s["sp_ready"], c + 1)
                ve.tensor_tensor(dz[:, :, :], gt(bank[0]), dact[:, :, :], MUL).then_inc(s["dz_ready"], 1)
                ve.wait_ge(s["tok_ready"], c + 1)
                ve.tensor_copy(tokm[:, :, :, :], tok_bank.rearrange("p k (r o) -> p k r o", r=R)
                               ).then_inc(s["tokm_ready"], 1)
                ve.wait_ge(s["sq_ready"], c + 1)
                ve.tensor_reduce(n4[:, :], sqm[:, :, :, :].rearrange("p k r o -> p (k r) o"), AX.X, ADD
                                 ).then_inc(s["norm_step"], 1)
                step(1)
                ve.tensor_tensor(n2[:, :], n4[:, 0:2 * R], n4[:, 2 * R:4 * R], MUL).then_inc(s["norm_step"], 1)
                step(2)
                ve.tensor_tensor(n1[:, :], n2[:, 0:R], n2[:, R:2 * R], ADD).then_inc(s["norm_step"], 1)
                step(3)
                ve.tensor_scalar(n1[:, :], n1[:, :], (EPS / 0.2) ** 2, None, MAX).then_inc(s["norm_ready"], 1)
                ve.wait_ge(s["inv_norm"], c + 1)
                ve.scalar_tensor_tensor(coef[:, :], inv[:, :], 0.2, theta[:, c, :], MIN, MUL
                                        ).then_inc(s["norm_step"], 1)
                step(4)
                for i in range(2):
                    ins = ve.tensor_tensor(gc[:, i, :, :], tokm[:, 1 + i, :, :],
                                           coef[:, :].unsqueeze(2).to_broadcast([128, R, D]), MUL)
                ins.then_inc(s["gc_ready"], 1)
                ve.wait_ge(s["gc_ready"], c + 1)
                for j in range(2):
                    for i in range(2):
                        ins = ve.tensor_tensor(u[:, j, i, :, :], gc[:, i, :, :],
                                               w_end[:, j, c, :].unsqueeze(2).to_broadcast([128, R, D]), MUL)
                ins.then_inc(s["u_ready"], 1)
                ve.wait_ge(s["sigy_ready"], c + 1)
                for g in range(G):
                    ins = ve.tensor_tensor(hy[:, g, :], y_bank[g], sig_y[:, g, :], MUL)
                ins.then_inc(s["h_ready"], 1)
                ve.wait_ge(s["h_ready"], c + 1)
                for r in (0, 1):
                    rows = slice(D * r, D * r + D)
                    ins = ve.tensor_copy(hc[rows, r, :, :], hy[rows, :, :])
                ins.then_inc(s["hc_v"], 1)
                ve.wait_ge(s["d_ready"], c + 1)
                for g in range(G):
                    ins = ve.scalar_tensor_tensor(t_st[:, g, :, :], s_st[:, g, :, :], b_cum_c[:, g, c, CH - 1:CH],
                                                  d_bank[g][:, 0, :, :], MUL, ADD)
                ins.then_inc(s["norm_step"], 1)
                step(5)
                for g in range(G):
                    ve.scalar_tensor_tensor(w_st[:, g, :, :], w_st[:, g, :, :], a_cum_c[:, g, c, CH - 1:CH],
                                            t_st[:, g, :, :], MUL, ADD)
                    ins = ve.scalar_tensor_tensor(s_st[:, g, :, :], s_st[:, g, :, :], e_cum_c[:, g, c, CH - 1:CH],
                                                  d_bank[g][:, 1, :, :], MUL, ADD)
                ins.then_inc(s["st_ready"], 1)
                ve.wait_ge(s["ah_ready"], c + 1)
                ve.tensor_tensor(am[:, :, :], qk_bank, m_mat_c[:, :, c, :], MUL).then_inc(s["am_ready"], 1)
                ve.wait_ge(s["st_ready"], c + 1)
                ve.wait_ge(s["y2_ready"], c + 1)
                for r in (0, 1):
                    ins = expand(ve.tensor_copy, r)
                ins.then_inc(s["exp_v"], 1)
            x_grp = x_tok[:, :, :].rearrange("p (g r h) d -> p g h r d", g=G, h=2)
            x1_grp = x1[:, :, :].rearrange("p (g r h) d -> p g h r d", g=G, h=2)
            shape = [128, R, H]
            MS = 6
            for m in range(4):
                g, half = m // 2, m % 2

                def done(ins, k):
                    ins.then_inc(s["mix_step"], 1)
                    ve.wait_ge(s["mix_step"], MS * m + k)

                ve.wait_ge(s["mix_gate"], m + 1)
                done(ve.tensor_tensor(gate[:, :, :], bank[2 + m % 2][:, :].rearrange("p (r h) -> p r h", r=R),
                                      gb[:, :].unsqueeze(1).to_broadcast(shape), ADD), 1)
                done(ve.tensor_tensor(gate[:, :, :], gate[:, :, :],
                                      norm_g[:, :].unsqueeze(1).to_broadcast(shape), MUL), 2)
                ve.wait_ge(s["osq_ready"], m + 1)
                done(ve.tensor_reduce(st4[:, 0, :], o_sq[:, :, :], AX.X, ADD), 3)
                ve.tensor_scalar(st4[:, 1, :], st4[:, 0, :], 1.0 / H, EPS, MUL, ADD).then_inc(s["ms_ready"], 1)
                ve.wait_ge(s["ms_inv"], 2 * m + 1)
                ve.tensor_tensor(gate[:, :, :], gate[:, :, :], st4[:, 1, :].unsqueeze(2).to_broadcast(shape), MUL
                                 ).then_inc(s["gate_step"], 1)
                ve.wait_ge(s["gate_step"], 2 * m + 1)
                ve.tensor_tensor(o_n[:, :, :], bank[m % 2][:, :].rearrange("p (r h) -> p r h", r=R),
                                 gate[:, :, :], MUL).then_inc(s["on_ready"], 1)
                ve.wait_ge(s["on_ready"], m + 1)
                done(ve.tensor_tensor(o_n[:, :, :], o_n[:, :, :], x_grp[:, g, half, :, :], ADD), 4)
                done(ve.tensor_reduce(st4[:, 2, :], o_n[:, :, :], AX.X, ADD), 5)
                ve.tensor_scalar(st4[:, 2, :], st4[:, 2, :], 1.0 / H, None, MUL).then_inc(s["gate_step"], 1)
                ve.wait_ge(s["gate_step"], 2 * m + 2)
                ve.tensor_tensor(o_n[:, :, :], o_n[:, :, :], st4[:, 2, :].unsqueeze(2).to_broadcast(shape), SUB
                                 ).then_inc(s["cen_ready"], 1)
                ve.wait_ge(s["csq_ready"], m + 1)
                done(ve.tensor_reduce(st4[:, 3, :], o_sq[:, :, :], AX.X, ADD), 6)
                ve.tensor_scalar(st4[:, 3, :], st4[:, 3, :], 1.0 / H, LN_EPS, MUL, ADD).then_inc(s["ms_ready"], 1)
                ve.wait_ge(s["ms_inv"], 2 * m + 2)
                ve.tensor_tensor(x1_grp[:, g, half, :, :], o_n[:, :, :],
                                 st4[:, 3, :].unsqueeze(2).to_broadcast(shape), MUL).then_inc(s["x1_ready"], 1)
            ve.wait_ge(s["f_loaded"], FL)
            ve.tensor_copy(masks[:, :, :], masks_in[:, :, :])
            ve.tensor_copy(ident_bf[:, :], ident[:, :]).then_inc(s["masks_ready"], 1)
            ve.wait_ge(s["bias_out"], 1)
            for l in range(LAYERS):
                ve.tensor_scalar(w1[:, l, :], w1[:, l, :], ln_gb[:, 0, l:l + 1], None, MUL)
                for k in range(3):
                    for part in range(2):
                        c = 3 * part + k
                        ins = ve.tensor_tensor(b1[0:HB[k], l, c:c + 1], b1[0:HB[k], l, c:c + 1],
                                               bank[7][0:HB[k], 6 * l + c:6 * l + c + 1], ADD)
            ins.then_inc(s["w1_ready"], 1)

            def norms(n, tile):
                ve.wait_ge(s["proj_out"], count(6, n, 3 * tile + 2))
                ve.tensor_reduce(ss[tile][:, :], qk_sq[:, :, :, :].rearrange("p k h d -> p (k h) d"), AX.X, ADD
                                 ).then_inc(s["ss_step"], 1)
                ve.wait_ge(s["ss_step"], count(2, n, tile + 1))
                ve.tensor_scalar(ss[tile][:, :], ss[tile][:, :], 1e-24, None, MAX).then_inc(s["ss_ready"], 1)

            def cos_part(n, tile):
                l, sl = spot(n)
                if n[1]:
                    ve.wait_ge(s["qk_turned"], count(4, n, 2 * tile - 2))
                ve.wait_ge(s["proj_out"], count(6, n, 3 * tile + 2))
                ve.tensor_tensor(rot[tile][:, :, :, :], qk[tile][:, :, :, :],
                                 cos_t[:, l, tile, :, :].unsqueeze(2).to_broadcast([128, 2, HEADS, DH]), MUL
                                 ).then_inc(s["c_ready"], 1)

            def sum_parts(n, tile):
                ve.wait_ge(s["s_ready"], count(4, n, 2 * tile + 2))
                ve.wait_ge(s["c_ready"], count(2, n, tile + 1))
                ve.tensor_tensor(rot[tile][:, :, :, :], rot[tile][:, :, :, :], rot_s[tile][:, :, :, :], ADD
                                 ).then_inc(s["sum_ready"], 1)

            def scale_qk(n, tile):
                ve.wait_ge(s["rn_ready"], count(2, n, tile + 1))
                ve.wait_ge(s["sum_ready"], count(2, n, tile + 1))
                flat = rot[tile][:, :, :, :].rearrange("p k h d -> p (k h) d")
                ve.tensor_tensor(flat, flat, rn[tile][:, :].unsqueeze(2).to_broadcast([128, 2 * HEADS, DH]), MUL
                                 ).then_inc(s["rot_ready"], 1)

            def copy_k(n, tile):
                l, sl = spot(n)
                ve.wait_ge(s["qk_turned"], count(4, n, 2 * tile + 2))
                ve.tensor_copy(kt[sl][:, :, 128 * tile:128 * tile + 128], heads4(6)).then_inc(s["kt_out"], 1)

            def maxima(n, w):
                ve.wait_ge(s["score_ready"], count(4, n, w + 1))
                ve.tensor_reduce(nmx[w % 2][:, :], heads4(w % 2), AX.X, MAX, negate=True).then_inc(s["max_ready"], 1)

            def inv_sums(n, w):
                ve.wait_ge(s["exp_done"], count(4, n, w + 1))
                ve.reciprocal(rr[w % 2][:, :], rs[w % 2][:, :]).then_inc(s["rr_ready"], 1)

            def copy_p(n, w):
                ve.wait_ge(s["p_turned"], count(4, n, w + 1))
                ve.tensor_copy(pt[:, :, :], heads4(2)).then_inc(s["p_out"], 1)

            def add_attention(n, tile):
                l, sl = spot(n)
                ve.wait_ge(s["wo_done"], count(2, n, tile + 1))
                ve.tensor_tensor(xa[sl][:, tile, :], xs[sl][:, tile, :], bank[3][:, 128 * tile:128 * tile + 128], ADD
                                 ).then_inc(s["xa_ready"], 1)

            def centre(n):
                l, sl = spot(n)
                ve.wait_ge(s["mu_done"], count(1, n, 1))
                ve.tensor_tensor(h_cen[:, :], h_fm[:, 0:T], bank[5][:, 0:T], SUB).then_inc(s["hc_ready"], 1)

            def variances(n):
                ve.wait_ge(s["var_done"], count(1, n, 1))
                ve.tensor_scalar(h_var[:, :], bank[7][:, 0:2], LN_EPS, None, ADD).then_inc(s["var_ready"], 1)

            def diagonal(n):
                ve.wait_ge(s["hinv_ready"], count(1, n, 1))
                for tile in range(2):
                    ins = ve.tensor_scalar(diag[:, tile, :], ident[:, :], h_inv[:, tile:tile + 1], None, MUL)
                ins.then_inc(s["diag_ready"], 1)

            def scale_h(n):
                ve.wait_ge(s["bc_done"], count(1, n, 1))
                ve.tensor_tensor(h_n[:, :], h_cen[:, :], bank[5][:, 0:T], MUL).then_inc(s["hn_ready"], 1)

            def gated(n, k):
                l, sl = spot(n)
                ve.wait_ge(s["gelu_done"], count(3, n, k + 1))
                ve.scalar_tensor_tensor(hh[0:HB[k], k, :], bank[(7, 5, 7)[k]][0:HB[k], T:2 * T], b1[0:HB[k], l, k:k + 1],
                                        gl[0:HB[k], k, :], ADD, MUL).then_inc(s["hh_ready"], 1)

            def finish(n):
                l, sl = spot(n)
                both = bank[5][:, 0:T].rearrange("p (t d) -> p t d", t=2)
                ve.wait_ge(s["w2_done"], count(1, n, 1))
                dst = y_tiles[:, batch(n), :, :] if l == 0 else yb[sl][:, :, :]
                ve.tensor_tensor(dst, xa[sl][:, :, :], both, ADD).then_inc(s["x_ready"], 1)

            FIN = 5

            def last_norm(n):
                l, sl = spot(n)
                nth = 0

                def done(ins):
                    nonlocal nth
                    nth += 1
                    ins.then_inc(s["fin_step"], 1)
                    ve.wait_ge(s["fin_step"], count(FIN, n, nth - B * FIN))

                ve.wait_ge(s["x_ready"], count(1, n, 2))
                done(ve.tensor_tensor(yb[sl][:, :, :], yb[sl][:, :, :], x1_tiles[:, batch(n), :, :], ADD))
                done(ve.tensor_reduce(y_sum[:, :], yb[sl][:, :, :], AX.X, ADD))
                done(ve.scalar_tensor_tensor(yb[sl][:, :, :], y_sum[:, :].unsqueeze(2).to_broadcast([128, 2, H]),
                                             -1.0 / H, yb[sl][:, :, :], MUL, ADD))
                done(ve.tensor_tensor(y_sq[:, :, :], yb[sl][:, :, :], yb[sl][:, :, :], MUL))
                done(ve.tensor_reduce(y_var[:, :], y_sq[:, :, :], AX.X, ADD))
                assert nth == FIN
                ve.tensor_scalar(y_var[:, :], y_var[:, :], 1.0 / H, LN_EPS, MUL, ADD).then_inc(s["yvar_ready"], 1)

            def last_scale(n):
                l, sl = spot(n)
                ve.wait_ge(s["yinv_ready"], count(1, n, 1 - B))
                for tile in range(2):
                    ins = ve.tensor_scalar(y_tiles[:, batch(n), tile, :], yb[sl][:, tile, :],
                                           y_inv[:, tile:tile + 1], None, MUL)
                ins.then_inc(s["y_ready"], 1)

            def project_first():
                ve.wait_ge(s["tabs_ready"], 1)
                norms((0, 0), 0)
                cos_part((0, 0), 0)
                sum_parts((0, 0), 0)
                scale_qk((0, 0), 0)
                norms((0, 0), 1)
                cos_part((0, 0), 1)
                sum_parts((0, 0), 1)
                copy_k((0, 0), 0)
                scale_qk((0, 0), 1)

            def step(a, p, f):
                if a:
                    maxima(a, 0)
                    copy_k(a, 1)
                    maxima(a, 1)
                if f:
                    centre(f)
                if a:
                    inv_sums(a, 0)
                    inv_sums(a, 1)
                    maxima(a, 2)
                if f:
                    variances(f)
                if a:
                    copy_p(a, 0)
                    maxima(a, 3)
                    inv_sums(a, 2)
                if f:
                    diagonal(f)
                if a:
                    copy_p(a, 1)
                if f:
                    scale_h(f)
                if p:
                    norms(p, 0)
                    cos_part(p, 0)
                if a:
                    inv_sums(a, 3)
                if p:
                    sum_parts(p, 0)
                if f:
                    gated(f, 0)
                if a:
                    copy_p(a, 2)
                if p:
                    scale_qk(p, 0)
                if f:
                    gated(f, 1)
                if a:
                    add_attention(a, 0)
                if p:
                    norms(p, 1)
                    cos_part(p, 1)
                if a:
                    copy_p(a, 3)
                if f:
                    gated(f, 2)
                if p:
                    sum_parts(p, 1)
                    copy_k(p, 0)
                    scale_qk(p, 1)
                if f:
                    finish(f)
                if a:
                    add_attention(a, 1)
                if f and spot(f)[0] == 1:
                    last_norm(f)
                    last_scale(f)

            over_items(ve, project_first, step)


def constants():
    ident = np.eye(128, dtype=np.float32)
    eyes = np.concatenate([np.tile(np.eye(CH, dtype=np.float32), (2, 1)),
                           np.repeat(np.eye(R, dtype=np.float32), D, axis=0)], 1)
    sel = np.zeros((96, 257), np.float32)
    sel[0:32, 0:128] = 0.1 / D
    sel[32:64, 128:256] = 0.9 / D
    sel[64:96, 256] = -0.1 / D
    half = np.arange(0, DH, 2, dtype=np.float32)
    inv_freq = (np.float32(1.0) / np.float32(10000.0) ** (half / np.float32(DH))).astype(np.float32)
    pos = np.arange(T, dtype=np.float32)
    freqs = np.tile(pos[:, None] * inv_freq[None, :], (1, 2))
    base = (half + np.float32(0.4 * DH)) / np.float32(1.4 * DH)
    power = (pos - T // 2) / np.float32(WIN // 2)
    scale = np.tile(base[None, :] ** power[:, None], (1, 2)).astype(np.float32)
    cos, sin = np.cos(freqs), np.sin(freqs)
    sign = np.where(np.arange(DH) < DH // 2, -1.0, 1.0).astype(np.float32)
    cs = np.stack([cos * scale * 8.0, cos / scale], 1)
    sn = np.stack([sin * scale * 8.0, sin / scale], 1) * sign
    tabs = np.stack([cs, sn], 1).reshape(2, 128, 2, 2, DH).transpose(1, 0, 2, 3, 4)
    i = np.arange(WIN)[:, None]
    j = np.arange(WIN)[None, :]
    low = np.float32(-1e30)
    causal = np.where(j <= i, 0, low)
    band = np.where(j >= i, 0, low)
    none = np.full((WIN, WIN), low)
    masks = np.stack([np.tile(np.concatenate(m, 1), (2, 1)) for m in
                      ((causal, none), (band, causal), (causal, band))], 1)
    return {"c_ident": ident, "c_eyes": eyes, "c_sel": sel, "c_tabs": np.ascontiguousarray(tabs, np.float32),
            "c_masks": np.ascontiguousarray(masks, np.float32)}


_INS = {"hidden": "L0_attn_hidden"}
for _n in "Wk Wv Wq Wo ckw ckb cvw cvb cqw cqb mW1 mW2 aW ab eW eb tW tb norm_g gW gb".split():
    _INS[_n] = "L0_attn_" + _n
for _n in "wqkv q_scale k_scale wo ln_g ln_b w1 b1 w2 b2".split():
    _INS["f_" + _n] = "L0_ffn_" + _n


def kernel(**inputs):
    import concourse.bacc as bacc
    from concourse.bass_utils import run_bass_kernel_spmd as run

    nc = bacc.Bacc("TRN2", target_bir_lowering=False, num_devices=1)
    arrays, args = {}, {}
    given = {n: np.ascontiguousarray(inputs[full]) for n, full in _INS.items()}
    given.update(constants())
    for name, a in given.items():
        arrays[f"in_{name}"] = a
        args[name] = nc.dram_tensor(f"in_{name}", a.shape, mybir.dt.from_np(a.dtype), kind="ExternalInput").ap()
    out = nc.dram_tensor("out_x", (B, T, H), mybir.dt.float32, kind="ExternalOutput").ap()
    build(nc, args, out)
    return run(nc, [arrays], core_ids=[0]).results[0]["out_x"]
```

```python
import numpy as np
from contextlib import ExitStack

import concourse.bass as bass
from concourse import mybir

B, T, H = 8, 256, 128
D, CH = 32, 64
NCH = T // CH
G, R = 2, 4
HEADS, DH, WIN = 8, 64, 64
INNER = HEADS * DH
HID = int(H * 4 * 2 / 3)
LAYERS = 2
PAIRS = HEADS // 2
NWIN = T // WIN
EPS = 1e-6
LN_EPS = 1e-5
NT = B * T // 128
HB = [128, 128, HID - 256]


def build(nc, t, out):
    f32, bf16 = mybir.dt.float32, mybir.dt.bfloat16
    ALU, ACT, AX = mybir.AluOpType, mybir.ActivationFunctionType, mybir.AxisListType
    MUL, ADD, SUB, MAX, MIN, POW = ALU.mult, ALU.add, ALU.subtract, ALU.max, ALU.min, ALU.pow

    with ExitStack() as ctx:
        def sb(name, shape, dt=f32):
            return ctx.enter_context(nc.sbuf_tensor(name, shape, dt))

        def sem(name):
            return ctx.enter_context(nc.semaphore(name))

        bank = [ctx.enter_context(nc.psum_tensor(f"bank{i}", [128, 512], f32)) for i in range(8)]

        ident = sb("ident", [128, 128])
        sel = sb("sel", [128, 257])
        eyes = sb("eyes", [128, CH + R])
        w_all = sb("w_all", [128, 320 + 12 + 3 + 1])
        w_t = w_all[:, 0:320]
        cw = w_all[:, 320:332].rearrange("p (i k) -> p i k", i=3)
        cb = w_all[:, 332:335]
        gate_bias = w_all[0:96, 335:336]
        norm_gb = sb("norm_gb", [128, 2, H])
        norm_g, gb = norm_gb[:, 0, :], norm_gb[:, 1, :]
        wo_bd = sb("wo_bd", [128, R, H])

        x_tok = sb("x_tok", [128, NT, H])
        x_fm = sb("x_fm", [H, B * T])
        kvq = sb("kvq", [128, 3, G, T])
        kvq_c = kvq[:, :, :, :].rearrange("p i g (c t) -> p i g c t", t=CH)
        w_end = sb("w_end", [128, 2, NCH, R])
        theta = sb("theta", [128, NCH, R])
        q_a = sb("q_a", [128, G, T])
        q_b = sb("q_b", [128, G, T])
        kc = sb("kc", [128, G, CH])
        qc = sb("qc", [128, R, G, CH])
        sig = sb("sig", [128, G, CH])
        act = sb("act", [128, G, CH])
        t_sp = sb("t_sp", [128, G, CH])
        dact = sb("dact", [128, G, CH])
        err = sb("err", [128, G, CH])
        dz = sb("dz", [128, G, CH])
        tokm = sb("tokm", [128, 4, R, D])
        sqm = sb("sqm", [128, 4, R, D])
        n4 = sb("n4", [128, 4 * R])
        n2 = sb("n2", [128, 2 * R])
        n1 = sb("n1", [128, R])
        inv = sb("inv", [128, R])
        minus_half = sb("minus_half", [128, 2 * HEADS])
        coef = sb("coef", [128, R])
        gc = sb("gc", [128, 2, R, D])
        u = sb("u", [128, 2, 2, R, D])
        q1 = sb("q1", [128, R, CH])
        sig_y = sb("sig_y", [128, G, CH])
        hy = sb("hy", [128, G, CH])
        hc = sb("hc", [128, R, G, CH])
        h_a = sb("h_a", [128, G, CH])
        h_b = sb("h_b", [128, G, CH])
        am = sb("am", [128, R, CH])
        w_st = sb("w_st", [128, G, 3, D])
        s_st = sb("s_st", [128, G, 3, D])
        t_st = sb("t_st", [128, G, 3, D])
        bd = sb("bd", [128, G, 5, 128])
        ret = sb("ret", [128, G, T])
        ret_c = ret[:, :, :].rearrange("p g (c t) -> p g c t", t=CH)
        gb_n = sb("gb_n", [128, H])
        bd_y = sb("bd_y", [128, G, 2, 128])
        act_y = sb("act_y", [128, G, CH])
        warm = sb("warm", [128, 1])
        eta_floor = sb("eta_floor", [128, 1])
        x_stage = sb("x_stage", [128, R * 128])
        st_sq, st_inv, st_mean, st_var, st_rstd = (sb(f"st_{n}", [128, 4, R]) for n in ("sq", "inv", "mean", "var", "rstd"))
        x1 = sb("x1", [128, NT, H])

        ident_bf = sb("ident_bf", [128, 128], bf16)
        masks_in = sb("masks_in", [128, 3, 2 * WIN])
        masks = sb("masks", [128, 3, 2 * WIN], bf16)
        tabs = sb("tabs", [128, 2, 2, 2, DH])
        scales = sb("scales", [128, LAYERS, 2, DH])
        cos_t = sb("cos_t", [128, LAYERS, 2, 2, DH])
        sin_t = sb("sin_t", [128, LAYERS, 2, 2, DH])
        wqkv = sb("wqkv", [H, LAYERS, 3 * INNER])
        wo_sb = sb("wo_sb", [128, LAYERS, 4, H])
        w1 = sb("w1", [H, LAYERS, 2 * HID])
        w2 = sb("w2", [128, LAYERS, 3, H])
        ln_gb = sb("ln_gb", [H, 2, LAYERS])
        b1 = sb("b1", [128, LAYERS, 6])
        mean_h = sb("mean_h", [128, 128])
        ones = sb("ones", [128, 128])
        xs = [sb(f"xs{i}", [128, 2, H]) for i in range(2)]
        xa = [sb(f"xa{i}", [128, 2, H]) for i in range(2)]
        fm = sb("fm", [H, T + 2])
        h_fm = sb("h_fm", [H, T + 2])
        qb = [sb(f"qb{i}", [128, NWIN, 4, 2, WIN]) for i in range(2)]
        kt = [sb(f"kt{i}", [128, 4, T]) for i in range(2)]
        ss = [sb(f"ss{i}", [128, 2 * HEADS]) for i in range(2)]
        rn = [sb(f"rn{i}", [128, 2 * HEADS]) for i in range(2)]
        h_var = sb("h_var", [128, 2])
        h_inv = sb("h_inv", [128, 2])
        diag = sb("diag", [128, 2, 128])
        nmx = [sb(f"nmx{i}", [128, 4]) for i in range(2)]
        rs = [sb(f"rs{i}", [128, 4]) for i in range(2)]
        rr = [sb(f"rr{i}", [128, 4]) for i in range(2)]
        hh = sb("hh", [128, 3, T])
        yb = [sb(f"yb{i}", [128, 2, H]) for i in range(2)]
        y_sum = sb("y_sum", [128, 2])
        y_sq = sb("y_sq", [128, 2, H])
        y_var = sb("y_var", [128, 2])
        y_inv = sb("y_inv", [128, 2])
        y_all = x_tok

        mixer_scratch = ExitStack()

        def sb_mixer(name, shape):
            return mixer_scratch.enter_context(nc.sbuf_tensor(name, shape, f32))

        keep_f = sb_mixer("keep_f", [128, G * T])
        eta_f = sb_mixer("eta_f", [128, G * T])
        first_f = sb_mixer("first_f", [128, G * T])
        a_cum = sb_mixer("a_cum", [128, G * T])
        b_cum = sb_mixer("b_cum", [128, G * T])
        e_cum = sb_mixer("e_cum", [128, G * T])
        keep_s = sb_mixer("keep_s", [128, R * T])
        eta_s = sb_mixer("eta_s", [128, R * T])
        eye_s = sb_mixer("eye_s", [128, R * T])
        p_mat = sb_mixer("p_mat", [128, R * T])
        m_mat = sb_mixer("m_mat", [128, R * T])
        sg_all = sb_mixer("sg_all", [128, B * T])
        sp_abs = sb_mixer("sp_abs", [128, B * T])
        mixer_scratch.close()
        vt = [sb(f"vt{i}", [128, 3, INNER]) for i in range(2)]
        qk = [sb(f"qk{i}", [128, 2, HEADS, DH]) for i in range(2)]
        qk_sq = sb("qk_sq", [128, 2, HEADS, DH])
        rot = [sb(f"rot{i}", [128, 2, HEADS, DH]) for i in range(2)]
        rot_s = [sb(f"rot_s{i}", [128, 2, HEADS, DH]) for i in range(2)]
        pm = [sb(f"pm{i}", [128, 4, 2 * WIN]) for i in range(2)]
        pt = sb("pt", [128, 4, 2 * WIN])
        ot = sb("ot", [128, 4, 128])
        h_cen = sb("h_cen", [H, T])
        h_sq = sb("h_sq", [H, T])
        h_n = sb("h_n", [H, T])
        gl = sb("gl", [128, 3, T])

        gates_c = sp_abs[:, :].rearrange("p (c i h) -> p c i h", c=NCH, i=R)
        gates = sp_abs[:, :].rearrange("p (g r h d) -> p g h r d", g=G, r=R, h=2)
        mixed = sg_all[:, :].rearrange("p (m r h) -> p m r h", m=4, r=R)

        squared = x_fm[:, :].rearrange("p (m r h) -> p m r h", m=4, r=R)

        x_fm_c = x_fm[:, :].rearrange("p (c x) -> p c x", c=NCH)

        def per_chunk(a, g_dim):
            return a[:, :].rearrange("p (g c t) -> p g c t", g=g_dim, t=CH)

        a_cum_c, b_cum_c, e_cum_c = (per_chunk(a, G) for a in (a_cum, b_cum, e_cum))
        m_mat_c, p_mat_c = per_chunk(m_mat, R), per_chunk(p_mat, R)
        q_a_c = q_a[:, :, :].rearrange("p g (c t) -> p g c t", t=CH)
        q_b_c = q_b[:, :, :].rearrange("p g (c t) -> p g c t", t=CH)
        def gt(b, g=None):
            v = b[:, 0:G * CH].rearrange("p (g t) -> p g t", g=G)
            return v if g is None else v[:, g, :]

        ak_bank = bank[2][:, 0:256].rearrange("p (k x) -> p k x", k=2)
        de_bank = bank[1][:, 128:384].rearrange("p (k x) -> p k x", k=2)
        ah_bank = bank[3][:, R * CH:2 * R * CH].rearrange("p (r t) -> p r t", r=R)
        qk_bank = bank[3][:, 0:R * CH].rearrange("p (r t) -> p r t", r=R)
        d_bank = [bank[4 + g][:, 0:6 * D].rearrange("p (j k o) -> p j k o", j=2, k=3) for g in range(G)]
        y_bank = [bank[6 + g][:, 0:CH] for g in range(G)]

        names = """x_loaded0 x_loaded1 x_loaded2 x_loaded3 w_loaded small_loaded end_loaded stored zeroed projected
          eye_ready theta_ready conv_first conv_v gates_ready gates_out spread_f spread_s theta_out
          keep_done factors_s scanned first_done mats_ready qab_ready gates_abs gates_relu gates_exp
          gates_ln kc_free kc_ready qc_ready z_ready qk_ready pred_ready da_ready ak_ready tok_ready
          y1_ready d_ready ah_ready y2_ready ret_done sig_ready act_ready sp_step sp_ready q1_ready
          err_ready dz_ready tokm_ready sq_ready norm_step norm_ready inv_norm ms_ready ms_inv gc_ready
          u_ready sigy_ready h_ready kept_ready hc_v hc_s hab_ready am_ready st_ready exp_v exp_s mix_out
          x_staged gates_turned gates_added gw_scaled osq_ready mix_step on_ready mean_ready csq_ready
          x1_ready f_loaded tabs_ready w1_ready w1_scaled bias_out f_zeroed xs_loaded xf_turned fm_ready
          proj proj_out ss_step rn_ready ss_ready sum_ready c_ready s_ready rot_ready qk_turned qt_out
          kt_out window_started score_ready max_ready exp_done rr_ready pn_ready p_turned p_out pv_done
          o_out wo_done xa_ready h_turned h_out mu_done hc_ready hsq_ready var_done diag_ready hn_ready
          w1_done gelu_done hh_ready w2_done x_ready pre_ready fin_step ymean_ready ysq_ready yvar_ready
          yinv_ready y_ready var_ready hinv_ready bc_done
        """.split()
        s = {n: sem(n) for n in names}

        block = ctx.enter_context(nc.Block())

        def over_chunks(eng, chunk, ready):
            chunk(0, None, True)
            with eng.Fori(1, NCH - 1) as c:
                chunk(c, c - 1, True)
            chunk(NCH - 1, NCH - 2, False)
            ready()
            chunk(None, NCH - 1, False)

        ORDER = (0, 2, 1, 3)
        TAIL = ((0, 0), (0, 1), (0, 2), (0, 3), (1, 0), (1, 1), (1, 2), (1, 3))

        def expand(copy, r):
            rows = slice(D * r, D * r + D)
            copy(bd[rows, :, 0:3, rows], w_st[rows, :, :, :])
            return copy(bd[rows, :, 3:5, rows], s_st[rows, :, 0:2, :])

        SMALL = 0
        FL = 0
        y_tiles = y_all[:, :, :].rearrange("p (b h) d -> p b h d", h=2)
        x1_tiles = x1[:, :, :].rearrange("p (b h) d -> p b h d", h=2)

        def count(per, n, k):
            it, c = n
            return it * (2 * per) + (c * per + k)

        def spot(n):
            return n[1] // B, n[1] % 2

        def batch(n):
            return n[0] * 2 + n[1] % B

        def proj_bank(n, k):
            return bank[4 + (k % 2 if n[1] == 0 else 0)]

        def over_items(eng, project_first, step):
            project_first()
            step((0, 0), (0, 1), None)
            with eng.Fori(0, B // 2 - 1) as it:
                step((it, 1), (it, 2), (it, 0))
                step((it, 2), (it, 3), (it, 1))
            step((0, B - 1), (0, B), (0, B - 2))
            step((0, B), (0, B + 1), (0, B - 1))
            with eng.Fori(0, B // 2 - 1) as it:
                step((it, B + 1), (it, B + 2), (it, B))
                step((it, B + 2), (it, B + 3), (it, B + 1))
            step((0, 2 * B - 1), None, (0, 2 * B - 2))
            step(None, None, (0, 2 * B - 1))

        def keys(w):
            return slice(0, WIN if w == 0 else 2 * WIN)

        def heads4(b):
            return bank[b][:, :].rearrange("p (k x) -> p k x", k=4)


        @block.sync
        def _(sp):
            nonlocal SMALL, FL
            sp.dma_start(w_all[:, :], t["w_all"]).then_inc(s["w_loaded"], 16)
            for i in range(4):
                cols = slice(2 * T * i, 2 * T * i + 2 * T)
                sp.dma_start(x_fm[:, cols], t["x_fm"][:, cols]).then_inc(s[f"x_loaded{i}"], 16)
            small = [(sel[:, :], t["c_sel"]), (eyes[:, :], t["c_eyes"]), (w_st[:, :, :, :], t["w_st"]),
                     (norm_gb[:, :, :], t["norm_gb"])]
            for dst, src in small:
                sp.dma_start(dst, src).then_inc(s["small_loaded"], 16)
            SMALL = 16 * len(small)
            f_loads = [(scales, "scales"), (tabs, "c_tabs"), (w1, "w1"), (ln_gb, "ln_gb"), (b1, "b1"),
                       (masks_in, "c_masks"), (ident, "c_ident"), (wqkv, "wqkv"), (wo_sb, "wo"), (w2, "w2")]
            for dst, name in f_loads:
                sp.dma_start(dst[tuple(slice(None) for _ in t[name].shape)], t[name]).then_inc(s["f_loaded"], 16)
            FL = 16 * len(f_loads)
            sp.dma_start(wo_bd[:, :, :], t["wo_bd"]).then_inc(s["end_loaded"], 16)
            sp.dma_start(x_tok[:, :, :], t["hidden"].rearrange("b (h p) d -> p (b h) d", p=128)
                         ).then_inc(s["end_loaded"], 16)
            with sp.Fori(0, PAIRS) as it:
                for sl in range(2):
                    sp.wait_ge(s["y_ready"], it * 2 + (sl + 1))
                    sp.dma_start(out[it * 2 + sl, :, :].rearrange("(h p) d -> p h d", p=128),
                                 y_tiles[:, it * 2 + sl, :, :]).then_inc(s["stored"], 16)
            sp.wait_ge(s["stored"], 16 * B)

        @block.gpsimd
        def _(po):
            po.memset(bd[:, :, :, :], 0.0)
            po.memset(hc[:, :, :, :], 0.0)
            po.memset(s_st[:, :, :, :], 0.0)
            po.memset(minus_half[:, :], -0.5)
            po.memset(eta_floor[:, :], 0.05)
            po.memset(first_f[:, :], 0.0).then_inc(s["zeroed"], 1)
            for i in range(2):
                po.memset(qb[i][:, :, :, :, :], 0.0)
            po.memset(fm[:, :], 0.0)
            po.memset(h_fm[:, :], 0.0)
            po.memset(mean_h[:, :], 1.0 / H)
            po.memset(ones[:, :], 1.0)
            po.memset(hh[:, :, :], 1.0).then_inc(s["f_zeroed"], 1)
            po.wait_ge(s["f_loaded"], FL)
            q = DH // 2
            for l in range(LAYERS):
                for k in range(2):
                    shape = [128, 2, DH]
                    po.tensor_tensor(cos_t[:, l, :, k, :], tabs[:, :, 0, k, :],
                                     scales[:, l, k, :].unsqueeze(1).to_broadcast(shape), MUL)
                    for to, fro in ((slice(0, q), slice(q, DH)), (slice(q, DH), slice(0, q))):
                        ins = po.tensor_tensor(sin_t[:, l, :, k, to], tabs[:, :, 1, k, to],
                                               scales[:, l, k, fro].unsqueeze(1).to_broadcast([128, 2, q]), MUL)
            ins.then_inc(s["tabs_ready"], 1)
            po.sem_inc(s["x_ready"], 1)
            po.wait_ge(s["scanned"], 3)
            po.wait_ge(s["conv_v"], 3)
            po.tensor_tensor(q_a[:, :, :], kvq[:, 2, :, :], a_cum[:, :].rearrange("p (g t) -> p g t", g=G), MUL)
            po.tensor_tensor(q_b[:, :, :], kvq[:, 2, :, :], b_cum[:, :].rearrange("p (g t) -> p g t", g=G), MUL
                             ).then_inc(s["qab_ready"], 1)

            def chunk(c, d, more):
                if c is not None:
                    po.wait_ge(s["conv_v"], 3)
                    po.wait_ge(s["kc_free"], c + 1)
                    po.tensor_copy(kc[:, :, :], kvq_c[:, 0, :, c, :]).then_inc(s["kc_ready"], 1)
                    for g in range(G):
                        ins = po.tensor_tensor(qc[:, :, g, :],
                                               kvq_c[:, 2, g, c, :].unsqueeze(1).to_broadcast([128, R, CH]),
                                               eyes[:, CH:CH + R].unsqueeze(2).to_broadcast([128, R, CH]), MUL)
                    ins.then_inc(s["qc_ready"], 1)
                if d is not None:
                    po.wait_ge(s["h_ready"], d + 1)
                    po.tensor_tensor(h_a[:, :, :], hy[:, :, :], a_cum_c[:, :, d, :], MUL)
                    po.tensor_tensor(h_b[:, :, :], hy[:, :, :], b_cum_c[:, :, d, :], MUL).then_inc(s["hab_ready"], 1)
                if c is not None:
                    po.wait_ge(s["act_ready"], c + 1)
                    po.tensor_tensor(t_sp[:, :, :], act[:, :, :], sig[:, :, :], MUL).then_inc(s["sp_step"], 1)
                    po.wait_ge(s["sp_step"], c * 2 + 1)
                    po.tensor_tensor(t_sp[:, :, :], act[:, :, :], t_sp[:, :, :], SUB).then_inc(s["sp_step"], 1)
                    po.wait_ge(s["sp_step"], c * 2 + 2)
                    po.tensor_tensor(dact[:, :, :], t_sp[:, :, :], sig[:, :, :], ADD).then_inc(s["sp_ready"], 1)
                    po.tensor_copy(x_stage[:, :], x_fm_c[:, c, :]).then_inc(s["x_staged"], 1)
                    po.wait_ge(s["norm_ready"], c + 1)
                    po.tensor_tensor(inv[:, :], n1[:, :], minus_half[:, 0:R], POW).then_inc(s["inv_norm"], 1)
                    if d is not None:
                        po.wait_ge(s["conv_v"], 3)
                        po.wait_ge(s["y2_ready"], d + 1)
                    po.tensor_copy(act_y[:, :, :], act[:, :, :])
                    po.tensor_copy(bd_y[:, :, 0, :], bd[:, :, 1, :])
                    po.tensor_copy(bd_y[:, :, 1, :], bd[:, :, 4, :]).then_inc(s["kept_ready"], 1)

            over_chunks(po, chunk, lambda: None)
            def load_xs(n):
                l, sl = spot(n)
                po.wait_ge(s["x1_ready"], 4 if n[1] else 3)
                if l:
                    po.wait_ge(s["x_ready"], count(1, n, 2 - B))
                if n[1] >= 2:
                    po.wait_ge(s["xa_ready"], count(2, n, -2))
                src = x1_tiles if l == 0 else y_tiles
                po.tensor_copy(xs[sl][:, :, :], src[:, batch(n), :, :]).then_inc(s["xs_loaded"], 1)

            def sin_part(n, tile, kind):
                l, sl = spot(n)
                po.wait_ge(s["proj_out"], count(6, n, 3 * tile + kind + 1))
                if kind == 0 and n[1]:
                    po.wait_ge(s["rot_ready"], count(2, n, tile - 1))
                for to, fro in ((slice(0, q), slice(q, DH)), (slice(q, DH), slice(0, q))):
                    ins = po.tensor_tensor(rot_s[tile][:, kind, :, to], qk[tile][:, kind, :, fro],
                                           sin_t[:, l, tile, kind, to].unsqueeze(1).to_broadcast([128, HEADS, q]), MUL)
                ins.then_inc(s["s_ready"], 1)

            def inv_norms(n, tile):
                po.wait_ge(s["ss_ready"], count(2, n, tile + 1))
                po.tensor_tensor(rn[tile][:, :], ss[tile][:, :], minus_half[:, :], POW).then_inc(s["rn_ready"], 1)

            def inv_std(n):
                po.wait_ge(s["var_ready"], count(1, n, 1))
                po.tensor_tensor(h_inv[:, :], h_var[:, :], minus_half[:, 0:2], POW).then_inc(s["hinv_ready"], 1)

            def normalise(n, w):
                po.wait_ge(s["rr_ready"], count(4, n, w + 1))
                p = pm[w % 2][:, :, keys(w)]
                po.tensor_tensor(p, p, rr[w % 2][:, :].unsqueeze(2).to_broadcast([128, 4, keys(w).stop]), MUL
                                 ).then_inc(s["pn_ready"], 1)

            def last_pre(n):
                l, sl = spot(n)
                po.wait_ge(s["x1_ready"], 4)
                po.wait_ge(s["xa_ready"], count(2, n, 2))
                po.tensor_tensor(yb[sl][:, :, :], xa[sl][:, :, :], x1_tiles[:, batch(n), :, :], ADD
                                 ).then_inc(s["pre_ready"], 1)

            def last_inv(n):
                po.wait_ge(s["yvar_ready"], count(1, n, 1 - B))
                po.tensor_tensor(y_inv[:, :], y_var[:, :], minus_half[:, 0:2], POW).then_inc(s["yinv_ready"], 1)

            def mixer_roots(first, last):
                for k in range(first, last):
                    po.wait_ge(s["ms_ready"], k + 1)
                    src, dst = ((st_sq, st_inv), (st_var, st_rstd))[TAIL[k][0]]
                    m = TAIL[k][1]
                    po.tensor_tensor(dst[:, m, :], src[:, m, :], minus_half[:, 0:R], POW).then_inc(s["ms_inv"], 1)

            def project_first():
                mixer_roots(0, 7)
                load_xs((0, 0))
                mixer_roots(7, 8)
                po.wait_ge(s["x1_ready"], 4)
                sin_part((0, 0), 0, 0)
                sin_part((0, 0), 0, 1)
                inv_norms((0, 0), 0)
                sin_part((0, 0), 1, 0)
                sin_part((0, 0), 1, 1)
                inv_norms((0, 0), 1)

            def step(a, p, f):
                if p:
                    load_xs(p)
                if a:
                    normalise(a, 0)
                    normalise(a, 1)
                if f:
                    inv_std(f)
                if p:
                    sin_part(p, 0, 0)
                if a:
                    normalise(a, 2)
                if f and spot(f)[0] == 1:
                    last_pre(f)
                if p:
                    sin_part(p, 0, 1)
                    inv_norms(p, 0)
                if a:
                    normalise(a, 3)
                if p:
                    sin_part(p, 1, 0)
                    sin_part(p, 1, 1)
                    inv_norms(p, 1)
                if f and spot(f)[0] == 1:
                    last_inv(f)

            over_items(po, project_first, step)

        @block.tensor
        def _(pe):
            pe.wait_ge(s["w_loaded"], 16)
            for i in range(4):
                pe.wait_ge(s[f"x_loaded{i}"], 16)
            for i in range(3):
                for g in range(G):
                    for r in range(R):
                        b = R * g + r
                        ins = pe.matmul(bank[i][D * r:D * r + D, T * g:T * g + T], w_t[:, D * i:D * i + D],
                                        x_fm[:, T * b:T * b + T], start=True, stop=True)
                ins.then_inc(s["projected"], 1)
            for i in range(4):
                pe.matmul(bank[3 + i][0:96, :], w_t[:, 96:192], x_fm[:, 512 * i:512 * i + 512],
                          start=True, stop=True).then_inc(s["gates_out"], 1)
            pe.wait_ge(s["small_loaded"], SMALL)
            pe.wait_ge(s["gates_ready"], 4)
            for i, col in ((7, 128), (0, 0)):
                if i == 0:
                    pe.wait_ge(s["conv_v"], 1)
                for g in range(G):
                    for r in range(R):
                        b = R * g + r
                        ins = pe.matmul(bank[i][D * r:D * r + D, T * g:T * g + T], sel[0:64, col:col + D],
                                        sg_all[0:64, T * b:T * b + T], start=True, stop=True)
                ins.then_inc(s["spread_f"], 1)
            pe.wait_ge(s["conv_v"], 3)
            pe.wait_ge(s["f_loaded"], FL)
            for l in range(LAYERS):
                for part in range(2):
                    for k in range(3):
                        at_w = HID * part + 128 * k
                        col = 6 * l + 3 * part + k
                        ins = pe.matmul(bank[2][0:HB[k], col:col + 1], w1[:, l, at_w:at_w + HB[k]],
                                        ln_gb[:, 1, l:l + 1], start=True, stop=True)
            ins.then_inc(s["bias_out"], 1)
            pe.wait_ge(s["gates_abs"], 1)
            pe.wait_ge(s["gates_relu"], 1)
            pe.wait_ge(s["conv_v"], 3)
            def spread_s(first_bank, col):
                for half in range(2):
                    for g in range(G):
                        at = T * R * g + 512 * half
                        ins = pe.matmul(bank[first_bank + half][CH * g:CH * g + CH, :], sel[0:64, col:col + CH],
                                        sg_all[0:64, at:at + 512], start=True, stop=True)
                ins.then_inc(s["spread_s"], 1)

            spread_s(3, 128)
            pe.wait_ge(s["w1_ready"], 1)
            spread_s(1, 0)
            pe.wait_ge(s["gates_relu"], 2)
            pe.wait_ge(s["gates_ln"], 1)
            for g in range(G):
                for r in range(R):
                    for c in range(NCH):
                        at = T * (R * g + r) + CH * c
                        ins = pe.matmul(bank[5][CH * g:CH * g + CH, R * c + r:R * c + r + 1],
                                        sg_all[:, at:at + CH], sel[:, 256:257], start=True, stop=True)
            ins.then_inc(s["theta_out"], 1)
            pe.wait_ge(s["theta_ready"], 1)
            pe.wait_ge(s["mats_ready"], 1)
            pe.wait_ge(s["qab_ready"], 1)
            pe.sem_inc(s["kc_free"], 1)
            pe.sem_inc(s["gates_added"], 1)

            def mix_out(i):
                g, half = ORDER[i] // 2, ORDER[i] % 2
                pe.wait_ge(s["gates_added"], 1 + NCH)
                pe.wait_ge(s["end_loaded"], 32)
                pe.wait_ge(s["ret_done"], NCH + 1 if half else NCH // 2 + 1)
                pe.matmul(bank[i][:, :], ret[:, g, 128 * half:128 * half + 128], wo_bd[:, :, :],
                          start=True, stop=True).then_inc(s["mix_out"], 1)

            def chunk(c, d, more):
                if c is not None:
                    pe.wait_ge(s["gates_added"], c + 1)
                    pe.wait_ge(s["kc_ready"], c + 1)
                    pe.wait_ge(s["exp_v"], c + 1)
                    pe.wait_ge(s["exp_s"], c + 1)
                    for g in range(G):
                        ins = pe.matmul(gt(bank[0], g), bd[:, g, 0, :], kc[:, g, :], start=True, stop=True)
                    ins.then_inc(s["z_ready"], 1)
                    pe.wait_ge(s["qc_ready"], c + 1)
                    for g in range(G):
                        ins = pe.matmul(qk_bank[CH * g:CH * g + CH, :, :], kc[:, g, :], qc[:, :, g, :],
                                        start=True, stop=True)
                    ins.then_inc(s["qk_ready"], 1)
                    pe.wait_ge(s["act_ready"], c + 1)
                    for g in range(G):
                        ins = pe.matmul(gt(bank[1], g), bd[:, g, 1, :], act[:, g, :], start=True, stop=True)
                    ins.then_inc(s["pred_ready"], 1)
                    pe.transpose(ak_bank[:, 1, :], kc[:, :, :], ident[:, :])
                    pe.transpose(ak_bank[:, 0, :], act[:, :, :], ident[:, :]).then_inc(s["ak_ready"], 1)
                    pe.wait_ge(s["err_ready"], c + 1)
                    for g in range(G):
                        ins = pe.matmul(gt(bank[0], g), bd[:, g, 2, :], err[:, g, :], start=True, stop=True)
                    ins.then_inc(s["da_ready"], 1)
                    pe.transpose(de_bank[:, 1, :], err[:, :, :], ident[:, :])
                    pe.wait_ge(s["dz_ready"], c + 1)
                    pe.transpose(de_bank[:, 0, :], dz[:, :, :], ident[:, :]).then_inc(s["tok_ready"], 1)
                if d is not None:
                    pe.wait_ge(s["kept_ready"], d + 1)
                    pe.wait_ge(s["hc_v"], d + 1)
                    pe.wait_ge(s["hc_s"], d + 1)
                    if c is not None:
                        pe.wait_ge(s["q1_ready"], c + 1)
                    for g in range(G):
                        ins = pe.matmul(ah_bank[CH * g:CH * g + CH, :, :], act_y[:, g, :], hc[:, :, g, :],
                                        start=True, stop=True)
                    ins.then_inc(s["ah_ready"], 1)
                    if c is None:
                        mix_out(1)
                if c is not None:
                    pe.wait_ge(s["gw_scaled"], 1)
                    pe.wait_ge(s["x_staged"], c + 1)
                    for i in range(R):
                        ins = pe.matmul(bank[0][:, 128 * i:128 * i + 128], x_stage[:, 128 * i:128 * i + 128],
                                        w_t[:, 192:320], start=True, stop=True)
                    ins.then_inc(s["gates_turned"], 1)
                if d is not None:
                    pe.wait_ge(s["hab_ready"], d + 1)
                    pe.wait_ge(s["am_ready"], d + 1)
                    for g in range(G):
                        pe.matmul(y_bank[g], bd_y[:, g, 0, :], h_a[:, g, :], start=True, stop=False)
                        pe.matmul(y_bank[g], bd_y[:, g, 1, :], h_b[:, g, :], start=False, stop=True)
                    for r in range(R):
                        for g in range(G):
                            rows, cols = slice(CH * g, CH * g + CH), slice(D * r, D * r + D)
                            ins = pe.matmul(y_bank[g][cols, :], gc[rows, 1, r, :], am[rows, r, :],
                                            start=False, stop=True, skip_group_check=True)
                    ins.then_inc(s["y2_ready"], 1)
                if c is not None:
                    pe.wait_ge(s["ret_done"], c + 1)
                    for g in range(G):
                        pe.matmul(y_bank[g], bd[:, g, 0, :], q_a_c[:, g, c, :], start=True, stop=False)
                        pe.matmul(y_bank[g], bd[:, g, 3, :], q_b_c[:, g, c, :], start=False, stop=True)
                    if not more:
                        pe.wait_ge(s["gc_ready"], c + 1)
                    if more:
                        pe.wait_ge(s["u_ready"], c + 1)
                        pe.sem_inc(s["kc_free"], 1)
                        for r in range(R):
                            for g in range(G):
                                rows, cols = slice(CH * g, CH * g + CH), slice(D * r, D * r + D)
                                pe.matmul(d_bank[g][cols, :, 0, :], tokm[rows, 3, r, :], u[rows, :, 0, r, :],
                                          start=True, stop=True)
                                pe.matmul(d_bank[g][cols, :, 1, :], tokm[rows, 0, r, :], u[rows, :, 1, r, :],
                                          start=True, stop=True)
                                for j in range(2):
                                    ins = pe.matmul(d_bank[g][cols, j, 2, :], u[rows, j, 1, r, :], tokm[rows, 0, r, :],
                                                    start=True, stop=True)
                        ins.then_inc(s["d_ready"], 1)
                    for r in range(R):
                        for g in range(G):
                            rows, cols = slice(CH * g, CH * g + CH), slice(D * r, D * r + D)
                            ins = pe.matmul(y_bank[g][cols, :], gc[rows, 0, r, :], q1[rows, r, :],
                                            start=False, stop=True, skip_group_check=True)
                    ins.then_inc(s["y1_ready"], 1)

            over_chunks(pe, chunk, lambda: mix_out(0))
            mix_out(2)
            mix_out(3)

            def turn_x(n):
                l, sl = spot(n)
                pe.wait_ge(s["xs_loaded"], count(1, n, 1))
                if n[1]:
                    pe.wait_ge(s["kt_out"], count(2, n, 0))
                for tile in range(2):
                    ins = pe.transpose(bank[6][:, 128 * tile:128 * tile + 128], xs[sl][:, tile, :], ident[:, :])
                ins.then_inc(s["xf_turned"], 1)

            def project(n, k):
                l, sl = spot(n)
                if k == 0:
                    pe.wait_ge(s["fm_ready"], count(1, n, 1))
                if n[1] or k > 1:
                    pe.wait_ge(s["proj_out"], count(6, n, k) - (n[1] == 0))
                tile, kind = k // 3, k % 3
                pe.matmul(proj_bank(n, k)[:, :], fm[:, 128 * tile:128 * tile + 128],
                          wqkv[:, l, INNER * kind:INNER * kind + INNER], start=True, stop=True).then_inc(s["proj"], 1)

            def turn_qk(n, i):
                tile, kind = i // 2, i % 2
                pe.wait_ge(s["rot_ready"], count(2, n, tile + 1))
                if i:
                    pe.wait_ge(s["qt_out" if i % 2 else "kt_out"], count(2, n, (i + 1) // 2))
                for h in range(4):
                    ins = pe.transpose(bank[6][:, 128 * h:128 * h + 128], rot[tile][:, kind, 2 * h:2 * h + 2, :],
                                       ident[:, :])
                ins.then_inc(s["qk_turned"], 1)

            def scores(n, w):
                l, sl = spot(n)
                if w % 2 == 0:
                    pe.wait_ge(s["qt_out"], count(2, n, w // 2 + 1))
                    pe.wait_ge(s["kt_out"], count(2, n, w // 2 + 1))
                if n[1] or w >= 2:
                    pe.wait_ge(s["exp_done"], count(4, n, w - 1))
                b = w % 2
                kind = (0, 1, 2, 1)[w]
                n_keys = keys(w).stop
                pe.matmul(heads4(b)[:, :, 0:n_keys], ident_bf[:, :],
                          masks[:, kind, 0:n_keys].unsqueeze(1).to_broadcast([128, 4, n_keys]),
                          start=True, stop=False)
                for h in range(4):
                    q_blocks = qb[sl][:, w, h, :, :]
                    if w == 2:
                        for c, key in ((0, 2 * WIN), (WIN, WIN)):
                            ins = pe.matmul(heads4(b)[:, h, c:c + WIN], q_blocks, kt[sl][:, h, key:key + WIN],
                                            start=False, stop=(h == 3 and c > 0))
                    else:
                        key = 0 if w < 2 else 2 * WIN
                        ins = pe.matmul(heads4(b)[:, h, 0:n_keys], q_blocks, kt[sl][:, h, key:key + n_keys],
                                        start=False, stop=(h == 3))
                ins.then_inc(s["score_ready"], 1)

            def turn_p(n, w):
                if n[1] or w:
                    pe.wait_ge(s["p_out"], count(4, n, w))
                pe.wait_ge(s["pn_ready"], count(4, n, w + 1))
                if w == 0:
                    pe.sem_inc(s["window_started"], 1)
                for h in range(4):
                    ins = pe.transpose(heads4(2)[keys(w), h, :], pm[w % 2][:, h, keys(w)], ident[:, :])
                ins.then_inc(s["p_turned"], 1)

            def weigh_v(n, w):
                l, sl = spot(n)
                src = (0, 0, 2, 1)[w]
                pe.wait_ge(s["p_out"], count(4, n, w + 1))
                if w == 2 or (n[1] and w == 0):
                    pe.wait_ge(s["xa_ready"], count(2, n, w // 2))
                if w == 0:
                    pe.sem_inc(s["window_started"], 1)
                for h in range(4):
                    for e in range(2):
                        c = 128 * h + WIN * (w % 2)
                        ins = pe.matmul(bank[3][DH * e:DH * e + DH, c:c + WIN],
                                        vt[sl][keys(w), src, DH * (2 * h + e):DH * (2 * h + e) + DH],
                                        pt[keys(w), h, WIN * e:WIN * e + WIN], start=True, stop=True)
                if w % 2:
                    ins.then_inc(s["pv_done"], 1)

            def project_o(n, tile):
                l, sl = spot(n)
                pe.wait_ge(s["o_out"], count(2, n, tile + 1))
                for h in range(4):
                    ins = pe.matmul(bank[3][:, 128 * tile:128 * tile + 128], ot[:, h, :], wo_sb[:, l, h, :],
                                    start=(h == 0), stop=(h == 3))
                ins.then_inc(s["wo_done"], 1)

            def turn_h(n):
                l, sl = spot(n)
                pe.wait_ge(s["xa_ready"], count(2, n, 2))
                for tile in range(2):
                    ins = pe.transpose(bank[7][:, 128 * tile:128 * tile + 128], xa[sl][:, tile, :], ident[:, :])
                ins.then_inc(s["h_turned"], 1)

            def mean(n):
                l, sl = spot(n)
                pe.wait_ge(s["h_out"], count(1, n, 1))
                pe.wait_ge(s["x_ready"], count(1, n, 1))
                pe.matmul(bank[5][:, 0:T], mean_h[:, :], h_fm[:, 0:T], start=True, stop=True
                          ).then_inc(s["mu_done"], 1)

            def variance(n):
                pe.wait_ge(s["hsq_ready"], count(1, n, 1))
                for tile in range(2):
                    ins = pe.matmul(bank[7][:, tile:tile + 1], h_sq[:, 128 * tile:128 * tile + 128], mean_h[:, 0:1],
                                    start=True, stop=True)
                ins.then_inc(s["var_done"], 1)

            def spread_inv(n):
                pe.wait_ge(s["diag_ready"], count(1, n, 1))
                for tile in range(2):
                    ins = pe.matmul(bank[5][:, 128 * tile:128 * tile + 128], ones[:, :], diag[:, tile, :],
                                    start=True, stop=True)
                ins.then_inc(s["bc_done"], 1)

            def ffn_up(n, k):
                l, sl = spot(n)
                if k == 0:
                    pe.wait_ge(s["hn_ready"], count(1, n, 1))
                if k == 2:
                    pe.wait_ge(s["hh_ready"], count(3, n, 1))
                for part, c in ((1, 0), (0, T)):
                    at_w = HID * part + 128 * k
                    ins = pe.matmul(bank[(7, 5, 7)[k]][0:HB[k], c:c + T], w1[:, l, at_w:at_w + HB[k]], h_n[:, :],
                                    start=True, stop=True)
                ins.then_inc(s["w1_done"], 1)

            def ffn_down(n):
                l, sl = spot(n)
                pe.wait_ge(s["hh_ready"], count(3, n, 3))
                for tile in range(2):
                    for k in range(3):
                        rows = HB[k] + (k == 2)
                        ins = pe.matmul(bank[5][:, 128 * tile:128 * tile + 128],
                                        hh[0:rows, k, 128 * tile:128 * tile + 128], w2[0:rows, l, k, :],
                                        start=(k == 0), stop=(k == 2))
                ins.then_inc(s["w2_done"], 1)

            def project_first():
                pe.wait_ge(s["f_zeroed"], 1)
                pe.wait_ge(s["w1_scaled"], 1)
                turn_x((0, 0))
                project((0, 0), 0)
                project((0, 0), 1)
                project((0, 0), 2)
                project((0, 0), 3)
                project((0, 0), 4)
                turn_qk((0, 0), 0)
                turn_qk((0, 0), 1)
                project((0, 0), 5)

            def step(a, p, f):
                if a:
                    scores(a, 0)
                    scores(a, 1)
                if f:
                    project_o(f, 1)
                if a:
                    turn_qk(a, 2)
                if f:
                    turn_h(f)
                if a:
                    turn_qk(a, 3)
                    turn_p(a, 0)
                if f:
                    mean(f)
                if p:
                    turn_x(p)
                if a:
                    scores(a, 2)
                if p:
                    project(p, 0)
                if f:
                    variance(f)
                if a:
                    scores(a, 3)
                if p:
                    project(p, 1)
                if a:
                    weigh_v(a, 0)
                    turn_p(a, 1)
                if f:
                    spread_inv(f)
                if p:
                    project(p, 2)
                if a:
                    weigh_v(a, 1)
                    turn_p(a, 2)
                if f:
                    ffn_up(f, 0)
                if p:
                    project(p, 3)
                if f:
                    ffn_up(f, 1)
                    ffn_up(f, 2)
                if p:
                    project(p, 4)
                if a:
                    project_o(a, 0)
                if p:
                    turn_qk(p, 0)
                if f:
                    ffn_down(f)
                if a:
                    weigh_v(a, 2)
                    turn_p(a, 3)
                if p:
                    turn_qk(p, 1)
                    project(p, 5)
                if a:
                    weigh_v(a, 3)

            over_items(pe, project_first, step)

        @block.scalar
        def _(ac):
            ac.wait_ge(s["w_loaded"], 16)
            for i in range(3):
                ac.wait_ge(s["projected"], i + 1)
                ac.activation(kvq[:, i, :, :], bank[i][:, :].rearrange("p (g t) -> p g t", g=G), ACT.Identity,
                              bias=cb[:, i:i + 1], scale=cw[:, i, 3:4]).then_inc(s["conv_first"], 1)
            for i in range(4):
                cols = slice(512 * i, 512 * i + 512)
                ac.wait_ge(s["gates_out"], i + 1)
                ac.activation(sg_all[0:64, cols], bank[3 + i][0:64, :], ACT.Sigmoid, bias=gate_bias[0:64]
                              ).then_inc(s["gates_ready"], 1)
            for i in range(4):
                ins = ac.activation(sp_abs[64:96, 512 * i:512 * i + 512], bank[3 + i][64:96, :], ACT.Abs, bias=gate_bias[64:96])
            ins.then_inc(s["gates_abs"], 1)
            ac.wait_ge(s["gates_abs"], 1)
            ac.activation(sp_abs[64:96, :], sp_abs[64:96, :], ACT.Exp, scale=-1.0).then_inc(s["gates_exp"], 1)
            ac.wait_ge(s["gates_exp"], 1)
            ac.activation(sg_all[96:128, :], sp_abs[64:96, :], ACT.Ln, bias=1.0).then_inc(s["gates_ln"], 1)
            ac.wait_ge(s["zeroed"], 1)
            ac.wait_ge(s["small_loaded"], SMALL)
            expand(ac.copy, 2)
            expand(ac.copy, 3).then_inc(s["exp_s"], 1)
            ac.sem_inc(s["ret_done"], 1)

            for i, (first_bank, dst, bias, scale) in enumerate(((3, eta_s, eta_floor[:, 0:1], 1.0), (1, keep_s, 1.0, -1.0))):
                ac.wait_ge(s["spread_s"], i + 1)
                for half in range(2):
                    ins = ac.activation(dst[:, 512 * half:512 * half + 512], bank[first_bank + half][:, :],
                                        ACT.Identity, bias=bias, scale=scale)
                ins.then_inc(s["factors_s"], 1)
            ac.wait_ge(s["f_loaded"], FL)
            ac.wait_ge(s["bias_out"], 1)
            for l in range(LAYERS):
                ac.activation(w1[:, l, :], w1[:, l, :], ACT.Copy, scale=ln_gb[:, 0, l:l + 1])
            ac.copy(masks[:, :, :], masks_in[:, :, :])
            ac.copy(ident_bf[:, :], ident[:, :]).then_inc(s["w1_scaled"], 1)

            def rms_squares(i):
                ac.wait_ge(s["mix_out"], i + 1)
                for r in range(R):
                    ins = ac.activation(squared[:, i, r, :], bank[i][:, 128 * r:128 * r + 128], ACT.Square,
                                        accum_out=st_sq[:, i, r:r + 1])
                ins.then_inc(s["osq_ready"], 1)

            def norm_squares(i):
                ac.wait_ge(s["mean_ready"], i + 1)
                for r in range(R):
                    ins = ac.activation(squared[:, i, r, :], mixed[:, i, r, :], ACT.Square, bias=st_mean[:, i, r:r + 1],
                                        accum_out=st_var[:, i, r:r + 1])
                ins.then_inc(s["csq_ready"], 1)

            def chunk(c, d, more):
                if c is not None:
                    ac.activation(warm[:, :], minus_half[:, 0:1], ACT.Sigmoid)
                    ac.wait_ge(s["z_ready"], c + 1)
                    ac.activation(sig[:, :, :], gt(bank[0]), ACT.Sigmoid).then_inc(s["sig_ready"], 1)
                if d is not None:
                    ac.wait_ge(s["h_ready"], d + 1)
                    for r in (2, 3):
                        rows = slice(D * r, D * r + D)
                        ins = ac.activation(hc[rows, r, :, :], hy[rows, :, :], ACT.Copy)
                    ins.then_inc(s["hc_s"], 1)
                if c is None:
                    rms_squares(0)
                    rms_squares(1)
                if c is not None:
                    ac.wait_ge(s["tokm_ready"], c * 2 + 1)
                    for k in (0, 3):
                        ins = ac.activation(sqm[:, k, :, :], tokm[:, k, :, :], ACT.Square)
                    ins.then_inc(s["sq_ready"], 1)
                    ac.wait_ge(s["tokm_ready"], c * 2 + 2)
                    ac.activation(sqm[:, 1:3, :, :], tokm[:, 1:3, :, :], ACT.Square).then_inc(s["sq_ready"], 1)
                if d is not None:
                    ac.wait_ge(s["y2_ready"], d + 1)
                    for g in range(G):
                        ins = ac.activation(ret_c[:, g, d, :], y_bank[g], ACT.Copy)
                    ins.then_inc(s["ret_done"], 1)
                if c is not None:
                    ac.wait_ge(s["y1_ready"], c + 1)
                    for g in range(G):
                        ins = ac.activation(sig_y[:, g, :], y_bank[g], ACT.Sigmoid)
                    ins.then_inc(s["sigy_ready"], 1)
                if more:
                    ac.wait_ge(s["kept_ready"], c + 1)
                    ac.wait_ge(s["st_ready"], c + 1)
                    expand(ac.copy, 2)
                    expand(ac.copy, 3).then_inc(s["exp_s"], 1)

            over_chunks(ac, chunk, lambda: None)
            rms_squares(2)
            rms_squares(3)
            norm_squares(0)
            norm_squares(1)
            norm_squares(2)

            def shifted(dst, src):
                ac.activation(dst[0:64, 0:T], src[0:64, 0:T], ACT.Copy)
                return ac.activation(dst[64:128, 1:T + 1], src[64:128, 0:T], ACT.Copy)

            def copy_x(n):
                ac.wait_ge(s["xf_turned"], count(1, n, 1))
                shifted(fm, bank[6]).then_inc(s["fm_ready"], 1)

            def copy_h(n):
                ac.wait_ge(s["h_turned"], count(1, n, 1))
                shifted(h_fm, bank[7]).then_inc(s["h_out"], 1)

            def copy_proj(n, k):
                l, sl = spot(n)
                tile, kind = k // 3, k % 3
                ac.wait_ge(s["proj"], count(6, n, k + 1))
                src = proj_bank(n, k)
                if kind < 2:
                    if kind == 0 and n[1]:
                        ac.wait_ge(s["rot_ready"], count(2, n, tile - 1))
                    if not (n[1] == 0 and tile == 0):
                        ac.wait_ge(s["ss_ready"], count(2, n, tile))
                    view = src[:, :].rearrange("p (h d) -> p h d", d=DH)
                    ac.activation(qk_sq[:, kind, :, :], view, ACT.Square)
                    ac.activation(qk[tile][:, kind, :, :], view, ACT.Copy).then_inc(s["proj_out"], 1)
                else:
                    ac.activation(vt[sl][:, tile, :], src[:, :], ACT.Copy)
                    rows = slice(64, 128) if tile == 0 else slice(0, 64)
                    ac.activation(vt[sl][rows, 2, :], src[rows, :], ACT.Copy).then_inc(s["proj_out"], 1)

            def exps(n, w):
                ac.wait_ge(s["max_ready"], count(4, n, w + 1))
                if n[1] or w >= 2:
                    ac.wait_ge(s["p_turned"], count(4, n, w - 1))
                for h in range(4):
                    ins = ac.activation(pm[w % 2][:, h, keys(w)], heads4(w % 2)[:, h, keys(w)], ACT.Exp, bias=nmx[w % 2][:, h:h + 1],
                                        accum_out=rs[w % 2][:, h:h + 1])
                ins.then_inc(s["exp_done"], 1)

            def copy_o(n, tile):
                ac.wait_ge(s["pv_done"], count(2, n, tile + 1))
                ac.activation(ot[:, :, :], heads4(3), ACT.Copy).then_inc(s["o_out"], 1)

            def copy_q(n, tile):
                l, sl = spot(n)
                ac.wait_ge(s["qk_turned"], count(4, n, 2 * tile + 1))
                for e in range(2):
                    rows = slice(DH * e, DH * e + DH)
                    ins = ac.activation(qb[sl][rows, 2 * tile:2 * tile + 2, :, e, :].rearrange("p w h q -> p h w q"),
                                        bank[6][rows, :].rearrange("p (h w q) -> p h w q", h=4, w=2), ACT.Copy)
                ins.then_inc(s["qt_out"], 1)

            def squares(n):
                ac.wait_ge(s["hc_ready"], count(1, n, 1))
                ac.activation(h_sq[:, :], h_cen[:, :], ACT.Square).then_inc(s["hsq_ready"], 1)

            def last_sq(n):
                l, sl = spot(n)
                ac.wait_ge(s["ymean_ready"], count(1, n, 1 - B))
                for tile in range(2):
                    ins = ac.activation(y_sq[:, tile, :], yb[sl][:, tile, :], ACT.Square, bias=y_sum[:, tile:tile + 1],
                                        accum_out=y_var[:, tile:tile + 1])
                ins.then_inc(s["ysq_ready"], 1)

            def gelu(n, k):
                l, sl = spot(n)
                ac.wait_ge(s["w1_done"], count(3, n, k + 1))
                ac.activation(gl[0:HB[k], k, :], bank[(7, 5, 7)[k]][0:HB[k], 0:T], ACT.Gelu, bias=b1[0:HB[k], l, 3 + k:4 + k]
                              ).then_inc(s["gelu_done"], 1)

            def project_first():
                ac.wait_ge(s["f_zeroed"], 1)
                copy_x((0, 0))
                norm_squares(3)
                copy_proj((0, 0), 0)
                copy_proj((0, 0), 1)
                copy_proj((0, 0), 2)
                copy_proj((0, 0), 3)
                copy_proj((0, 0), 4)
                copy_q((0, 0), 0)

            def step(a, p, f):
                if a:
                    copy_proj(a, 5)
                if f:
                    copy_o(f, 1)
                if a:
                    ac.activation(warm[:, :], minus_half[:, 0:1], ACT.Exp)
                    exps(a, 0)
                    copy_q(a, 1)
                if f:
                    copy_h(f)
                if a:
                    exps(a, 1)
                if p:
                    copy_x(p)
                if f:
                    squares(f)
                if p:
                    copy_proj(p, 0)
                if a:
                    exps(a, 2)
                if p:
                    copy_proj(p, 1)
                if a:
                    exps(a, 3)
                if p:
                    copy_proj(p, 2)
                if f:
                    gelu(f, 0)
                if p:
                    copy_proj(p, 3)
                if f:
                    gelu(f, 1)
                if a:
                    copy_o(a, 0)
                if f:
                    gelu(f, 2)
                if p:
                    copy_proj(p, 4)
                    copy_q(p, 0)
                if f and spot(f)[0] == 1:
                    last_sq(f)

            over_items(ac, project_first, step)

        @block.vector
        def _(ve):
            ve.wait_ge(s["small_loaded"], SMALL)
            ve.tensor_copy(eye_s[:, :].rearrange("p (n t) -> p n t", t=CH),
                           eyes[:, 0:CH].unsqueeze(1).to_broadcast([128, R * NCH, CH])).then_inc(s["eye_ready"], 1)
            ve.tensor_tensor(w_t[:, 192:320], w_t[:, 192:320], norm_g, MUL)
            ve.tensor_tensor(gb_n[:, :], gb, norm_g, MUL).then_inc(s["gw_scaled"], 1)
            for i in range(3):
                src = bank[i][:, :].rearrange("p (g t) -> p g t", g=G)
                ve.wait_ge(s["conv_first"], i + 1)
                for d in (1, 2, 3):
                    ins = ve.scalar_tensor_tensor(kvq[:, i, :, d:], src[:, :, 0:T - d], cw[:, i, 3 - d:4 - d],
                                                  kvq[:, i, :, d:], MUL, ADD)
                    if d < 3:
                        ins.then_inc(s["norm_step"], 1)
                        ve.wait_ge(s["norm_step"], 2 * i + d)
                ins.then_inc(s["conv_v"], 1)
            ve.wait_ge(s["gates_ready"], 4)
            ve.wait_ge(s["gates_abs"], 1)
            for i in range(4):
                ins = ve.tensor_scalar(sg_all[64:96, 512 * i:512 * i + 512], bank[3 + i][64:96, :],
                                       gate_bias[64:96], 0.0, ADD, MAX)
                if i % 2:
                    ins.then_inc(s["gates_relu"], 1)
            ve.wait_ge(s["bias_out"], 1)
            b1_cols = b1[:, :, :].rearrange("p l (i k) -> p l i k", k=3)
            more = bank[2][:, 0:6 * LAYERS].rearrange("p (l i k) -> p l i k", l=LAYERS, k=3)
            for rows, k in ((slice(0, 128), slice(0, 2)), (slice(0, HB[2]), slice(2, 3))):
                ins = ve.tensor_tensor(b1_cols[rows, :, :, k], b1_cols[rows, :, :, k], more[rows, :, :, k], ADD)
            ins.then_inc(s["w1_ready"], 1)
            f_first = first_f[:, :].rearrange("p (n t) -> p n t", t=CH)[:, :, 0]

            def starts(a):
                return a[:, :].rearrange("p (n t) -> p n t", t=CH)[:, :, 0]

            ve.wait_ge(s["zeroed"], 1)
            ve.wait_ge(s["spread_f"], 1)
            ve.tensor_scalar(eta_f[:, :], bank[7][:, :], 0.05, None, ADD).then_inc(s["keep_done"], 1)
            ve.wait_ge(s["keep_done"], 1)
            ve.tensor_copy(f_first, starts(eta_f)).then_inc(s["first_done"], 1)
            ve.wait_ge(s["first_done"], 1)
            ve.memset(starts(eta_f), 0.0).then_inc(s["first_done"], 1)
            ve.wait_ge(s["first_done"], 2)
            ve.tensor_tensor_scan(e_cum[:, :], eta_f[:, :], first_f[:, :], 0.0, MUL, ADD).then_inc(s["scanned"], 1)
            ve.wait_ge(s["spread_f"], 2)
            ve.tensor_scalar(keep_f[:, :], bank[0][:, :], -1.0, 1.0, MUL, ADD).then_inc(s["keep_done"], 1)
            ve.wait_ge(s["scanned"], 1)
            ve.wait_ge(s["keep_done"], 2)
            ve.tensor_copy(f_first, starts(keep_f)).then_inc(s["first_done"], 1)
            ve.wait_ge(s["first_done"], 3)
            ve.memset(starts(keep_f), 0.0).then_inc(s["first_done"], 1)
            ve.wait_ge(s["first_done"], 4)
            ve.tensor_tensor_scan(a_cum[:, :], keep_f[:, :], first_f[:, :], 0.0, MUL, ADD).then_inc(s["scanned"], 1)
            ve.tensor_tensor_scan(b_cum[:, :], keep_f[:, :], e_cum[:, :], 0.0, MUL, ADD).then_inc(s["scanned"], 1)
            ve.wait_ge(s["factors_s"], 1)
            ve.wait_ge(s["eye_ready"], 1)
            ve.memset(starts(eta_s), 0.0).then_inc(s["first_done"], 1)
            ve.wait_ge(s["first_done"], 5)
            ve.tensor_tensor_scan(p_mat[:, :], eta_s[:, :], eye_s[:, :], 0.0, MUL, ADD).then_inc(s["scanned"], 1)
            ve.wait_ge(s["factors_s"], 2)
            ve.memset(starts(keep_s), 0.0).then_inc(s["first_done"], 1)
            ve.wait_ge(s["first_done"], 6)
            ve.wait_ge(s["scanned"], 4)
            ve.tensor_tensor_scan(m_mat[:, :], keep_s[:, :], p_mat[:, :], 0.0, MUL, ADD).then_inc(s["scanned"], 1)
            ve.wait_ge(s["scanned"], 5)
            ve.tensor_copy(w_end[:, 0, :, :], m_mat_c[:, :, :, CH - 1].rearrange("p r c -> p c r"))
            ve.tensor_copy(w_end[:, 1, :, :], p_mat_c[:, :, :, CH - 1].rearrange("p r c -> p c r")
                           ).then_inc(s["mats_ready"], 1)
            ve.wait_ge(s["mats_ready"], 1)
            expand(ve.tensor_copy, 0)
            expand(ve.tensor_copy, 1).then_inc(s["exp_v"], 1)
            ve.wait_ge(s["theta_out"], 1)
            ve.tensor_copy(theta[:, :, :], bank[5][:, 0:NCH * R].rearrange("p (c r) -> p c r", r=R)
                           ).then_inc(s["theta_ready"], 1)
            N0 = 6
            NS = 5

            x_grp = x_tok[:, :, :].rearrange("p (g r h) d -> p g h r d", g=G, h=2)
            x1_grp = x1[:, :, :].rearrange("p (g r h) d -> p g h r d", g=G, h=2)

            def rms_mean(i):
                ve.wait_ge(s["osq_ready"], i + 1)
                ve.tensor_scalar(st_sq[:, i, :], st_sq[:, i, :], 1.0 / H, EPS, MUL, ADD).then_inc(s["ms_ready"], 1)

            def mix(i):
                g, half = ORDER[i] // 2, ORDER[i] % 2
                ve.wait_ge(s["ms_inv"], TAIL.index((0, i)) + 1)
                for r in range(R):
                    ins = ve.scalar_tensor_tensor(mixed[:, i, r, :], bank[i][:, 128 * r:128 * r + 128],
                                                  st_inv[:, i, r:r + 1], gates[:, g, half, r, :], MUL, MUL)
                ins.then_inc(s["on_ready"], 1)
                ve.wait_ge(s["on_ready"], i + 1)
                ve.tensor_tensor(mixed[:, i, :, :], mixed[:, i, :, :], x_grp[:, g, half, :, :], ADD
                                 ).then_inc(s["mix_step"], 1)
                ve.wait_ge(s["mix_step"], 2 * i + 1)
                ve.tensor_reduce(st_mean[:, i, :], mixed[:, i, :, :], AX.X, ADD).then_inc(s["mix_step"], 1)
                ve.wait_ge(s["mix_step"], 2 * i + 2)
                ve.tensor_scalar(st_mean[:, i, :], st_mean[:, i, :], -1.0 / H, None, MUL).then_inc(s["mean_ready"], 1)

            def norm_variance(i):
                ve.wait_ge(s["csq_ready"], i + 1)
                ve.tensor_scalar(st_var[:, i, :], st_var[:, i, :], 1.0 / H, LN_EPS, MUL, ADD).then_inc(s["ms_ready"], 1)

            def norm_scale(i):
                g, half = ORDER[i] // 2, ORDER[i] % 2
                ve.wait_ge(s["mean_ready"], i + 1)
                ve.wait_ge(s["ms_inv"], TAIL.index((1, i)) + 1)
                for r in range(R):
                    ins = ve.tensor_scalar(x1_grp[:, g, half, r, :], mixed[:, i, r, :], st_mean[:, i, r:r + 1],
                                           st_rstd[:, i, r:r + 1], ADD, MUL)
                ins.then_inc(s["x1_ready"], 1)

            def chunk(c, d, more):
                def step(k):
                    ve.wait_ge(s["norm_step"], c * NS + (N0 + k))

                if d is not None:
                    ve.wait_ge(s["sigy_ready"], d + 1)
                    for g in range(G):
                        ins = ve.tensor_tensor(hy[:, g, :], y_bank[g], sig_y[:, g, :], MUL)
                    ins.then_inc(s["h_ready"], 1)
                    ve.wait_ge(s["h_ready"], d + 1)
                    for r in (0, 1):
                        rows = slice(D * r, D * r + D)
                        ins = ve.tensor_copy(hc[rows, r, :, :], hy[rows, :, :])
                    ins.then_inc(s["hc_v"], 1)
                if c is not None:
                    ve.wait_ge(s["sig_ready"], c + 1)
                    ve.tensor_tensor(act[:, :, :], gt(bank[0]), sig[:, :, :], MUL).then_inc(s["act_ready"], 1)
                    ve.wait_ge(s["qk_ready"], c + 1)
                    ve.tensor_tensor(q1[:, :, :], qk_bank, m_mat_c[:, :, c, :], MUL).then_inc(s["q1_ready"], 1)
                    ve.wait_ge(s["pred_ready"], c + 1)
                    ve.tensor_tensor(err[:, :, :], gt(bank[1]), kvq_c[:, 1, :, c, :], SUB).then_inc(s["err_ready"], 1)
                    ve.wait_ge(s["ak_ready"], c + 1)
                    for k in range(2):
                        ins = ve.tensor_copy(tokm[:, 3 * k, :, :], ak_bank[:, k, :].rearrange("p (r o) -> p r o", r=R))
                    ins.then_inc(s["tokm_ready"], 1)
                    ve.wait_ge(s["da_ready"], c + 1)
                    ve.wait_ge(s["sp_ready"], c + 1)
                    ve.tensor_tensor(dz[:, :, :], gt(bank[0]), dact[:, :, :], MUL).then_inc(s["dz_ready"], 1)
                    ve.wait_ge(s["sq_ready"], c * 2 + 1)
                    for k in (0, 3):
                        ve.tensor_reduce(n4[:, R * k:R * k + R], sqm[:, k, :, :], AX.X, ADD)
                    ve.wait_ge(s["tok_ready"], c + 1)
                    ve.tensor_copy(tokm[:, 1:3, :, :], de_bank.rearrange("p k (r o) -> p k r o", r=R)
                                   ).then_inc(s["tokm_ready"], 1)
                if d is not None:
                    if c is None:
                        rms_mean(0)
                    ve.wait_ge(s["ah_ready"], d + 1)
                    ve.tensor_tensor(am[:, :, :], ah_bank, m_mat_c[:, :, d, :], MUL).then_inc(s["am_ready"], 1)
                if c is not None:
                    ve.wait_ge(s["sq_ready"], c * 2 + 2)
                    ve.tensor_reduce(n4[:, R:3 * R], sqm[:, 1:3, :, :].rearrange("p k r o -> p (k r) o"), AX.X, ADD
                                     ).then_inc(s["norm_step"], 1)
                    step(1)
                    ve.tensor_tensor(n2[:, :], n4[:, 0:2 * R], n4[:, 2 * R:4 * R], MUL).then_inc(s["norm_step"], 1)
                    step(2)
                    ve.tensor_tensor(n1[:, :], n2[:, 0:R], n2[:, R:2 * R], ADD).then_inc(s["norm_step"], 1)
                    step(3)
                    ve.tensor_scalar(n1[:, :], n1[:, :], (EPS / 0.2) ** 2, None, MAX).then_inc(s["norm_ready"], 1)
                    ve.wait_ge(s["gates_turned"], c + 1)
                    ve.tensor_tensor(gates_c[:, c, :, :], bank[0][:, :].rearrange("p (i h) -> p i h", i=R),
                                     gb_n[:, :].unsqueeze(1).to_broadcast([128, R, H]), ADD
                                     ).then_inc(s["gates_added"], 1)
                    ve.wait_ge(s["inv_norm"], c + 1)
                    ve.scalar_tensor_tensor(coef[:, :], inv[:, :], 0.2, theta[:, c, :], MIN, MUL
                                            ).then_inc(s["norm_step"], 1)
                    step(4)
                    if d is not None:
                        ve.wait_ge(s["y2_ready"], d + 1)
                    for i in range(2):
                        ins = ve.tensor_tensor(gc[:, i, :, :], tokm[:, 1 + i, :, :],
                                               coef[:, :].unsqueeze(2).to_broadcast([128, R, D]), MUL)
                    ins.then_inc(s["gc_ready"], 1)
                    ve.wait_ge(s["gc_ready"], c + 1)
                if more:
                    for j in range(2):
                        for i in range(2):
                            ins = ve.tensor_tensor(u[:, j, i, :, :], gc[:, i, :, :],
                                                   w_end[:, j, c, :].unsqueeze(2).to_broadcast([128, R, D]), MUL)
                    ins.then_inc(s["u_ready"], 1)
                    ve.wait_ge(s["d_ready"], c + 1)
                    for g in range(G):
                        ins = ve.scalar_tensor_tensor(t_st[:, g, :, :], s_st[:, g, :, :], b_cum_c[:, g, c, CH - 1:CH],
                                                      d_bank[g][:, 0, :, :], MUL, ADD)
                    ins.then_inc(s["norm_step"], 1)
                    for g in range(G):
                        ve.scalar_tensor_tensor(s_st[:, g, :, :], s_st[:, g, :, :], e_cum_c[:, g, c, CH - 1:CH],
                                                d_bank[g][:, 1, :, :], MUL, ADD)
                    step(5)
                    for g in range(G):
                        ins = ve.scalar_tensor_tensor(w_st[:, g, :, :], w_st[:, g, :, :],
                                                      a_cum_c[:, g, c, CH - 1:CH], t_st[:, g, :, :], MUL, ADD)
                    ins.then_inc(s["st_ready"], 1)
                    ve.wait_ge(s["st_ready"], c + 1)
                    ve.wait_ge(s["y1_ready"], c + 1)
                    ve.wait_ge(s["kept_ready"], c + 1)
                    for r in (0, 1):
                        ins = expand(ve.tensor_copy, r)
                    ins.then_inc(s["exp_v"], 1)

            over_chunks(ve, chunk, lambda: None)
            mix(0)
            rms_mean(1)
            mix(1)
            rms_mean(2)
            rms_mean(3)
            mix(2)
            norm_variance(0)
            norm_variance(1)
            mix(3)
            norm_variance(2)
            norm_scale(0)
            norm_scale(1)
            norm_scale(2)
            norm_variance(3)
            norm_scale(3)

            def norms(n, tile):
                ve.wait_ge(s["proj_out"], count(6, n, 3 * tile + 2))
                ve.tensor_reduce(ss[tile][:, :], qk_sq[:, :, :, :].rearrange("p k h d -> p (k h) d"), AX.X, ADD
                                 ).then_inc(s["ss_step"], 1)
                ve.wait_ge(s["ss_step"], count(2, n, tile + 1))
                ve.tensor_scalar(ss[tile][:, :], ss[tile][:, :], 1e-24, None, MAX).then_inc(s["ss_ready"], 1)

            def cos_part(n, tile):
                l, sl = spot(n)
                if n[1]:
                    ve.wait_ge(s["qk_turned"], count(4, n, 2 * tile - 2))
                ve.wait_ge(s["proj_out"], count(6, n, 3 * tile + 2))
                ve.tensor_tensor(rot[tile][:, :, :, :], qk[tile][:, :, :, :],
                                 cos_t[:, l, tile, :, :].unsqueeze(2).to_broadcast([128, 2, HEADS, DH]), MUL
                                 ).then_inc(s["c_ready"], 1)

            def sum_parts(n, tile):
                ve.wait_ge(s["s_ready"], count(4, n, 2 * tile + 2))
                ve.wait_ge(s["c_ready"], count(2, n, tile + 1))
                ve.tensor_tensor(rot[tile][:, :, :, :], rot[tile][:, :, :, :], rot_s[tile][:, :, :, :], ADD
                                 ).then_inc(s["sum_ready"], 1)

            def scale_qk(n, tile):
                ve.wait_ge(s["rn_ready"], count(2, n, tile + 1))
                ve.wait_ge(s["sum_ready"], count(2, n, tile + 1))
                flat = rot[tile][:, :, :, :].rearrange("p k h d -> p (k h) d")
                ve.tensor_tensor(flat, flat, rn[tile][:, :].unsqueeze(2).to_broadcast([128, 2 * HEADS, DH]), MUL
                                 ).then_inc(s["rot_ready"], 1)

            def copy_k(n, tile):
                l, sl = spot(n)
                ve.wait_ge(s["qk_turned"], count(4, n, 2 * tile + 2))
                ve.tensor_copy(kt[sl][:, :, 128 * tile:128 * tile + 128], heads4(6)).then_inc(s["kt_out"], 1)

            def maxima(n, w):
                ve.wait_ge(s["score_ready"], count(4, n, w + 1))
                ve.tensor_reduce(nmx[w % 2][:, :], heads4(w % 2)[:, :, keys(w)], AX.X, MAX, negate=True).then_inc(s["max_ready"], 1)

            def inv_sums(n, w):
                ve.wait_ge(s["exp_done"], count(4, n, w + 1))
                ve.reciprocal(rr[w % 2][:, :], rs[w % 2][:, :]).then_inc(s["rr_ready"], 1)

            def copy_p(n, w):
                ve.wait_ge(s["p_turned"], count(4, n, w + 1))
                ve.tensor_copy(pt[keys(w), :, :], heads4(2)[keys(w), :, :]).then_inc(s["p_out"], 1)

            def add_attention(n, tile):
                l, sl = spot(n)
                ve.wait_ge(s["wo_done"], count(2, n, tile + 1))
                ve.tensor_tensor(xa[sl][:, tile, :], xs[sl][:, tile, :], bank[3][:, 128 * tile:128 * tile + 128], ADD
                                 ).then_inc(s["xa_ready"], 1)

            def centre(n):
                l, sl = spot(n)
                ve.wait_ge(s["mu_done"], count(1, n, 1))
                ve.tensor_tensor(h_cen[:, :], h_fm[:, 0:T], bank[5][:, 0:T], SUB).then_inc(s["hc_ready"], 1)

            def variances(n):
                ve.wait_ge(s["var_done"], count(1, n, 1))
                ve.tensor_scalar(h_var[:, :], bank[7][:, 0:2], LN_EPS, None, ADD).then_inc(s["var_ready"], 1)

            def diagonal(n):
                ve.wait_ge(s["hinv_ready"], count(1, n, 1))
                for tile in range(2):
                    ins = ve.tensor_scalar(diag[:, tile, :], ident[:, :], h_inv[:, tile:tile + 1], None, MUL)
                ins.then_inc(s["diag_ready"], 1)

            def scale_h(n):
                ve.wait_ge(s["bc_done"], count(1, n, 1))
                ve.tensor_tensor(h_n[:, :], h_cen[:, :], bank[5][:, 0:T], MUL).then_inc(s["hn_ready"], 1)

            def gated(n, k):
                l, sl = spot(n)
                ve.wait_ge(s["gelu_done"], count(3, n, k + 1))
                ve.scalar_tensor_tensor(hh[0:HB[k], k, :], bank[(7, 5, 7)[k]][0:HB[k], T:2 * T], b1[0:HB[k], l, k:k + 1],
                                        gl[0:HB[k], k, :], ADD, MUL).then_inc(s["hh_ready"], 1)

            def finish(n):
                l, sl = spot(n)
                both = bank[5][:, 0:T].rearrange("p (t d) -> p t d", t=2)
                ve.wait_ge(s["w2_done"], count(1, n, 1))
                if l:
                    ve.wait_ge(s["pre_ready"], count(1, n, 1 - B))
                dst = yb[sl][:, :, :] if l else y_tiles[:, batch(n), :, :]
                ve.tensor_tensor(dst, (yb if l else xa)[sl][:, :, :], both, ADD).then_inc(s["x_ready"], 1)

            def last_sum(n):
                l, sl = spot(n)
                ve.wait_ge(s["x_ready"], count(1, n, 2))
                ve.tensor_reduce(y_sum[:, :], yb[sl][:, :, :], AX.X, ADD).then_inc(s["fin_step"], 1)

            def last_mean(n):
                ve.wait_ge(s["fin_step"], count(1, n, 1 - B))
                ve.tensor_scalar(y_sum[:, :], y_sum[:, :], -1.0 / H, None, MUL).then_inc(s["ymean_ready"], 1)

            def last_var(n):
                ve.wait_ge(s["ysq_ready"], count(1, n, 1 - B))
                ve.tensor_scalar(y_var[:, :], y_var[:, :], 1.0 / H, LN_EPS, MUL, ADD).then_inc(s["yvar_ready"], 1)

            def last_scale(n):
                l, sl = spot(n)
                ve.wait_ge(s["yinv_ready"], count(1, n, 1 - B))
                for tile in range(2):
                    ins = ve.tensor_scalar(y_tiles[:, batch(n), tile, :], yb[sl][:, tile, :],
                                           y_sum[:, tile:tile + 1], y_inv[:, tile:tile + 1], ADD, MUL)
                ins.then_inc(s["y_ready"], 1)

            def project_first():
                ve.wait_ge(s["tabs_ready"], 1)
                norms((0, 0), 0)
                cos_part((0, 0), 0)
                sum_parts((0, 0), 0)
                scale_qk((0, 0), 0)
                norms((0, 0), 1)
                cos_part((0, 0), 1)
                copy_k((0, 0), 0)
                sum_parts((0, 0), 1)

            def step(a, p, f):
                if a:
                    maxima(a, 0)
                    scale_qk(a, 1)
                if f:
                    add_attention(f, 1)
                if a:
                    maxima(a, 1)
                    inv_sums(a, 0)
                    copy_k(a, 1)
                if f:
                    centre(f)
                if a:
                    copy_p(a, 0)
                    inv_sums(a, 1)
                    maxima(a, 2)
                if f:
                    variances(f)
                if a:
                    maxima(a, 3)
                if f:
                    diagonal(f)
                if a:
                    inv_sums(a, 2)
                    copy_p(a, 1)
                if f:
                    scale_h(f)
                if p:
                    norms(p, 0)
                if a:
                    inv_sums(a, 3)
                    copy_p(a, 2)
                if p:
                    cos_part(p, 0)
                if f:
                    gated(f, 0)
                if p:
                    sum_parts(p, 0)
                if f:
                    gated(f, 1)
                if p:
                    scale_qk(p, 0)
                if f:
                    gated(f, 2)
                if a:
                    add_attention(a, 0)
                if p:
                    norms(p, 1)
                    cos_part(p, 1)
                if f:
                    finish(f)
                if f and spot(f)[0] == 1:
                    last_sum(f)
                    last_mean(f)
                if a:
                    copy_p(a, 3)
                if p:
                    copy_k(p, 0)
                if f and spot(f)[0] == 1:
                    last_var(f)
                if p:
                    sum_parts(p, 1)
                if f and spot(f)[0] == 1:
                    last_scale(f)

            over_items(ve, project_first, step)


def constants():
    ident = np.eye(128, dtype=np.float32)
    eyes = np.concatenate([np.tile(np.eye(CH, dtype=np.float32), (2, 1)),
                           np.repeat(np.eye(R, dtype=np.float32), D, axis=0)], 1)
    sel = np.zeros((128, 257), np.float32)
    sel[0:32, 0:128] = 0.1 / D
    sel[32:64, 128:256] = 0.9 / D
    sel[64:128, 256] = -0.1 / D
    half = np.arange(0, DH, 2, dtype=np.float32)
    inv_freq = (np.float32(1.0) / np.float32(10000.0) ** (half / np.float32(DH))).astype(np.float32)
    pos = np.arange(T, dtype=np.float32)
    freqs = np.tile(pos[:, None] * inv_freq[None, :], (1, 2))
    base = (half + np.float32(0.4 * DH)) / np.float32(1.4 * DH)
    power = (pos - T // 2) / np.float32(WIN // 2)
    scale = np.tile(base[None, :] ** power[:, None], (1, 2)).astype(np.float32)
    cos, sin = np.cos(freqs), np.sin(freqs)
    sign = np.where(np.arange(DH) < DH // 2, -1.0, 1.0).astype(np.float32)
    cs = np.stack([cos * scale * 8.0, cos / scale], 1)
    sn = np.stack([sin * scale * 8.0, sin / scale], 1) * sign
    tabs = np.stack([cs, sn], 1).reshape(2, 128, 2, 2, DH).transpose(1, 0, 2, 3, 4)
    i = np.arange(WIN)[:, None]
    j = np.arange(WIN)[None, :]
    low = np.float32(-1e30)
    causal = np.where(j <= i, 0, low)
    band = np.where(j >= i, 0, low)
    none = np.full((WIN, WIN), low)
    masks = np.stack([np.tile(np.concatenate(m, 1), (2, 1)) for m in
                      ((causal, none), (band, causal), (causal, band))], 1)
    return {"c_ident": ident, "c_eyes": eyes, "c_sel": sel, "c_tabs": np.ascontiguousarray(tabs, np.float32),
            "c_masks": np.ascontiguousarray(masks, np.float32)}


def laid_out(a):
    f = {n: a["L0_ffn_" + n] for n in "wqkv q_scale k_scale wo ln_g ln_b w1 b1 w2 b2".split()}
    m = {n[8:]: v for n, v in a.items() if n.startswith("L0_attn_")}
    f32 = np.float32

    def heights(k):
        return slice(128 * k, 128 * k + HB[k])

    w_all = np.zeros((128, 336), f32)
    w_all[:, 0:320] = np.concatenate([m[n] for n in ("Wk", "Wv", "Wq", "aW", "eW", "tW", "gW")]).T
    w_all[:, 320:332] = np.tile(np.concatenate([m["ckw"], m["cvw"], m["cqw"]], 1), (R, 1))
    w_all[:, 332:335] = np.tile(np.stack([m["ckb"], m["cvb"], m["cqb"]], 1), (R, 1))
    w_all[0:96, 335] = np.concatenate([m["ab"], m["eb"], m["tb"]])
    w_st = np.tile(np.stack([m["mW1"].T, m["mW2"].T, m["mW2"]], 1)[None], (R, 1, 1, 1)).reshape(128, 1, 3, D)
    wo_bd = np.zeros((R, D, R, H), f32)
    for r in range(R):
        wo_bd[r, :, r, :] = m["Wo"].T
    w2 = np.zeros((128, LAYERS, 3, H), f32)
    b1 = np.zeros((128, LAYERS, 6), f32)
    for l in range(LAYERS):
        for k in range(3):
            w2[0:HB[k], l, k, :] = f["w2"][l, heights(k)]
            for part in range(2):
                b1[0:HB[k], l, 3 * part + k] = f["b1"][l, HID * part:HID * part + HID][heights(k)]
        w2[HB[2], l, 2, :] = f["b2"][l]
    scales = np.stack([f["q_scale"], f["k_scale"]], 1)
    return {"hidden": m["hidden"], "x_fm": m["hidden"].reshape(B * T, H).T, "w_all": w_all,
            "w_st": np.tile(w_st, (1, G, 1, 1)), "wo_bd": wo_bd.reshape(128, R, H),
            "norm_gb": np.tile(np.stack([m["norm_g"], m["gb"]])[None], (128, 1, 1)),
            "wqkv": f["wqkv"].transpose(1, 0, 2), "wo": f["wo"].reshape(LAYERS, 4, 128, H).transpose(2, 0, 1, 3),
            "w1": f["w1"].transpose(1, 0, 2), "w2": w2, "b1": b1,
            "scales": np.tile(scales[None], (128, 1, 1, 1)), "ln_gb": np.stack([f["ln_g"], f["ln_b"]]).transpose(2, 0, 1)}


def kernel(**inputs):
    import concourse.bacc as bacc
    from concourse.bass_utils import run_bass_kernel_spmd as run

    nc = bacc.Bacc("TRN2", target_bir_lowering=False, num_devices=1)
    arrays, args = {}, {}
    given = {n: np.ascontiguousarray(a) for n, a in laid_out({n: np.asarray(a) for n, a in inputs.items()}).items()}
    given.update(constants())
    for name, a in given.items():
        arrays[f"in_{name}"] = a
        args[name] = nc.dram_tensor(f"in_{name}", a.shape, mybir.dt.from_np(a.dtype), kind="ExternalInput").ap()
    out = nc.dram_tensor("out_x", (B, T, H), mybir.dt.float32, kind="ExternalOutput").ap()
    build(nc, args, out)
    return run(nc, [arrays], core_ids=[0]).results[0]["out_x"]
```
